# Optimizing a Trainium2 kernel written in Bass

```python
import numpy as np
import jax
import jax.numpy as jnp

def _softmax(x, axis=-1):
    return jax.nn.softmax(x, axis=axis)

def _gelu(x):
    return jax.nn.gelu(x, approximate=True)

def _silu(x):
    return jax.nn.silu(x)

def _sigmoid(x):
    return jax.nn.sigmoid(x)

def _layernorm(x, axis=-1, eps=1e-05):
    m = jnp.mean(x, axis=axis, keepdims=True)
    v = jnp.var(x, axis=axis, keepdims=True)
    return (x - m) / jnp.sqrt(v + eps)

def _scatter_add(tgt, idx, src, axis=0):
    return tgt.at[idx].add(src)

def _segment_sum(src, seg, n):
    return jax.ops.segment_sum(src, seg, n)
kernel_name = 'mk_xattn_ffn_d2_seqx_r4_708d5a'

def setup_inputs(seed: int=0):
    np.random.seed(seed)
    _w = jnp.asarray

    def _rec_inputs():
        import jax
        import jax.numpy as jnp
        _rk = jax.random.key(seed)
        x = -0.0002928 + 1 * jax.random.normal(jax.random.fold_in(_rk, 1), (16, 128, 256), jnp.float32)
        _lenS = 128 - jax.random.randint(jax.random.fold_in(_rk, 7), (16,), 0, max(1, 128 // 4) + 1, jnp.int32)
        _lenS2 = 128 - jax.random.randint(jax.random.fold_in(_rk, 8), (16,), 0, max(1, 128 // 4) + 1, jnp.int32)
        _ctx_1024P = jax.random.normal(jax.random.fold_in(_rk, 11), (16, 16, 256), jnp.float32)
        _ctx_1024c = jax.random.dirichlet(jax.random.fold_in(_rk, 511), 0.3 * jnp.ones((16,), jnp.float32), (16, 128))
        _ctx_1024t = jnp.einsum('bsk,bkd->bsd', _ctx_1024c, _ctx_1024P)
        _ctx_1024t = _ctx_1024t * jax.lax.rsqrt(jnp.mean(jnp.square(_ctx_1024t)) + 1e-12) * 0.953939
        ctx_1024 = -1.39393e-06 + 0.999914 * (_ctx_1024t + 0.3 * jax.random.normal(jax.random.fold_in(_rk, 611), (16, 128, 256), jnp.float32))
        fside_BxSxS2_0 = jax.random.uniform(jax.random.fold_in(_rk, 12), (16, 128, 128), jnp.float32, 0.0, 1)
        _validS = jnp.arange(128)[None, :] < _lenS[:, None]
        _validS2 = jnp.arange(128)[None, :] < _lenS2[:, None]
        _causal = jnp.tril(jnp.ones((128, 128), dtype=bool))
        mask_Bx1xSxS2_ff0 = jnp.where(jnp.ones((16, 1, 128, 128), dtype=bool), 0.0, -1000000000.0).astype(jnp.float32)
        return (x, ctx_1024, fside_BxSxS2_0, mask_Bx1xSxS2_ff0)
    x, ctx_1024, fside_BxSxS2_0, mask_Bx1xSxS2_ff0 = _rec_inputs()

    def _L0_xattn_setup():
        import jax, jax.numpy as jnp
        import numpy as np
        B, F, T, D, N, K = (2, 512, 512, 256, 16, 16)
        H = D // N
        key = jax.random.key(seed)
        ks = jax.random.split(key, 12)
        inp = {'query_inputs': jax.random.normal(ks[0], (B, F, D), jnp.float32), 'source_inputs': jax.random.normal(ks[1], (B, T, D), jnp.float32), 'query_source_dist': jax.random.uniform(ks[2], (B, F, T), jnp.float32), 'bias': jnp.zeros((B, 1, F, T), jnp.float32), 'Wq': jax.random.normal(ks[3], (D, N, H), jnp.float32) / np.sqrt(D), 'Wk': jax.random.normal(ks[4], (D, N, H), jnp.float32) / np.sqrt(D), 'Wv': jax.random.normal(ks[5], (D, N, H), jnp.float32) / np.sqrt(D), 'Wo': jax.random.normal(ks[6], (N, H, D), jnp.float32) / np.sqrt(D), 'Wb1': jax.random.normal(ks[7], (1, K), jnp.float32), 'bb1': jnp.zeros((K,), jnp.float32), 'Wb2': jax.random.normal(ks[8], (K, 1), jnp.float32) / np.sqrt(K), 'bb2': jnp.zeros((1,), jnp.float32)}
        return inp
    _L0_xattn_all = _L0_xattn_setup()
    _L0_xattn_in = {k: v for k, v in _L0_xattn_all.items() if k in ('Wq', 'Wk', 'Wv', 'Wo', 'Wb1', 'bb1', 'Wb2', 'bb2')}
    del _L0_xattn_all

    def _L0_ffn_setup():
        import jax, jax.numpy as jnp
        import numpy as np
        B, T, C, H, E = (1, 64, 256, 512, 8)
        STD = 0.02
        key = jax.random.key(seed)
        ks = jax.random.split(key, 8)
        f32 = jnp.float32
        return {'x': jax.random.normal(ks[0], (B, T, C), f32), 'up': jax.random.normal(ks[1], (E, H, C), f32) * STD, 'gate': jax.random.normal(ks[2], (E, H, C), f32) * STD, 'down': jax.random.normal(ks[3], (E, C, H), f32) * STD, 'router': jax.random.normal(ks[4], (E, C), f32) * STD, 'w_up_s': jax.random.normal(ks[5], (H, C), f32) * STD, 'w_gate_s': jax.random.normal(ks[6], (H, C), f32) * STD, 'w_down_s': jax.random.normal(ks[7], (C, H), f32) * STD}
    _L0_ffn_all = _L0_ffn_setup()
    _L0_ffn_in = {k: v for k, v in _L0_ffn_all.items() if k in ('up', 'gate', 'down', 'router', 'w_up_s', 'w_gate_s', 'w_down_s')}
    del _L0_ffn_all

    def _L1_xattn_setup():
        import jax, jax.numpy as jnp
        import numpy as np
        D_MODEL = 256
        NUM_HEADS = 16
        D_K = D_MODEL // NUM_HEADS
        key = jax.random.key(seed)
        ks = jax.random.split(key, 11)
        B, L = (4, 512)
        s = 0.02
        return {'query': jax.random.normal(ks[0], (B, L, D_MODEL), jnp.float32), 'key': jax.random.normal(ks[1], (B, L, D_MODEL), jnp.float32), 'value': jax.random.normal(ks[2], (B, L, D_MODEL), jnp.float32), 'Wq': jax.random.normal(ks[3], (D_MODEL, D_MODEL), jnp.float32) * s, 'bq': jnp.zeros((D_MODEL,), jnp.float32), 'Wk': jax.random.normal(ks[4], (D_MODEL, D_MODEL), jnp.float32) * s, 'bk': jnp.zeros((D_MODEL,), jnp.float32), 'Wv': jax.random.normal(ks[5], (D_MODEL, D_MODEL), jnp.float32) * s, 'bv': jnp.zeros((D_MODEL,), jnp.float32), 'Wo': jax.random.normal(ks[6], (D_MODEL, D_MODEL), jnp.float32) * s, 'bo': jnp.zeros((D_MODEL,), jnp.float32)}
    _L1_xattn_all = _L1_xattn_setup()
    _L1_xattn_in = {k: v for k, v in _L1_xattn_all.items() if k in ('Wq', 'bq', 'Wk', 'bk', 'Wv', 'bv', 'Wo', 'bo')}
    del _L1_xattn_all

    def _L1_ffn_setup():
        import jax, jax.numpy as jnp
        import numpy as np
        B, S, H, I, E, TOPK, KS = (4, 1024, 256, 128, 16, 2, 3)
        key = jax.random.key(seed)
        ks = jax.random.split(key, 9)
        sc = 0.02
        return {'hidden_states': jax.random.normal(ks[0], (B, S, H), dtype=jnp.float32), 'router_w': jax.random.normal(ks[1], (H, E), dtype=jnp.float32) * sc, 'router_bias': jnp.zeros((E,), dtype=jnp.float32), 'expert_gate_w': jax.random.normal(ks[2], (E - 1, H, I), dtype=jnp.float32) * sc, 'expert_up_w': jax.random.normal(ks[3], (E - 1, H, I), dtype=jnp.float32) * sc, 'expert_down_w': jax.random.normal(ks[4], (E - 1, I, H), dtype=jnp.float32) * sc, 'conv_w': jax.random.normal(ks[5], (I, H, KS), dtype=jnp.float32) * sc, 'shared_up_w': jax.random.normal(ks[6], (H, I), dtype=jnp.float32) * sc, 'shared_down_w': jax.random.normal(ks[7], (I, H), dtype=jnp.float32) * sc}
    _L1_ffn_all = _L1_ffn_setup()
    _L1_ffn_in = {k: v for k, v in _L1_ffn_all.items() if k in ('router_w', 'router_bias', 'expert_gate_w', 'expert_up_w', 'expert_down_w', 'conv_w', 'shared_up_w', 'shared_down_w')}
    del _L1_ffn_all
    return {'x': x, 'ctx_1024': ctx_1024, 'fside_BxSxS2_0': fside_BxSxS2_0, 'mask_Bx1xSxS2_ff0': mask_Bx1xSxS2_ff0, 'L0_xattn_Wq': _L0_xattn_in['Wq'], 'L0_xattn_Wk': _L0_xattn_in['Wk'], 'L0_xattn_Wv': _L0_xattn_in['Wv'], 'L0_xattn_Wo': _L0_xattn_in['Wo'], 'L0_xattn_Wb1': _L0_xattn_in['Wb1'], 'L0_xattn_bb1': _L0_xattn_in['bb1'], 'L0_xattn_Wb2': _L0_xattn_in['Wb2'], 'L0_xattn_bb2': _L0_xattn_in['bb2'], 'L0_ffn_up': _L0_ffn_in['up'], 'L0_ffn_gate': _L0_ffn_in['gate'], 'L0_ffn_down': _L0_ffn_in['down'], 'L0_ffn_router': _L0_ffn_in['router'], 'L0_ffn_w_up_s': _L0_ffn_in['w_up_s'], 'L0_ffn_w_gate_s': _L0_ffn_in['w_gate_s'], 'L0_ffn_w_down_s': _L0_ffn_in['w_down_s'], 'L1_xattn_Wq': _L1_xattn_in['Wq'], 'L1_xattn_bq': _L1_xattn_in['bq'], 'L1_xattn_Wk': _L1_xattn_in['Wk'], 'L1_xattn_bk': _L1_xattn_in['bk'], 'L1_xattn_Wv': _L1_xattn_in['Wv'], 'L1_xattn_bv': _L1_xattn_in['bv'], 'L1_xattn_Wo': _L1_xattn_in['Wo'], 'L1_xattn_bo': _L1_xattn_in['bo'], 'L1_ffn_router_w': _L1_ffn_in['router_w'], 'L1_ffn_router_bias': _L1_ffn_in['router_bias'], 'L1_ffn_expert_gate_w': _L1_ffn_in['expert_gate_w'], 'L1_ffn_expert_up_w': _L1_ffn_in['expert_up_w'], 'L1_ffn_expert_down_w': _L1_ffn_in['expert_down_w'], 'L1_ffn_conv_w': _L1_ffn_in['conv_w'], 'L1_ffn_shared_up_w': _L1_ffn_in['shared_up_w'], 'L1_ffn_shared_down_w': _L1_ffn_in['shared_down_w']}

def reference(x, ctx_1024, fside_BxSxS2_0, mask_Bx1xSxS2_ff0, L0_xattn_Wq, L0_xattn_Wk, L0_xattn_Wv, L0_xattn_Wo, L0_xattn_Wb1, L0_xattn_bb1, L0_xattn_Wb2, L0_xattn_bb2, L0_ffn_up, L0_ffn_gate, L0_ffn_down, L0_ffn_router, L0_ffn_w_up_s, L0_ffn_w_gate_s, L0_ffn_w_down_s, L1_xattn_Wq, L1_xattn_bq, L1_xattn_Wk, L1_xattn_bk, L1_xattn_Wv, L1_xattn_bv, L1_xattn_Wo, L1_xattn_bo, L1_ffn_router_w, L1_ffn_router_bias, L1_ffn_expert_gate_w, L1_ffn_expert_up_w, L1_ffn_expert_down_w, L1_ffn_conv_w, L1_ffn_shared_up_w, L1_ffn_shared_down_w):
    import jax
    import jax.numpy as jnp

    def _L0_xattn_ref(query_inputs, source_inputs, query_source_dist, bias, Wq, Wk, Wv, Wo, Wb1, bb1, Wb2, bb2):
        import jax, jax.numpy as jnp
        import numpy as np
        B, F, T, D, N, K = (2, 512, 512, 256, 16, 16)
        H = D // N
        depth = Wq.shape[-1]
        q = jnp.einsum('bfd,dnh->bfnh', query_inputs, Wq) * depth ** (-0.5)
        k = jnp.einsum('btd,dnh->btnh', source_inputs, Wk)
        v = jnp.einsum('btd,dnh->btnh', source_inputs, Wv)
        h = jax.nn.relu(query_source_dist[..., None] * Wb1[0] + bb1)
        qs_bias = (h @ Wb2)[..., 0] + bb2[0]
        logits = jnp.einsum('btnh,bfnh->bnft', k, q)
        logits = logits + bias + qs_bias[:, None, :, :]
        weights = jax.nn.softmax(logits, axis=-1)
        attn = jnp.einsum('bnft,btnh->bfnh', weights, v)
        out = jnp.einsum('bfnh,nhd->bfd', attn, Wo)
        return out

    def _L0_ffn_ref(x, up, gate, down, router, w_up_s, w_gate_s, w_down_s):
        import jax, jax.numpy as jnp
        import numpy as np
        B, T, C, H, E = (1, 64, 256, 512, 8)
        STD = 0.02
        b, t, c = x.shape
        x_ = x.reshape(b * t, c)
        logits = x_ @ router.T
        idx = jnp.argmax(logits, axis=-1)
        onehot = jax.nn.one_hot(idx, router.shape[0], dtype=x.dtype)
        u = jnp.einsum('bc,ehc->ebh', x_, up)
        g = jnp.einsum('bc,ehc->ebh', x_, gate)
        h = jax.nn.silu(g) * u
        ye = jnp.einsum('ebh,ech->ebc', h, down)
        y = jnp.einsum('ebc,be->bc', ye, onehot)
        ys = jax.nn.silu(x_ @ w_gate_s.T) * (x_ @ w_up_s.T) @ w_down_s.T
        return (y + ys).reshape(b, t, c)

    def _L1_xattn_ref(query, key, value, Wq, bq, Wk, bk, Wv, bv, Wo, bo):
        import jax, jax.numpy as jnp
        import numpy as np
        D_MODEL = 256
        NUM_HEADS = 16
        D_K = D_MODEL // NUM_HEADS
        B, Lq, _ = query.shape
        Lk = key.shape[1]
        q = (query @ Wq.T + bq).reshape(B, Lq, NUM_HEADS, D_K).transpose(0, 2, 1, 3)
        k = (key @ Wk.T + bk).reshape(B, Lk, NUM_HEADS, D_K).transpose(0, 2, 1, 3)
        v = (value @ Wv.T + bv).reshape(B, Lk, NUM_HEADS, D_K).transpose(0, 2, 1, 3)
        scores = jnp.einsum('bhqd,bhkd->bhqk', q, k) / jnp.sqrt(jnp.float32(D_K))
        attn = jax.nn.softmax(scores, axis=-1)
        out = jnp.einsum('bhqk,bhkd->bhqd', attn, v)
        out = out.transpose(0, 2, 1, 3).reshape(B, Lq, D_MODEL)
        return out @ Wo.T + bo

    def _L1_ffn_ref(hidden_states, router_w, router_bias, expert_gate_w, expert_up_w, expert_down_w, conv_w, shared_up_w, shared_down_w):
        import jax, jax.numpy as jnp
        import numpy as np
        B, S, H, I, E, TOPK, KS = (4, 1024, 256, 128, 16, 2, 3)
        b, s, h = hidden_states.shape
        flat = hidden_states.reshape(b * s, h)
        logits = (flat @ router_w).astype(jnp.float32) + router_bias
        probs = jax.nn.softmax(logits, axis=-1)
        top_w, top_i = jax.lax.top_k(probs, TOPK)
        norm_w = top_w / (jnp.sum(top_w, axis=-1, keepdims=True) + 1e-06)
        norm_w = norm_w.astype(hidden_states.dtype)
        combine = jnp.sum(jax.nn.one_hot(top_i, E, dtype=norm_w.dtype) * norm_w[..., None], axis=1)
        routed = combine[:, E - 1:E] * flat
        for e in range(E - 1):
            y = jax.nn.silu(flat @ expert_gate_w[e]) * (flat @ expert_up_w[e]) @ expert_down_w[e]
            routed = routed + combine[:, e:e + 1] * y
        routed = routed.reshape(b, s, h)
        x_ncw = jnp.transpose(hidden_states, (0, 2, 1))
        gate = jax.lax.conv_general_dilated(x_ncw, conv_w, window_strides=(1,), padding=[(KS - 1, 0)], dimension_numbers=('NCW', 'OIW', 'NCW'))
        gate = jnp.transpose(gate, (0, 2, 1))
        shared = jax.nn.silu(gate) * (hidden_states @ shared_up_w) @ shared_down_w
        return shared + routed
    x = x + _L0_xattn_ref(_layernorm(x, axis=-1), ctx_1024, fside_BxSxS2_0, mask_Bx1xSxS2_ff0, L0_xattn_Wq, L0_xattn_Wk, L0_xattn_Wv, L0_xattn_Wo, L0_xattn_Wb1, L0_xattn_bb1, L0_xattn_Wb2, L0_xattn_bb2)
    x = x + _L0_ffn_ref(_layernorm(x, axis=-1), L0_ffn_up, L0_ffn_gate, L0_ffn_down, L0_ffn_router, L0_ffn_w_up_s, L0_ffn_w_gate_s, L0_ffn_w_down_s)
    x = x + _L1_xattn_ref(_layernorm(x, axis=-1), ctx_1024, ctx_1024, L1_xattn_Wq, L1_xattn_bq, L1_xattn_Wk, L1_xattn_bk, L1_xattn_Wv, L1_xattn_bv, L1_xattn_Wo, L1_xattn_bo)
    x = x + _L1_ffn_ref(_layernorm(x, axis=-1), L1_ffn_router_w, L1_ffn_router_bias, L1_ffn_expert_gate_w, L1_ffn_expert_up_w, L1_ffn_expert_down_w, L1_ffn_conv_w, L1_ffn_shared_up_w, L1_ffn_shared_down_w)
    return x

_drawn_inputs = setup_inputs


def setup_inputs(seed=0):
    import zlib

    import numpy as np

    out = dict(_drawn_inputs(seed))
    spreads = {'L0_xattn_bb1': (0.0, 0.8),
     'L1_xattn_bq': (0.0, 0.8),
     'L1_xattn_bk': (0.0, 0.8),
     'L1_xattn_bv': (0.0, 0.1),
     'L1_xattn_bo': (0.0, 0.1),
     'L1_ffn_router_bias': (0.0, 0.1)}
    factors = {'fside_BxSxS2_0': 4.96,
     'L0_xattn_Wb1': 7.874,
     'L0_xattn_Wb2': 8.0,
     'L1_xattn_Wq': 8.0,
     'L1_xattn_Wk': 8.0,
     'L1_ffn_expert_gate_w': 8.0,
     'L1_ffn_expert_up_w': 8.0,
     'L1_ffn_expert_down_w': 8.0,
     'L1_ffn_conv_w': 3.226,
     'L1_ffn_shared_up_w': 3.083,
     'L1_ffn_shared_down_w': 3.13}
    for name, (base, spread) in spreads.items():
        noise = np.random.default_rng([zlib.crc32(name.encode()), seed]).standard_normal(out[name].shape)
        drawn = base * np.exp(spread * noise) if base else spread * noise
        out[name] = jnp.asarray(drawn.astype(out[name].dtype))
    for name, factor in factors.items():
        out[name] = (out[name] * factor).astype(out[name].dtype)
    return out
```

```python
from contextlib import ExitStack

import numpy as np
import concourse.bass as bass
from concourse import mybir

F32 = mybir.dt.float32
I32 = mybir.dt.int32
U32 = mybir.dt.uint32
ALU = mybir.AluOpType
ACT = mybir.ActivationFunctionType
AX = mybir.AxisListType

P = 128
NB = 16
D = 256
KC = D // P
NH, HD = 16, 16
NBANK = 4
VW = HD + 1
KB = 16
MG = 4
PADW = P + 2
EPS = 1e-5

E0, H0 = 8, 512
HC0 = H0 // P
T0 = (NB * P + E0 * (P - 1)) // P
W0 = KC * 2 * H0 + HC0 * D

E1, H1 = 16, 128
R1 = E1 - 1
T1 = (2 * NB * P + R1 * (P - 1)) // P
W1 = KC * 2 * H1 + D
CONV = 3

JT = (1, 2)
NS = T0
assert NS * JT[0] == T0 and NS * JT[1] == T1 and NS % 2 == 1

C_ID, C_TRI, C_ONE, C_PAR, C_PRI, C_TIL = 0, 128, 256, 384, 386, 402
C_SEG = C_TIL + 48
C_END = C_SEG + NB * E1


def head_of(bank, i):
    return (i // 2) * 8 + 2 * bank + i % 2


def build_program(nc, t, out, rows):
    with ExitStack() as ctx:
        def sb(name, shape, dt=F32):
            return ctx.enter_context(nc.sbuf_tensor(name, shape, dt))

        def sem(name):
            return ctx.enter_context(nc.semaphore(name))

        ps = [ctx.enter_context(nc.psum_tensor(f"bank{i}", [P, 512], F32)) for i in range(8)]
        ps_s, ps_pa, ps_pb, ps_pm, ps_po = ps[0:4], ps[4], ps[5], ps[6], ps[7]

        cst = sb("cst", [P, C_END])
        ident, tri, ones = cst[:, C_ID:C_ID + P], cst[:, C_TRI:C_TRI + P], cst[:, C_ONE:C_ONE + P]
        par = cst[:, C_PAR:C_PAR + 2]
        x_res = sb("x_res", [P, NB, D])
        xn_all = sb("xn_all", [P, NB, D])
        xnT_all = sb("xnT_all", [P, KC, NB, PADW])
        w_att = sb("w_att", [P, 2, 4, KC, D])
        rt = sb("rt", [P, KC, E0 + E1])
        w_ffn = sb("w_ffn", [P, E0, W0])
        w_sh = sb("w_sh", [P, W0])
        qs_all = w_att[:, 1].rearrange("p a k d -> p (a k d)").rearrange("p (b s) -> p b s", b=NB)
        sc = w_ffn[:, 7, 0:2048].rearrange("p (g i s) -> p g i s", g=NBANK, i=4)
        pr = w_ffn[:, 6, 0:2048].rearrange("p (g i s) -> p g i s", g=NBANK, i=4)
        pt = w_ffn[:, 5, 0:2048].rearrange("p (g i s) -> p g i s", g=NBANK, i=4)
        dist = w_ffn[:, 4, 0:2048].rearrange("p (b s) -> p b s", b=NB)
        bias_all = w_ffn[:, 3, 0:2048].rearrange("p (b s) -> p b s", b=NB)
        hid = [w_ffn[:, 4 + i, 2048:2560] for i in range(4)]

        mlp = sb("mlp", [P, 3 * KB + 1])
        a_bc, b_bc, c_bc, bb2 = mlp[:, 0:KB], mlp[:, KB:2 * KB], mlp[:, 2 * KB:3 * KB], mlp[:, 3 * KB:3 * KB + 1]
        qkb = sb("qkb", [P, 2, KC])
        qb4 = sb("qb4", [P, KC])
        kbm = sb("kbm", [P, KC, 2])
        bvo = sb("bvo", [P, 2, D])
        rbias = sb("rbias", [P, E1])
        work = sb("work", [P, 5120])

        def attention_tile(at_column, *shape):
            n = int(np.prod(shape))
            return work[:, at_column:at_column + n], at_column + n

        col = 0
        ctx_k, col = attention_tile(col, KC, P)
        ctx_v, col = attention_tile(col, KC, P)
        xn, col = attention_tile(col, D)
        xnT, col = attention_tile(col, KC, P)
        qT, col = attention_tile(col, KC, P)
        kz, col = attention_tile(col, KC, 2, P)
        attn, col = attention_tile(col, D)
        attnT, col = attention_tile(col, KC, P)
        xn1, col = attention_tile(col, D)
        xn1T, col = attention_tile(col, KC, P)
        ctx_k, ctx_v, xnT, qT, attnT, xn1T = (
            v.rearrange("p (k s) -> p k s", k=KC) for v in (ctx_k, ctx_v, xnT, qT, attnT, xn1T))
        kz = kz.rearrange("p (k h s) -> p k h s", k=KC, h=2)
        sg = work[:, 0:1024].rearrange("p (a s) -> p a s", a=2)
        hT = work[:, 1024:2048].rearrange("p (a s) -> p a s", a=2)
        xs = work[:, 2048:3072].rearrange("p (a j d) -> p a j d", a=2, j=2)
        xsT = work[:, 3072:3584]
        hs = work[:, 3584:4096]
        hsT = work[:, 0:512]
        sgs = work[:, 512:1024]
        ys = work[:, 4096:5120].rearrange("p (a j d) -> p a j d", a=2, j=2)
        rw = [work[:, 2048 + 256 * i:2304 + 256 * i] for i in range(12)]
        va = sb("va", [P, NH, VW])
        mx = sb("mx", [P, NBANK, 4])
        rsum = sb("rsum", [P, NH])
        lg = sb("lg", [P, NB, E1])
        picks = rw[6]
        slot = sb("slot", [P, 2, NB], I32)
        tile_expert = sb("tile_expert", [P, T1], I32)
        wgt = sb("wgt", [P, 2, NB])
        small = sb("small", [P, 8, NB])
        need_i = sb("need_i", [P, E1], I32)
        te_f = sb("te_f", [P, T1])
        seg = cst[:, C_SEG:C_END]
        zeros = sb("zeros", [P, D])
        rows_b = xnT_all[:].rearrange("p k b s -> p (k b s)")[:, 0:NB * D].rearrange("p (b d) -> p b d", b=NB)
        w1_ffn = w_ffn[:, 0:4, :].rearrange("p a w -> p (a w)")[:, 0:R1 * W1].rearrange("p (e w) -> p e w", e=R1)
        ln_st = sb("ln_st", [P, 2, 6])
        ln_mv = sb("ln_mv", [P, 2, 2])
        ln_ve = sb("ln_ve", [P, 2])
        ln_rs = sb("ln_rs", [P, 2])
        mhalf = sb("mhalf", [P, 1])

        consts_in, x_in, mlp_in, dist_in, watt0_in, watt1_in, small_in = map(
            sem, ("consts_in", "x_in", "mlp_in", "dist_in", "watt0_in", "watt1_in", "small_in"))
        ctx_k_in, ctx_v_in = sem("ctx_k_in"), sem("ctx_v_in")
        x0_in = sem("x0_in")
        setup_pool, setup_dve = sem("setup_pool"), sem("setup_dve")
        stats_done, aggr_done, var_ready, rstd_ready = map(sem, ("stats_done", "aggr_done", "var_ready", "rstd_ready"))
        stats1_done, aggr1_done, var1_ready, rstd1_ready = map(
            sem, ("stats1_done", "aggr1_done", "var1_ready", "rstd1_ready"))
        xn_ready, xnT_in_psum, xnT_ready = map(sem, ("xn_ready", "xnT_in_psum", "xnT_ready"))
        k_in_psum, kz_ready, q_in_psum, q_ready = map(sem, ("k_in_psum", "kz_ready", "q_in_psum", "q_ready"))
        v_in_psum, v_ready = sem("v_in_psum"), sem("v_ready")
        scores_in_psum, biased, max_ready, shifted, probs_ready = map(
            sem, ("scores_in_psum", "biased", "max_ready", "shifted", "probs_ready"))
        pt_in_psum, pt_ready, av_in_psum, rsum_ready, attn_ready = map(
            sem, ("pt_in_psum", "pt_ready", "av_in_psum", "rsum_ready", "attn_ready"))
        attnT_in_psum, attnT_ready, wo_in_psum, x1_ready = map(
            sem, ("attnT_in_psum", "attnT_ready", "wo_in_psum", "x1_ready"))
        xn1_kept = sem("xn1_kept")
        xn1_ready, xn1T_in_psum, xn1T_ready, xnT_kept, lg_in_psum, lg_ready = map(
            sem, ("xn1_ready", "xn1T_in_psum", "xn1T_ready", "xnT_kept", "lg_in_psum", "lg_ready"))
        hid_ready, hid_scaled, hid_added, bias_ready, bo_added = map(
            sem, ("hid_ready", "hid_scaled", "hid_added", "bias_ready", "bo_added"))
        stored = sem("stored")
        x2_ready, bv_ready = sem("x2_ready"), sem("bv_ready")
        zeros_set = sem("zeros_set")
        route_step = sem("route_step")
        rows_zeroed = [sem(f"rows_zeroed{i}") for i in range(2)]
        ffn_in = [sem(f"ffn_in{i}") for i in range(4)]
        centred, exp_ready = sem("centred"), sem("exp_ready")
        picks_ready = [sem(f"picks_ready{i}") for i in range(2)]
        ranks_in_psum = [sem(f"ranks_in_psum{i}") for i in range(2)]
        slots_ready = [sem(f"slots_ready{i}") for i in range(2)]
        scattered = [sem(f"scattered{i}") for i in range(2)]
        gathered = [sem(f"gathered{i}") for i in range(5)]
        sh_gu_in_psum, sh_silu, sh_hidden, sh_used, sh_added = (
            [sem(f"{name}{i}") for i in range(2)]
            for name in ("sh_gu_in_psum", "sh_silu", "sh_hidden", "sh_used", "sh_added"))
        xs_in = [[sem(f"xs_in{i}{p}") for p in range(2)] for i in range(2)]
        ys_stored = [[sem(f"ys_stored{i}{p}") for p in range(2)] for i in range(2)]
        xsT_in_psum, xsT_ready, gu_in_psum, silu_ready, hs_ready, hsT_in_psum, hsT_ready, ys_in_psum, ys_ready = (
            [sem(f"{name}{i}") for i in range(2)]
            for name in ("xsT_in_psum", "xsT_ready", "gu_in_psum", "silu_ready", "hs_ready", "hsT_in_psum",
                         "hsT_ready", "ys_in_psum", "ys_ready"))
        weighted = sem("weighted")
        out_ready = sem("out_ready")
        waits_ended = sem("waits_ended")

        block = ctx.enter_context(nc.Block())

        def pipeline(eng, body, mlp_part=False):
            body(0, None, None)
            body(1, 0, None)
            body(2, 1, 0)
            if mlp_part:
                with eng.Fori(3, NB - MG) as n:
                    body(n, n - 1, n - 2)
                with eng.Fori(NB - MG, NB) as n:
                    body(n, n - 1, n - 2, False)
            else:
                with eng.Fori(3, NB) as n:
                    body(n, n - 1, n - 2)
            body(None, NB - 1, NB - 2)
            body(None, None, NB - 1)

        def apart(eng):
            eng.sem_inc(waits_ended, 1)

        def shared_steps(eng, layer, body):
            if layer == 0:
                for c in range(HC0):
                    body(0, c, c)
                with eng.Fori(1, NB // MG) as g:
                    for c in range(HC0):
                        body(g, c, g * HC0 + c)
            else:
                for g in range(NB // MG):
                    body(g, 0, g)

        def half(layer, g, c):
            return c % 2 if layer == 0 else g % 2

        def at(layer, b):
            return b + NB * layer

        @block.sync
        def _(sp):
            sp.dma_start(cst[:], t["consts"]).then_inc(consts_in, 16)
            sp.dma_start(ctx_k[:], t["ctxT"][:, :, 0:P]).then_inc(ctx_k_in, 16)
            sp.dma_start(x_res[:, 0:2, :], t["x"][:, 0:2, :]).then_inc(x0_in, 16)
            sp.dma_start(w_att[:, 0], t["w_att0"]).then_inc(watt0_in, 16)
            sp.dma_start(ctx_v[:], t["ctxT"][:, :, 0:P]).then_inc(ctx_v_in, 16)
            sp.dma_start(rt[:], t["rt"]).then_inc(small_in, 16)
            sp.dma_start(x_res[:, 2:NB, :], t["x"][:, 2:NB, :]).then_inc(x_in, 16)

            def attention(layer, first):
                def load_k(n):
                    sp.wait_ge(k_in_psum, at(layer, n))
                    sp.dma_start(ctx_k[:], t["ctxT"][:, :, bass.ds(n * P, P)]).then_inc(ctx_k_in, 16)

                def load_v(n):
                    sp.wait_ge(v_in_psum, at(layer, n))
                    sp.dma_start(ctx_v[:], t["ctxT"][:, :, bass.ds(n * P, P)]).then_inc(ctx_v_in, 16)

                if layer:
                    load_k(0)
                    load_v(0)
                with sp.Fori(1, NB) as n:
                    load_k(n)
                    load_v(n)

            sp.wait_ge(zeros_set, 1)
            for layer, tiles in ((0, T0), (1, T1 + NB)):
                sp.dma_start(rows[layer][0:tiles * P].rearrange("(t p) d -> p t d", p=P),
                             zeros[:].unsqueeze(1).broadcast_to([P, tiles, D])).then_inc(rows_zeroed[layer], 16)
            sp.dma_start(w_sh[:], t["w_sh0"]).then_inc(ffn_in[0], 16)
            for e in range(3):
                sp.dma_start(w_ffn[:, e, :], t["w_ffn0"][:, e, :]).then_inc(ffn_in[1], 16)
            attention(0, True)

            def sorted_tiles(layer):
                tiles = rows[layer][0:NS * JT[layer] * P].rearrange("(n j p) d -> n p j d", j=JT[layer], p=P)
                nj = JT[layer]

                def load(n, p):
                    if not (static(n) and n < 2):
                        sp.wait_ge(xsT_in_psum[layer], n - 1)
                    sp.dma_start(xs[:, p, 0:nj, :], tiles[n]).then_inc(xs_in[layer][p], 16)

                def store(b, p):
                    sp.wait_ge(ys_ready[layer], b + 1)
                    sp.dma_start(tiles[b], ys[:, p, 0:nj, :]).then_inc(ys_stored[layer][p], 16)

                sp.wait_ge(scattered[layer], 16 * NB * (1 + layer))
                load(0, 0)
                load(1, 1)

                def body(n, b, p):
                    if n is not None and not (static(n) and n + 2 >= NS):
                        load(n + 2, p)
                    if b is not None:
                        store(b, 1 - p)

                body(0, None, 0)
                body(1, 0, 1)
                body(2, 1, 0)
                with sp.Fori(1, (NS - 3) // 2) as i:
                    body(i * 2 + 1, i * 2, 1)
                    body(i * 2 + 2, i * 2 + 1, 0)
                body(NS - 2, NS - 3, 1)
                store(NS - 2, 1)
                store(NS - 1, 0)

            sp.wait_ge(lg_ready, NB)
            sp.wait_ge(av_in_psum, NB)
            sp.wait_ge(bias_ready, NB)
            for e in range(3, E0):
                sp.dma_start(w_ffn[:, e, :], t["w_ffn0"][:, e, :]).then_inc(ffn_in[2], 16)
            sp.dma_start(w_att[:, 1], t["w_att1"]).then_inc(watt1_in, 16)
            sorted_tiles(0)
            sp.wait_ge(ys_in_psum[0], NS)
            for p in range(2):
                sp.wait_ge(ys_stored[0][p], 16 * ((NS + 1 - p) // 2))
            sp.wait_ge(sh_used[0], NB)
            sp.dma_start(w_sh[:, 0:t["w_sh1"].shape[1]], t["w_sh1"]).then_inc(ffn_in[3], 16)
            sp.dma_start(w1_ffn, t["w_ffn1"]).then_inc(ffn_in[3], 16)
            attention(1, False)
            sorted_tiles(1)
            for g in range(NB // MG):
                sp.wait_ge(out_ready, g + 1)
                sp.dma_start(out[g * MG:(g + 1) * MG].rearrange("b t c -> t b c"), x_res[:, g * MG:(g + 1) * MG])\
                    .then_inc(stored, 16)
            sp.wait_ge(stored, 16 * (NB // MG))

        @block.gpsimd
        def _(pool):
            nc.gpsimd.memset(zeros[:], 0.0).then_inc(zeros_set, 1)
            nc.gpsimd.memset(mhalf[:], -0.5).then_inc(setup_pool, 1)
            nc.gpsimd.memset(va[:], 1.0).then_inc(setup_pool, 1)
            nc.gpsimd.memset(xnT_all[:, :, :, 0:2], 0.0).then_inc(setup_pool, 1)
            pool.wait_ge(setup_pool, 1)

            def mlp_units(group, k0, done):
                sums = qs_all[:, bass.ds(group * MG, MG), :].rearrange("p b s -> p (b s)")
                for i in range(4):
                    pool.wait_ge(hid_ready, done + i + 1)
                    coef = c_bc[:, bass.ds(k0 + i, 1)].broadcast_to([P, 512])
                    apart(pool)
                    nc.gpsimd.tensor_tensor(hid[i], hid[i], coef, ALU.mult).then_inc(hid_scaled, 1)
                for i in range(4):
                    pool.wait_ge(hid_scaled, done + i + 1)
                    if not static(done) or done + i:
                        pool.wait_ge(hid_added, done + i)
                    apart(pool)
                    nc.gpsimd.tensor_tensor(sums, sums, hid[i], ALU.add).then_inc(hid_added, 1)

            def bias_of(n, done):
                pool.wait_ge(hid_added, done)
                apart(pool)
                nc.gpsimd.tensor_tensor(bias_all[:, n, :], bias_all[:, n, :], qs_all[:, n, :], ALU.add)\
                    .then_inc(bias_ready, 1)

            def rstd(layer, n):
                pool.wait_ge(var_ready, at(layer, n) + 1)
                nc.gpsimd.tensor_tensor(ln_rs[:, 0:1], ln_ve[:, 0:1], mhalf[:], ALU.pow).then_inc(rstd_ready, 1)

            def rstd1(layer, b):
                pool.wait_ge(var1_ready, at(layer, b) + 1)
                nc.gpsimd.tensor_tensor(ln_rs[:, 1:2], ln_ve[:, 1:2], mhalf[:], ALU.pow).then_inc(rstd1_ready, 1)

            def keep(layer, b):
                pool.wait_ge(xn1_ready, at(layer, b) + 1)
                apart(pool)
                nc.gpsimd.tensor_copy(xn_all[:, b, :], xn1[:]).then_inc(xn1_kept, 1)

            rstd(0, 0)
            pool.wait_ge(mlp_in, 16)
            pool.wait_ge(setup_dve, 1)
            for q in range(4):
                mlp_units(0, 4 * q, 4 * q)
            pool.wait_ge(dist_in, 32)
            bias_of(0, 16)

            def body(n, b, c, mlp_on=True):
                if n is not None and mlp_on:
                    mlp_units(n // 4 + 1, (n % 4) * 4, n * 4 + 16)
                if n is not None:
                    bias_of_next(n, mlp_on)
                if b is not None:
                    rstd1(0, b)
                    keep(0, b)

            def bias_of_next(n, mlp_on):
                nn = n + 1
                if mlp_on:
                    bias_of(nn, n * 4 + 20)
                else:
                    bias_of(nn, 64)
                rstd(0, nn)

            body(0, None, None)
            body(1, 0, None)
            body(2, 1, 0)
            with pool.Fori(3, NB - MG) as n:
                body(n, n - 1, n - 2)
            with pool.Fori(NB - MG, NB - 1) as n:
                body(n, n - 1, n - 2, False)
            body(None, NB - 2, NB - 3)
            body(None, NB - 1, NB - 2)

            def scatter(layer):
                pool.wait_ge(slots_ready[layer], 1)
                pool.wait_ge(rows_zeroed[layer], 16)
                pool.wait_ge(xn1_kept, NB * (layer + 1))
                for a in range(1 + layer):
                    for b in range(NB):
                        nc.gpsimd.indirect_dma_start(
                            rows[layer], bass.IndirectOffsetOnAxis(ap=slot[:, a, b:b + 1], axis=0),
                            xn_all[:, b, :], None).then_inc(scattered[layer], 16)

            def gather(layer, a, b, to, signal):
                nc.gpsimd.indirect_dma_start(
                    to, None, rows[layer], bass.IndirectOffsetOnAxis(ap=slot[:, a, b:b + 1], axis=0))\
                    .then_inc(signal, 16)

            def tiles_stored(layer):
                for p in range(2):
                    pool.wait_ge(ys_stored[layer][p], 16 * ((NS + 1 - p) // 2))

            scatter(0)
            tiles_stored(0)
            for b in range(NB):
                gather(0, 0, b, xn_all[:, b, :], gathered[4])
            pool.wait_ge(gathered[4], 16 * NB)
            pool.wait_ge(sh_added[0], NB)
            nc.gpsimd.memset(va[:, :, HD:VW], 1.0)

            def add_ffn(n):
                nc.gpsimd.tensor_tensor(x_res[:, n, :], x_res[:, n, :], xn_all[:, n, :], ALU.add).then_inc(x2_ready, 1)

            def second(n, b, c):
                if n is not None:
                    pool.wait_ge(xn_ready, at(1, n) + 1)
                    apart(pool)
                    nc.gpsimd.tensor_tensor(x_res[:, n, :], x_res[:, n, :], bvo[:, 1, :], ALU.add).then_inc(bo_added, 1)
                    if not (static(n) and n == NB - 1):
                        add_ffn(n + 1)
                        rstd(1, n + 1)
                if b is not None:
                    rstd1(1, b)
                    keep(1, b)

            add_ffn(0)
            rstd(1, 0)
            second(0, None, None)
            second(1, 0, None)
            second(2, 1, 0)
            with pool.Fori(3, NB - 1) as n:
                second(n, n - 1, n - 2)
            second(NB - 1, NB - 2, NB - 3)
            second(None, NB - 1, NB - 2)
            scatter(1)
            tiles_stored(1)
            pool.wait_ge(sh_used[1], NB // MG)
            for b in range(NB):
                gather(1, 0, b, xn_all[:, b, :], gathered[b // MG])
                gather(1, 1, b, rows_b[:, b, :], gathered[b // MG])

        @block.scalar
        def _(act):
            A = nc.scalar.activation

            def mlp_units(group, k0, done):
                for i in range(4):
                    if not static(done) or done:
                        act.wait_ge(hid_added, done - 3 + i)
                    A(hid[i], dist[:, bass.ds(group * MG, MG), :].rearrange("p b s -> p (b s)"), ACT.Relu,
                      bias=b_bc[:, bass.ds(k0 + i, 1)], scale=a_bc[:, bass.ds(k0 + i, 1)]).then_inc(hid_ready, 1)

            def attention(layer):
                def keys(n):
                    act.wait_ge(k_in_psum, at(layer, n) + 1)
                    pk = ps_pm[:, 0:KC * P].rearrange("p (k s) -> p k s", k=KC)
                    for h in range(2):
                        if layer == 0:
                            last = A(kz[:, :, h, :], pk, ACT.Copy, scale=par[:, h:h + 1])
                        else:
                            for k in range(KC):
                                last = A(kz[:, k, h, :], pk[:, k, :], ACT.Identity, scale=par[:, h:h + 1],
                                         bias=kbm[:, k, h:h + 1])
                    last.then_inc(kz_ready, 1)

                def body(n, b, c, mlp_on=True):
                    if n is not None:
                        keys(n)

                    def weightsT(j):
                        act.wait_ge(pt_in_psum, at(layer, b) * 4 + j + 1)
                        if j == 0 and not (layer == 0 and static(b) and b == 0):
                            act.wait_ge(av_in_psum, at(layer, b))
                        bank = ps_pa if j % 2 == 0 else ps_pb
                        A(pt[:, j].rearrange("p i s -> p (i s)"), bank[:, :], ACT.Copy).then_inc(pt_ready, 1)

                    def probs(j):
                        act.wait_ge(shifted, at(layer, n) * 4 + j + 1)
                        if not (layer == 0 and static(n) and n == 0):
                            act.wait_ge(pt_in_psum, at(layer, n) * 4 - 3 + j)
                        A(pr[:, j], sc[:, j], ACT.Exp).then_inc(probs_ready, 1)

                    if b is not None:
                        weightsT(0)
                        weightsT(1)
                    if n is not None:
                        act.wait_ge(xnT_in_psum, at(layer, n) + 1)
                        A(xnT[:].rearrange("p k s -> p (k s)"), ps_pm[:, 0:D], ACT.Copy).then_inc(xnT_ready, 1)
                    if b is not None:
                        weightsT(2)
                    if n is not None:
                        act.wait_ge(q_in_psum, at(layer, n) + 1)
                        if layer == 0:
                            A(qT[:].rearrange("p k s -> p (k s)"), ps_pm[:, 0:D], ACT.Copy, scale=0.25)\
                                .then_inc(q_ready, 1)
                        else:
                            for k in range(KC):
                                last = A(qT[:, k, :], ps_pm[:, k * P:(k + 1) * P], ACT.Identity, scale=0.25,
                                         bias=qb4[:, k:k + 1])
                            last.then_inc(q_ready, 1)
                    if b is not None:
                        weightsT(3)
                    if n is not None:
                        if layer == 0 and mlp_on:
                            mlp_units(n // 4 + 1, (n % 4) * 4, n * 4 + 16)
                        probs(0)
                    if n is not None and layer == 0:
                        act.wait_ge(v_in_psum, at(layer, n) + 1)
                        A(va[:, :, 0:HD], ps_pm[:, 0:D].rearrange("p (h d) -> p h d", h=NH), ACT.Copy)\
                            .then_inc(v_ready, 1)
                    if c is not None:
                        act.wait_ge(xn1T_in_psum, at(layer, c) + 1)
                        A(xn1T[:].rearrange("p k s -> p (k s)"), ps_pb[:, 0:D], ACT.Copy).then_inc(xn1T_ready, 1)
                        A(xnT_all[:, :, c, 2:PADW], ps_pb[:, 0:D].rearrange("p (k s) -> p k s", k=KC), ACT.Copy)\
                            .then_inc(xnT_kept, 1)
                    if n is not None:
                        probs(1)
                    if b is not None:
                        act.wait_ge(attnT_in_psum, at(layer, b) + 1)
                        A(attnT[:].rearrange("p k s -> p (k s)"), ps_pa[:, 0:D], ACT.Copy).then_inc(attnT_ready, 1)
                    if n is not None:
                        probs(2)
                    if c is not None:
                        act.wait_ge(lg_in_psum, at(layer, c) + 1)
                        ne = E1 if layer else E0
                        A(lg[:, c, 0:ne], ps_pb[:, 0:ne], ACT.Copy).then_inc(lg_ready, 1)
                    if n is not None:
                        probs(3)

                pipeline(act, body, layer == 0)

            act.dma_start(mlp[:], t["mlp"]).then_inc(mlp_in, 16)
            act.dma_start(dist, t["dist"]).then_inc(dist_in, 16)
            act.dma_start(bias_all, t["mask"]).then_inc(dist_in, 16)
            act.dma_start(qkb[:], t["qkb"]).then_inc(small_in, 16)
            act.dma_start(bvo[:], t["bvo"]).then_inc(small_in, 16)
            act.dma_start(rbias[:], t["rbias"]).then_inc(small_in, 16)
            act.wait_ge(mlp_in, 16)
            act.wait_ge(dist_in, 32)
            act.wait_ge(consts_in, 16)
            act.wait_ge(setup_pool, 3)
            for q in range(4):
                mlp_units(0, 4 * q, 4 * q)
            attention(0)

            def shared(layer):
                def body(g, c, q):
                    h = half(layer, g, c)
                    act.wait_ge(sh_gu_in_psum[layer], q + 1)
                    if not static(q) or q >= 2:
                        act.wait_ge(sh_hidden[layer], q - 1)
                    A(sg[:, h, :], ps[h][:, :], ACT.Silu).then_inc(sh_silu[layer], 1)
                shared_steps(act, layer, body)

            def sorted_tiles(layer):
                def body(n, b, p):
                    def rowsT(n):
                        act.wait_ge(xsT_in_psum[layer], n + 1)
                        w = D * JT[layer]
                        if not (static(n) and n == 0):
                            act.wait_ge(gu_in_psum[layer], n)
                        A(xsT[:, 0:w], ps[4][:, 0:w], ACT.Copy).then_inc(xsT_ready[layer], 1)

                    if b is not None:
                        w = HC0 * P if layer == 0 else 2 * P
                        act.wait_ge(hsT_in_psum[layer], b + 1)
                        if not (static(b) and b == 0):
                            act.wait_ge(ys_in_psum[layer], b)
                        A(hsT[:, 0:w], ps[2][:, 0:w], ACT.Copy).then_inc(hsT_ready[layer], 1)
                    if n is not None:
                        if static(n) and n == 0:
                            rowsT(0)
                        act.wait_ge(gu_in_psum[layer], n + 1)
                        if not (static(n) and n == 0):
                            act.wait_ge(hs_ready[layer], n)
                        if layer == 0:
                            A(sgs[:, 0:H0], ps[0][:, 0:H0], ACT.Silu).then_inc(silu_ready[layer], 1)
                        else:
                            A(sgs[:, 0:2 * H1].rearrange("p (j h) -> p j h", j=2),
                              ps[0][:, :].rearrange("p (j a h) -> p j a h", j=2, a=2)[:, :, 0, :], ACT.Silu)\
                                .then_inc(silu_ready[layer], 1)
                        if not (static(n) and n == NS - 1):
                            rowsT(n + 1)
                    if b is not None:
                        act.wait_ge(ys_in_psum[layer], b + 1)
                        if not (static(b) and b < 2):
                            act.wait_ge(ys_stored[layer][1 - p], (b // 2) * 16)
                        w = D * JT[layer]
                        A(ys[:, 1 - p, 0:JT[layer], :].rearrange("p j d -> p (j d)"), ps[3][:, 0:w], ACT.Copy)\
                            .then_inc(ys_ready[layer], 1)

                body(0, None, 0)
                body(1, 0, 1)
                body(2, 1, 0)
                with act.Fori(1, (NS - 3) // 2) as i:
                    body(i * 2 + 1, i * 2, 1)
                    body(i * 2 + 2, i * 2 + 1, 0)
                body(NS - 2, NS - 3, 1)
                body(NS - 1, NS - 2, 0)
                body(None, NS - 1, 1)

            act.wait_ge(xn1_kept, NB)
            shared(0)
            sorted_tiles(0)
            attention(1)
            act.wait_ge(centred, 1)
            A(rw[1], rw[0], ACT.Exp).then_inc(exp_ready, 1)
            act.wait_ge(xn1_kept, 2 * NB)
            shared(1)
            sorted_tiles(1)

        @block.tensor
        def _(pe):
            mm, tr = nc.tensor.matmul, nc.tensor.transpose

            def attention(layer):
                wq, wk, wv, wo = (w_att[:, layer, i] for i in range(4))
                r0 = E0 if layer else 0
                ne = E1 if layer else E0

                def first(i):
                    return layer == 0 and static(i) and i == 0

                def body(n, b, c, mlp_on=True):
                    def weightsT(j):
                        pe.wait_ge(probs_ready, at(layer, b) * 4 + j + 1)
                        if j == 0 and not first(b):
                            pe.wait_ge(attnT_ready, at(layer, b))
                        if j == 1:
                            done = at(layer, b) - (0 if static(b) and b == 0 else 1)
                            if not (static(done) and done <= 0):
                                pe.wait_ge(lg_ready, done)
                        if j >= 2:
                            pe.wait_ge(pt_ready, at(layer, b) * 4 + j - 1)
                        bank = ps_pa if j % 2 == 0 else ps_pb
                        for i in range(4):
                            last = tr(bank[:, i * P:(i + 1) * P], pr[:, j, i, :], ident)
                        last.then_inc(pt_in_psum, 1)

                    def values(j):
                        pe.wait_ge(pt_ready, at(layer, b) * 4 + j + 1)
                        if j == 0:
                            pe.wait_ge(v_ready, at(layer, b) + 1)
                            if not first(b):
                                pe.wait_ge(x1_ready, at(layer, b))
                        for i in range(4):
                            h = head_of(j, i)
                            last = mm(ps_po[:, h * VW:(h + 1) * VW], pt[:, j, i, :], va[:, h, :], start=True, stop=True)
                        if j == 3:
                            last.then_inc(av_in_psum, 1)

                    if n is not None:
                        pe.wait_ge(ctx_k_in, (at(layer, n) + 1) * 16)
                        if not first(n):
                            pe.wait_ge(v_ready, at(layer, n))
                        for m in range(KC):
                            for k in range(KC):
                                last = mm(ps_pm[:, m * P:(m + 1) * P], wk[:, k, m * P:(m + 1) * P], ctx_k[:, k, :],
                                          start=(k == 0), stop=(k == KC - 1))
                        last.then_inc(k_in_psum, 1)
                    if b is not None:
                        weightsT(0)
                        weightsT(1)
                    if n is not None:
                        pe.wait_ge(xn_ready, at(layer, n) + 1)
                        pe.wait_ge(kz_ready, at(layer, n) + 1)
                        for k in range(KC):
                            last = tr(ps_pm[:, k * P:(k + 1) * P], xn[:, k * P:(k + 1) * P], ident)
                        last.then_inc(xnT_in_psum, 1)
                    if b is not None:
                        weightsT(2)
                    if n is not None:
                        pe.wait_ge(xnT_ready, at(layer, n) + 1)
                        for m in range(KC):
                            for k in range(KC):
                                last = mm(ps_pm[:, m * P:(m + 1) * P], wq[:, k, m * P:(m + 1) * P], xnT[:, k, :],
                                          start=(k == 0), stop=(k == KC - 1))
                        last.then_inc(q_in_psum, 1)
                    if b is not None:
                        weightsT(3)
                        values(0)
                    if n is not None:
                        pe.wait_ge(q_ready, at(layer, n) + 1)
                        if not first(n):
                            pe.wait_ge(shifted, at(layer, n) * 4)
                        for k in range(KC):
                            for j in range(NBANK):
                                r = slice(32 * j, 32 * j + 32)
                                last = mm(ps_s[j][:, k * 256:(k + 1) * 256], qT[r, k, :],
                                          kz[r, k].rearrange("p h s -> p (h s)"), start=True, stop=True)
                        last.then_inc(scores_in_psum, 1)
                    if b is not None:
                        values(1)
                        values(2)
                        values(3)
                    if n is not None:
                        pe.wait_ge(ctx_v_in, (at(layer, n) + 1) * 16)
                        for k in range(KC):
                            last = mm(ps_pm[:, 0:D], ctx_v[:, k, :], wv[:, k, :], start=(k == 0), stop=(k == KC - 1))
                        last.then_inc(v_in_psum, 1)
                    if c is not None:
                        pe.wait_ge(xn1_ready, at(layer, c) + 1)
                        pe.wait_ge(pt_ready, (at(layer, c) + (2 if b is not None else 1)) * 4)
                        if b is None:
                            pe.wait_ge(lg_ready, at(layer, c))
                        for k in range(KC):
                            last = tr(ps_pb[:, k * P:(k + 1) * P], xn1[:, k * P:(k + 1) * P], ident)
                        last.then_inc(xn1T_in_psum, 1)
                    if b is not None:
                        pe.wait_ge(attn_ready, at(layer, b) + 1)
                        pe.wait_ge(pt_ready, at(layer, b) * 4 + 3)
                        for k in range(KC):
                            last = tr(ps_pa[:, k * P:(k + 1) * P], attn[:, k * P:(k + 1) * P], ident)
                        last.then_inc(attnT_in_psum, 1)
                    if c is not None:
                        pe.wait_ge(xn1T_ready, at(layer, c) + 1)
                        pe.wait_ge(xnT_kept, at(layer, c) + 1)
                        for k in range(KC):
                            last = mm(ps_pb[:, 0:ne], xn1T[:, k, :], rt[:, k, r0:r0 + ne], start=(k == 0), stop=(k == KC - 1))
                        last.then_inc(lg_in_psum, 1)
                    if b is not None:
                        pe.wait_ge(attnT_ready, at(layer, b) + 1)
                        for k in range(KC):
                            last = mm(ps_po[:, 0:D], attnT[:, k, :], wo[:, k, :], start=(k == 0), stop=(k == KC - 1))
                        last.then_inc(wo_in_psum, 1)

                pipeline(pe, body)

            pe.wait_ge(consts_in, 16)
            pe.wait_ge(watt0_in, 16)
            pe.wait_ge(small_in, 64)
            attention(0)

            def ranks(layer):
                w = NB * (E1 if layer else E0)
                pe.wait_ge(picks_ready[layer], 1)
                mm(ps_pm[:, 0:w], tri, picks[:, 0:w], start=True, stop=True)
                mm(ps_po[:, 0:w], ones, picks[:, 0:w], start=True, stop=True).then_inc(ranks_in_psum[layer], 1)

            def shared(layer, groups=None):
                wd = 2 * KC * H0 if layer == 0 else (CONV + 1) * KC * H1

                def down(g, c, q):
                    h = half(layer, g, c)
                    pe.wait_ge(sh_hidden[layer], q + 1)
                    if c == 0 and not (static(g) and g == 0):
                        pe.wait_ge(sh_added[layer], g * MG)
                    last_c = c == HC0 - 1 or layer == 1
                    for i in range(MG):
                        last = mm(ps[4 + i][:, 0:D], hT[:, h, i * P:(i + 1) * P], w_sh[:, wd + c * D:wd + (c + 1) * D],
                                  start=(c == 0), stop=last_c)
                    last.then_inc(sh_used[layer], 1)

                def body(g, c, q):
                    h = half(layer, g, c)
                    if not static(q) or q >= 2:
                        pe.wait_ge(sh_hidden[layer], q - 1)
                    batches = bass.ds(g * MG, MG)
                    gate, up = ps[h][:, :].rearrange("p (b s) -> p b s", b=MG), \
                        ps[2 + h][:, :].rearrange("p (b s) -> p b s", b=MG)
                    if layer == 0:
                        for o, to in ((0, gate), (H0, up)):
                            for k in range(KC):
                                at_w = k * 2 * H0 + o + c * P
                                last = mm(to, w_sh[:, at_w:at_w + P], xnT_all[:, k, batches, 2:PADW],
                                          start=(k == 0), stop=(k == KC - 1))
                    else:
                        for k in range(KC):
                            for o in range(CONV):
                                at_w = (k * CONV + o) * H1
                                mm(gate, w_sh[:, at_w:at_w + H1], xnT_all[:, k, batches, o:o + P],
                                   start=(k == 0 and o == 0), stop=(k == KC - 1 and o == CONV - 1))
                        for k in range(KC):
                            at_w = (KC * CONV + k) * H1
                            last = mm(up, w_sh[:, at_w:at_w + H1], xnT_all[:, k, batches, 2:PADW],
                                      start=(k == 0), stop=(k == KC - 1))
                    last.then_inc(sh_gu_in_psum[layer], 1)
                    if layer == 1 or c > 0:
                        if layer == 0:
                            down(g, c - 1, q - 1)
                        elif g > 0:
                            down(g - 1, 0, q - 1)
                    elif not static(g):
                        down(g - 1, HC0 - 1, q - 1)

                shared_steps(pe, layer, body)
                g = NB // MG - 1
                down(g, HC0 - 1 if layer == 0 else 0, (g + 1) * HC0 - 1 if layer == 0 else g)

            def sorted_tiles(layer):
                nj = JT[layer]

                def rowsT(n, p):
                    pe.wait_ge(xs_in[layer][p], (n // 2 + 1) * 16)
                    if not (static(n) and n == 0):
                        pe.wait_ge(xsT_ready[layer], n)
                    for j in range(nj):
                        for k in range(KC):
                            last = tr(ps[4][:, (j * KC + k) * P:(j * KC + k + 1) * P], xs[:, p, j, k * P:(k + 1) * P],
                                      ident)
                    last.then_inc(xsT_in_psum[layer], 1)

                def expert(n, j):
                    apart(pe)
                    if layer == 0:
                        return pe.value_load(tile_expert[0:1, bass.ds(n, 1)], min_val=0, max_val=E0 - 1)
                    return pe.value_load(tile_expert[0:1, bass.ds(n * 2 + j, 1)], min_val=0, max_val=R1 - 1)

                def body(n, b, p):
                    if b is not None:
                        pe.wait_ge(hs_ready[layer], b + 1)
                        if not (static(b) and b == 0):
                            pe.wait_ge(hsT_ready[layer], b)
                        for k in range(HC0 if layer == 0 else 2):
                            last = tr(ps[2][:, k * P:(k + 1) * P], hs[:, k * P:(k + 1) * P], ident)
                        last.then_inc(hsT_in_psum[layer], 1)
                    if n is not None:
                        if static(n) and n == 0:
                            rowsT(0, 0)
                        pe.wait_ge(xsT_ready[layer], n + 1)
                        for j in range(nj):
                            e = expert(n, j)
                            if layer == 0:
                                for o in range(2):
                                    for k in range(KC):
                                        at_w = k * 2 * H0 + o * H0
                                        last = mm(ps[o][:, :], xsT[:, k * P:(k + 1) * P], w_ffn[:, e, at_w:at_w + H0],
                                                  start=(k == 0), stop=(k == KC - 1))
                            else:
                                for k in range(KC):
                                    last = mm(ps[0][:, j * 256:(j + 1) * 256],
                                              xsT[:, (j * KC + k) * P:(j * KC + k + 1) * P],
                                              w1_ffn[:, e, k * 256:(k + 1) * 256], start=(k == 0), stop=(k == KC - 1))
                        last.then_inc(gu_in_psum[layer], 1)
                        if not (static(n) and n == NS - 1):
                            rowsT(n + 1, 1 - p)
                    if b is not None:
                        pe.wait_ge(hsT_ready[layer], b + 1)
                        if not (static(b) and b == 0):
                            pe.wait_ge(ys_ready[layer], b)
                        for j in range(nj):
                            e = expert(b, j)
                            if layer == 0:
                                for k in range(HC0):
                                    at_w = 2 * KC * H0 + k * D
                                    last = mm(ps[3][:, 0:D], hsT[:, k * P:(k + 1) * P], w_ffn[:, e, at_w:at_w + D],
                                              start=(k == 0), stop=(k == HC0 - 1))
                            else:
                                last = mm(ps[3][:, j * D:(j + 1) * D], hsT[:, j * P:(j + 1) * P],
                                          w1_ffn[:, e, 512:768], start=True, stop=True)
                        last.then_inc(ys_in_psum[layer], 1)

                body(0, None, 0)
                body(1, 0, 1)
                body(2, 1, 0)
                with pe.Fori(1, (NS - 3) // 2) as i:
                    body(i * 2 + 1, i * 2, 1)
                    body(i * 2 + 2, i * 2 + 1, 0)
                body(NS - 2, NS - 3, 1)
                body(NS - 1, NS - 2, 0)
                body(None, NS - 1, 1)

            def ffn(layer):
                pe.wait_ge(lg_ready, NB * (layer + 1))
                pe.wait_ge(x1_ready, NB * (layer + 1))
                ranks(layer)
                pe.wait_ge(ffn_in[0] if layer == 0 else ffn_in[3], 16 if layer == 0 else 32)
                pe.wait_ge(slots_ready[layer], 1)
                shared(layer)
                pe.wait_ge(sh_added[layer], NB)
                if layer == 0:
                    pe.wait_ge(ffn_in[1], 48)
                    pe.wait_ge(ffn_in[2], 80)
                sorted_tiles(layer)

            ffn(0)
            pe.wait_ge(ys_ready[0], NS)
            pe.wait_ge(watt1_in, 16)
            attention(1)
            ffn(1)

        @block.vector
        def _(dve):
            V = nc.vector

            def attention(layer):
                def stats(n):
                    if layer:
                        dve.wait_ge(x2_ready, n + 1)
                        apart(dve)
                    apart(dve)
                    V.bn_stats(ln_st[:, 0, :], x_res[:, n, :]).then_inc(stats_done, 1)
                    dve.wait_ge(stats_done, at(layer, n) + 1)
                    apart(dve)
                    V.bn_aggr(ln_mv[:, 0, :], ln_st[:, 0, :]).then_inc(aggr_done, 1)
                    dve.wait_ge(aggr_done, at(layer, n) + 1)
                    V.tensor_scalar(ln_ve[:, 0:1], ln_mv[:, 0, 1:2], EPS, None, ALU.add).then_inc(var_ready, 1)

                def normalise(n):
                    dve.wait_ge(rstd_ready, at(layer, n) + 1)
                    if not (layer == 0 and static(n) and n == 0):
                        dve.wait_ge(xnT_in_psum, at(layer, n))
                    V.tensor_scalar(xn[:], x_res[:, n, :], ln_mv[:, 0, 0:1], ln_rs[:, 0:1], ALU.subtract, ALU.mult)\
                        .then_inc(xn_ready, 1)

                def shift(n, j):
                    first = layer == 0 and static(n) and n == 0
                    s4 = ps_s[j][:, :].rearrange("p (i s) -> p i s", i=4)
                    if layer == 0:
                        if not first:
                            dve.wait_ge(probs_ready, at(layer, n) * 4 - 3 + j)
                        V.tensor_tensor(sc[:, j], s4, bias_all[:, n, :].unsqueeze(1).broadcast_to([P, 4, P]), ALU.add)\
                            .then_inc(biased, 1)
                        dve.wait_ge(biased, at(layer, n) * 4 + j + 1)
                        s4 = sc[:, j]
                    V.tensor_reduce(mx[:, j, :], s4, AX.X, ALU.max).then_inc(max_ready, 1)
                    dve.wait_ge(max_ready, at(layer, n) * 4 + j + 1)
                    if layer and not first:
                        dve.wait_ge(probs_ready, at(layer, n) * 4 - 3 + j)
                    V.tensor_tensor(sc[:, j], s4, mx[:, j, :].unsqueeze(2).broadcast_to([P, 4, P]), ALU.subtract)\
                        .then_inc(shifted, 1)

                def body(n, b, c, mlp_on=True):
                    if n is not None:
                        if layer == 0:
                            dve.wait_ge(bias_ready, n + 1)
                        dve.wait_ge(scores_in_psum, at(layer, n) + 1)
                        shift(n, 0)
                        shift(n, 1)
                    if b is not None:
                        dve.wait_ge(av_in_psum, at(layer, b) + 1)
                        po = ps_po[:, 0:NH * VW].rearrange("p (h d) -> p h d", h=NH)
                        V.reciprocal(rsum[:].unsqueeze(2), po[:, :, HD:VW]).then_inc(rsum_ready, 1)
                        dve.wait_ge(rsum_ready, at(layer, b) + 1)
                        if not (layer == 0 and static(b) and b == 0):
                            dve.wait_ge(attnT_in_psum, at(layer, b))
                        V.tensor_tensor(attn[:].rearrange("p (h d) -> p h d", h=NH), po[:, :, 0:HD],
                                        rsum[:].unsqueeze(2).broadcast_to([P, NH, HD]), ALU.mult).then_inc(attn_ready, 1)
                    if n is not None and layer:
                        dve.wait_ge(v_in_psum, at(layer, n) + 1)
                        V.tensor_tensor(va[:, :, 0:HD], ps_pm[:, 0:D].rearrange("p (h d) -> p h d", h=NH),
                                        bvo[:, 0, :].rearrange("p (h d) -> p h d", h=NH), ALU.add).then_inc(v_ready, 1)
                    if n is not None:
                        shift(n, 2)
                        shift(n, 3)
                    if b is not None:
                        dve.wait_ge(wo_in_psum, at(layer, b) + 1)
                        if layer:
                            dve.wait_ge(bo_added, b + 1)
                        V.tensor_tensor(x_res[:, b, :], ps_po[:, 0:D], x_res[:, b, :], ALU.add).then_inc(x1_ready, 1)
                        dve.wait_ge(x1_ready, at(layer, b) + 1)
                        apart(dve)
                        V.bn_stats(ln_st[:, 1, :], x_res[:, b, :]).then_inc(stats1_done, 1)
                        dve.wait_ge(stats1_done, at(layer, b) + 1)
                        apart(dve)
                        V.bn_aggr(ln_mv[:, 1, :], ln_st[:, 1, :]).then_inc(aggr1_done, 1)
                        dve.wait_ge(aggr1_done, at(layer, b) + 1)
                        V.tensor_scalar(ln_ve[:, 1:2], ln_mv[:, 1, 1:2], EPS, None, ALU.add).then_inc(var1_ready, 1)
                    if n is not None and not (static(n) and n == NB - 1):
                        stats(n + 1)
                        normalise(n + 1)
                    if b is not None:
                        dve.wait_ge(rstd1_ready, at(layer, b) + 1)
                        if not (layer == 0 and static(b) and b == 0):
                            dve.wait_ge(xn1T_in_psum, at(layer, b))
                            dve.wait_ge(xn1_kept, at(layer, b))
                        V.tensor_scalar(xn1[:], x_res[:, b, :], ln_mv[:, 1, 0:1], ln_rs[:, 1:2],
                                        ALU.subtract, ALU.mult).then_inc(xn1_ready, 1)

                stats(0)
                normalise(0)
                body(0, None, None)
                body(1, 0, None)
                body(2, 1, 0)
                with dve.Fori(3, NB - 1) as n:
                    body(n, n - 1, n - 2)
                body(NB - 1, NB - 2, NB - 3)
                body(None, NB - 1, NB - 2)

            dve.wait_ge(x0_in, 16)
            dve.wait_ge(dist_in, 32)
            dve.wait_ge(mlp_in, 16)
            V.tensor_scalar(qs_all.rearrange("p b s -> p (b s)"), dist.rearrange("p b s -> p (b s)"), 0.0, bb2,
                            ALU.mult, ALU.add).then_inc(setup_dve, 1)
            dve.wait_ge(x_in, 16)
            dve.wait_ge(small_in, 64)
            dve.wait_ge(consts_in, 16)
            V.tensor_scalar(qb4[:], qkb[:, 0, :], 0.25, None, ALU.mult).then_inc(setup_dve, 1)
            for k in range(KC):
                V.tensor_scalar(kbm[:, k, :], par, qkb[:, 1, k:k + 1], None, ALU.mult).then_inc(setup_dve, 1)
            attention(0)

            chain = [0]

            def then(instruction):
                chain[0] += 1
                instruction.then_inc(route_step, 1)
                dve.wait_ge(route_step, chain[0])

            def routing(layer):
                ne = E1 if layer else E0
                w = NB * ne
                be = lambda v: v[:, 0:w].rearrange("p (b e) -> p b e", b=NB)
                eb = lambda v: v[:, 0:w].rearrange("p (e b) -> p e b", e=ne)
                over_e = lambda v: v.unsqueeze(2).broadcast_to([P, NB, ne])
                over_b = lambda v: v.unsqueeze(1).broadcast_to([P, NB, ne])
                prio = cst[:, C_PRI:C_PRI + ne]
                dve.wait_ge(lg_ready, NB * (layer + 1))
                dve.wait_ge(xn1_kept, NB * (layer + 1))

                def pick(values, to, best):
                    then(V.tensor_reduce(best, values, AX.X, ALU.max))
                    then(V.tensor_tensor(be(rw[7]), values, over_e(best), ALU.is_equal))
                    then(V.tensor_tensor(be(rw[7]), be(rw[7]), over_b(prio), ALU.mult))
                    then(V.tensor_reduce(small[:, 7, :], be(rw[7]), AX.X, ALU.max))
                    then(V.tensor_tensor(to, be(rw[7]), over_e(small[:, 7, :]), ALU.is_equal))

                if layer == 0:
                    pick(lg[:, :, 0:ne], be(rw[3]), small[:, 0, :])
                    then(V.tensor_copy(picks[:, 0:w], rw[3][:, 0:w]))
                    chosen = [rw[3]]
                else:
                    then(V.tensor_tensor(be(rw[0]), lg[:], over_b(rbias[:]), ALU.add))
                    then(V.tensor_reduce(small[:, 0, :], be(rw[0]), AX.X, ALU.max))
                    V.tensor_tensor(be(rw[0]), be(rw[0]), over_e(small[:, 0, :]), ALU.subtract).then_inc(centred, 1)
                    dve.wait_ge(exp_ready, 1)
                    then(V.tensor_reduce(small[:, 1, :], be(rw[1]), AX.X, ALU.add))
                    then(V.reciprocal(small[:, 2, :], small[:, 1, :]))
                    then(V.tensor_tensor(be(rw[2]), be(rw[1]), over_e(small[:, 2, :]), ALU.mult))
                    pick(be(rw[2]), be(rw[3]), small[:, 3, :])
                    then(V.scalar_tensor_tensor(rw[4], rw[3], -2.0, rw[2], ALU.mult, ALU.add))
                    pick(be(rw[4]), be(rw[5]), small[:, 4, :])
                    then(V.tensor_tensor(picks[:, 0:w], rw[3], rw[5], ALU.add))
                    then(V.tensor_tensor(small[:, 5, :], small[:, 3, :], small[:, 4, :], ALU.add))
                    then(V.tensor_scalar(small[:, 5, :], small[:, 5, :], 1e-6, None, ALU.add))
                    then(V.reciprocal(small[:, 6, :], small[:, 5, :]))
                    then(V.tensor_tensor(wgt[:, 0, :], small[:, 3, :], small[:, 6, :], ALU.mult))
                    then(V.tensor_tensor(wgt[:, 1, :], small[:, 4, :], small[:, 6, :], ALU.mult))
                    chosen = [rw[3], rw[5]]
                then(V.tensor_copy(small[:, 7, :], small[:, 0, :]))
                V.tensor_copy(small[:, 6, :], small[:, 0, :]).then_inc(picks_ready[layer], 1)
                dve.wait_ge(ranks_in_psum[layer], 1)
                then(V.tensor_copy(eb(rw[8]), be(ps_po).rearrange("p b e -> p e b")))
                then(V.tensor_tensor_scan(rw[9][:, 0:w], seg[:, 0:w], rw[8][:, 0:w], 0.0, ALU.mult, ALU.add))
                total = eb(rw[9])[:, :, NB - 1]
                need, upto = small[:, 1, 0:ne], small[:, 2, 0:ne]
                then(V.tensor_scalar(need_i[:, 0:ne], total, float(P - 1), None, ALU.add))
                then(V.tensor_scalar(need_i[:, 0:ne], need_i[:, 0:ne], P.bit_length() - 1, None, ALU.arith_shift_right))
                then(V.tensor_copy(need, need_i[:, 0:ne]))
                then(V.tensor_tensor_scan(upto, ones[:, 0:ne], need, 0.0, ALU.mult, ALU.add))
                then(V.tensor_tensor(small[:, 3, 0:ne], upto, need, ALU.subtract))
                if layer:
                    then(V.memset(small[:, 3, R1:E1], float(T1)))
                then(V.tensor_scalar(small[:, 3, 0:ne], small[:, 3, 0:ne], float(P), None, ALU.mult))
                then(V.tensor_tensor(rw[9][:, 0:w], rw[9][:, 0:w], rw[8][:, 0:w], ALU.subtract))
                then(V.tensor_tensor(be(rw[10]), be(ps_pm), eb(rw[9]).rearrange("p e b -> p b e"), ALU.add))
                then(V.tensor_tensor(be(rw[10]), be(rw[10]), over_b(small[:, 3, 0:ne]), ALU.add))
                for a, one in enumerate(chosen):
                    then(V.tensor_tensor(be(rw[11]), be(rw[10]), be(one), ALU.mult))
                    then(V.tensor_reduce(small[:, 4 + a, :], be(rw[11]), AX.X, ALU.add))
                    then(V.tensor_copy(slot[:, a, :], small[:, 4 + a, :]))
                nt, nr = (T1, R1) if layer else (T0, E0)
                big = work[:, 2048:2048 + nt * nr].rearrange("p (t e) -> p t e", t=nt)
                then(V.tensor_tensor(big, upto[:, 0:nr].unsqueeze(1).broadcast_to([P, nt, nr]),
                                     cst[:, C_TIL:C_TIL + nt].unsqueeze(2).broadcast_to([P, nt, nr]), ALU.is_le))
                then(V.tensor_reduce(te_f[:, 0:nt], big, AX.X, ALU.add))
                then(V.tensor_scalar(te_f[:, 0:nt], te_f[:, 0:nt], float(nr - 1), None, ALU.min))
                V.tensor_copy(tile_expert[:, 0:nt], te_f[:, 0:nt]).then_inc(slots_ready[layer], 1)

            def shared(layer):
                def add(g):
                    dve.wait_ge(sh_used[layer], g * HC0 + HC0 if layer == 0 else g + 1)
                    for i in range(MG):
                        V.tensor_tensor(x_res[:, g * MG + i, :], ps[4 + i][:, 0:D], x_res[:, g * MG + i, :], ALU.add)\
                            .then_inc(sh_added[layer], 1)

                def body(g, c, q):
                    h = half(layer, g, c)
                    dve.wait_ge(sh_silu[layer], q + 1)
                    if not static(q) or q >= 2:
                        dve.wait_ge(sh_used[layer], q - 1)
                    V.tensor_tensor(hT[:, h, :], ps[2 + h][:, :], sg[:, h, :], ALU.mult).then_inc(sh_hidden[layer], 1)
                    if c == 0 and not (static(g) and g == 0):
                        add(g - 1)

                shared_steps(dve, layer, body)
                add(NB // MG - 1)

            def sorted_tiles(layer):
                def body(n):
                    dve.wait_ge(silu_ready[layer], n + 1)
                    if not (static(n) and n == 0):
                        dve.wait_ge(hsT_in_psum[layer], n)
                    if layer == 0:
                        V.tensor_tensor(hs[:, 0:H0], ps[1][:, :], sgs[:, 0:H0], ALU.mult).then_inc(hs_ready[layer], 1)
                    else:
                        V.tensor_tensor(hs[:, 0:2 * H1].rearrange("p (j h) -> p j h", j=2),
                                        ps[0][:, :].rearrange("p (j a h) -> p j a h", j=2, a=2)[:, :, 1, :],
                                        sgs[:, 0:2 * H1].rearrange("p (j h) -> p j h", j=2), ALU.mult)\
                            .then_inc(hs_ready[layer], 1)
                body(0)
                with dve.Fori(1, NS) as n:
                    body(n)

            routing(0)
            shared(0)
            sorted_tiles(0)
            dve.wait_ge(ys_ready[0], NS)
            attention(1)
            routing(1)
            shared(1)
            sorted_tiles(1)
            for g in range(NB // MG):
                dve.wait_ge(gathered[g], 2 * MG * 16)
                for b in range(g * MG, (g + 1) * MG):
                    V.scalar_tensor_tensor(x_res[:, b, :], xn_all[:, b, :], wgt[:, 0, b:b + 1], x_res[:, b, :],
                                           ALU.mult, ALU.add).then_inc(weighted, 1)
                for b in range(g * MG, (g + 1) * MG):
                    dve.wait_ge(weighted, b + 1)
                    last = V.scalar_tensor_tensor(x_res[:, b, :], rows_b[:, b, :], wgt[:, 1, b:b + 1], x_res[:, b, :],
                                                  ALU.mult, ALU.add)
                last.then_inc(out_ready, 1)


def static(i):
    return isinstance(i, int)


def kernel(**inputs):
    import numpy as _np
    import concourse.bacc as _bacc
    from concourse import mybir as _mybir
    from concourse.bass_utils import run_bass_kernel_spmd as _run

    a = {k: _np.asarray(v) for k, v in inputs.items()}

    def chunks(w):
        return w.reshape(w.shape[0] // P, P, -1).transpose(1, 0, 2)

    cst = _np.zeros((P, C_END), _np.float32)
    i = _np.arange(P)
    cst[:, C_ID:C_ID + P] = i[:, None] == i[None, :]
    cst[:, C_TRI:C_TRI + P] = i[:, None] < i[None, :]
    cst[:, C_ONE:C_ONE + P] = 1
    cst[:, C_PAR] = i % 32 < HD
    cst[:, C_PAR + 1] = i % 32 >= HD
    cst[:, C_PRI:C_PRI + E1] = E1 - _np.arange(E1)
    cst[:, C_TIL:C_SEG] = _np.arange(C_SEG - C_TIL)
    cst[:, C_SEG:C_END] = _np.arange(NB * E1) % NB > 0
    bc = lambda v: _np.ascontiguousarray(_np.broadcast_to(v.reshape(1, -1), (P, v.size)))
    host = {
        "consts": cst,
        "x": a["x"].transpose(1, 0, 2),
        "ctxT": chunks(a["ctx_1024"].reshape(NB * P, D).T),
        "dist": a["fside_BxSxS2_0"].transpose(1, 0, 2),
        "mask": a["mask_Bx1xSxS2_ff0"][:, 0].transpose(1, 0, 2),
        "w_att0": _np.stack([chunks(a["L0_xattn_Wq"].reshape(D, D)), chunks(a["L0_xattn_Wk"].reshape(D, D)),
                             chunks(a["L0_xattn_Wv"].reshape(D, D)), chunks(a["L0_xattn_Wo"].reshape(D, D))], 1),
        "w_att1": _np.stack([chunks(a["L1_xattn_W" + x].T) for x in "qkvo"], 1),
        "rt": chunks(_np.concatenate([a["L0_ffn_router"].T, a["L1_ffn_router_w"]], 1)),
        "mlp": bc(_np.concatenate([a["L0_xattn_Wb1"][0], a["L0_xattn_bb1"], a["L0_xattn_Wb2"][:, 0],
                                   a["L0_xattn_bb2"]])),
        "qkb": _np.stack([a["L1_xattn_bq"].reshape(KC, P).T, a["L1_xattn_bk"].reshape(KC, P).T], 1),
        "bvo": bc(_np.concatenate([a["L1_xattn_bv"], a["L1_xattn_bo"]])).reshape(P, 2, D),
        "w_ffn0": _np.concatenate([
            _np.concatenate([a["L0_ffn_gate"], a["L0_ffn_up"]], 1).transpose(2, 0, 1)
            .reshape(KC, P, E0, 2 * H0).transpose(1, 2, 0, 3).reshape(P, E0, -1),
            a["L0_ffn_down"].transpose(2, 0, 1).reshape(HC0, P, E0, D).transpose(1, 2, 0, 3).reshape(P, E0, -1)], 2),
        "w_sh0": _np.concatenate([
            chunks(_np.concatenate([a["L0_ffn_w_gate_s"], a["L0_ffn_w_up_s"]], 0).T).reshape(P, -1),
            chunks(a["L0_ffn_w_down_s"].T).reshape(P, -1)], 1),
        "w_ffn1": _np.concatenate([
            _np.concatenate([a["L1_ffn_expert_gate_w"], a["L1_ffn_expert_up_w"]], 2).transpose(1, 0, 2)
            .reshape(KC, P, R1, 2 * H1).transpose(1, 2, 0, 3).reshape(P, R1, -1),
            a["L1_ffn_expert_down_w"].transpose(1, 0, 2)], 2),
        "w_sh1": _np.concatenate([
            a["L1_ffn_conv_w"].transpose(1, 2, 0).reshape(KC, P, CONV * H1).transpose(1, 0, 2).reshape(P, -1),
            chunks(a["L1_ffn_shared_up_w"]).reshape(P, -1), a["L1_ffn_shared_down_w"]], 1),
        "rbias": bc(a["L1_ffn_router_bias"]),
    }
    nc = _bacc.Bacc("TRN2", target_bir_lowering=False, num_devices=1)
    arrays, aps = {}, {}
    for name, v in host.items():
        v = _np.ascontiguousarray(v)
        arrays[f"in_{name}"] = v
        aps[name] = nc.dram_tensor(f"in_{name}", v.shape, _mybir.dt.from_np(v.dtype), kind="ExternalInput").ap()
    out = nc.dram_tensor("out_0", (NB, P, D), _mybir.dt.float32, kind="ExternalOutput").ap()
    rows = [nc.dram_tensor("rows0", (T0 * P, D), _mybir.dt.float32).ap(),
            nc.dram_tensor("rows1", ((T1 + NB) * P, D), _mybir.dt.float32).ap()]
    build_program(nc, aps, out, rows)
    r = _run(nc, [arrays], core_ids=[0])
    return r.results[0]["out_0"]
```

```python
from contextlib import ExitStack

import numpy as np
import concourse.bass as bass
from concourse import mybir

F32 = mybir.dt.float32
I32 = mybir.dt.int32
U32 = mybir.dt.uint32
ALU = mybir.AluOpType
ACT = mybir.ActivationFunctionType
AX = mybir.AxisListType

P = 128
NB = 16
D = 256
KC = D // P
NH, HD = 16, 16
NBANK = 4
VW = HD + 1
KB = 16
MG = 4
PADW = P + 2
EPS = 1e-5

E0, H0 = 8, 512
HC0 = H0 // P
T0 = (NB * P + E0 * (P - 1)) // P
W0 = KC * 2 * H0 + HC0 * D

E1, H1 = 16, 128
R1 = E1 - 1
T1 = (2 * NB * P + R1 * (P - 1)) // P
W1 = KC * 2 * H1 + D
CONV = 3

JT = (1, 2)
NS = T0
assert NS * JT[0] == T0 and NS * JT[1] == T1 and NS % 2 == 1

C_ID, C_TRI, C_ONE, C_PAR, C_PRI, C_TIL = 0, 128, 256, 384, 386, 402
C_SEG = C_TIL + 48
C_END = C_SEG + NB * E1


def head_of(bank, i):
    return (i // 2) * 8 + 2 * bank + i % 2


def build_program(nc, t, out, rows):
    with ExitStack() as ctx:
        def sb(name, shape, dt=F32):
            return ctx.enter_context(nc.sbuf_tensor(name, shape, dt))

        def sem(name):
            return ctx.enter_context(nc.semaphore(name))

        ps = [ctx.enter_context(nc.psum_tensor(f"bank{i}", [P, 512], F32)) for i in range(8)]
        ps_s, ps_pa, ps_pb, ps_pm, ps_po = ps[0:4], ps[4], ps[5], ps[6], ps[7]

        cst = sb("cst", [P, C_END])
        ident, tri, ones = cst[:, C_ID:C_ID + P], cst[:, C_TRI:C_TRI + P], cst[:, C_ONE:C_ONE + P]
        par = cst[:, C_PAR:C_PAR + 2]
        x_res = sb("x_res", [P, NB, D])
        xn_all = sb("xn_all", [P, NB, D])
        xnT_all = sb("xnT_all", [P, KC, NB, PADW])
        w_att = sb("w_att", [P, 2, 4, KC, D])
        rt = sb("rt", [P, KC, E0 + E1])
        w_ffn = sb("w_ffn", [P, E0, W0])
        w_sh = sb("w_sh", [P, W0])
        sc = w_ffn[:, 7, 0:2048].rearrange("p (g i s) -> p g i s", g=NBANK, i=4)
        pr = w_ffn[:, 6, 0:2048].rearrange("p (g i s) -> p g i s", g=NBANK, i=4)
        pt = w_ffn[:, 5, 0:2048].rearrange("p (g i s) -> p g i s", g=NBANK, i=4)
        dist = w_ffn[:, 4, 0:2048].rearrange("p (b s) -> p b s", b=NB)
        bias_all = w_ffn[:, 3, 0:2048].rearrange("p (b s) -> p b s", b=NB)
        hid = [w_ffn[:, 4 + i, 2048:2560] for i in range(4)]

        mlp = sb("mlp", [P, 3 * KB + 1])
        a_bc, b_bc, c_bc, bb2 = mlp[:, 0:KB], mlp[:, KB:2 * KB], mlp[:, 2 * KB:3 * KB], mlp[:, 3 * KB:3 * KB + 1]
        qkb = sb("qkb", [P, 2, KC])
        qb4 = sb("qb4", [P, KC])
        kbm = sb("kbm", [P, KC, 2])
        bvo = sb("bvo", [P, 2, D])
        rbias = sb("rbias", [P, E1])
        work = sb("work", [P, 5120])

        def attention_tile(at_column, *shape):
            n = int(np.prod(shape))
            return work[:, at_column:at_column + n], at_column + n

        col = 0
        ctx_k, col = attention_tile(col, KC, P)
        ctx_v, col = attention_tile(col, KC, P)
        xn, col = attention_tile(col, D)
        xnT, col = attention_tile(col, KC, P)
        qT, col = attention_tile(col, KC, P)
        kz, col = attention_tile(col, KC, 2, P)
        attn, col = attention_tile(col, D)
        attnT, col = attention_tile(col, KC, P)
        xn1, col = attention_tile(col, D)
        xn1T, col = attention_tile(col, KC, P)
        ctx_k, ctx_v, xnT, qT, attnT, xn1T = (
            v.rearrange("p (k s) -> p k s", k=KC) for v in (ctx_k, ctx_v, xnT, qT, attnT, xn1T))
        kz = kz.rearrange("p (k h s) -> p k h s", k=KC, h=2)
        acc0, col = attention_tile(col, MG * P)
        acc, col = attention_tile(col, MG * P)
        sg = work[:, 3072:4096].rearrange("p (a s) -> p a s", a=2)
        hT = work[:, 4096:5120].rearrange("p (a s) -> p a s", a=2)
        xs = work[:, 2048:3072].rearrange("p (a j d) -> p a j d", a=2, j=2)
        xsT = work[:, 3072:3584]
        hs = work[:, 3584:4096]
        hsT = work[:, 0:512]
        sgs = work[:, 512:1024]
        ys = work[:, 4096:5120].rearrange("p (a j d) -> p a j d", a=2, j=2)
        rw = [work[:, 256 * i:256 * (i + 1)] for i in range(12)]
        va = sb("va", [P, NH, VW])
        mx = sb("mx", [P, NBANK, 4])
        rsum = sb("rsum", [P, NH])
        lg = sb("lg", [P, NB, E1])
        picks = rw[6]
        slot = sb("slot", [P, 2, NB], I32)
        step_experts = sb("step_experts", [P, NS], I32)
        wgt = sb("wgt", [P, 2, NB])
        small = sb("small", [P, 8, NB])
        need_i = sb("need_i", [P, E1], I32)
        te_f = sb("te_f", [P, T1])
        seg = cst[:, C_SEG:C_END]
        zeros = sb("zeros", [P, D])
        rows_b = xnT_all[:].rearrange("p k b s -> p (k b s)")[:, 0:NB * D].rearrange("p (b d) -> p b d", b=NB)
        w1_ffn = w_ffn[:, 0:4, :].rearrange("p a w -> p (a w)")[:, 0:R1 * W1].rearrange("p (e w) -> p e w", e=R1)
        ln_st = sb("ln_st", [P, 2, 6])
        ln_mv = sb("ln_mv", [P, 2, 2])
        ln_ve = sb("ln_ve", [P, 2])
        ln_rs = sb("ln_rs", [P, 2])
        mhalf = sb("mhalf", [P, 1])

        consts_in, x_in, mlp_in, dist_in, watt0_in, watt1_in, small_in = map(
            sem, ("consts_in", "x_in", "mlp_in", "dist_in", "watt0_in", "watt1_in", "small_in"))
        ctx_k_in, ctx_v_in = sem("ctx_k_in"), sem("ctx_v_in")
        x0_in, dist0_in, mask0_in = sem("x0_in"), sem("dist0_in"), sem("mask0_in")
        setup_pool, setup_dve = sem("setup_pool"), sem("setup_dve")
        stats_done, aggr_done, var_ready, rstd_ready = map(sem, ("stats_done", "aggr_done", "var_ready", "rstd_ready"))
        stats1_done, aggr1_done, var1_ready, rstd1_ready = map(
            sem, ("stats1_done", "aggr1_done", "var1_ready", "rstd1_ready"))
        xn_ready, xnT_in_psum, xnT_ready = map(sem, ("xn_ready", "xnT_in_psum", "xnT_ready"))
        k_in_psum, kz_ready, q_in_psum, q_ready = map(sem, ("k_in_psum", "kz_ready", "q_in_psum", "q_ready"))
        v_in_psum, v_ready = sem("v_in_psum"), sem("v_ready")
        scores_in_psum, biased, max_ready, shifted, probs_ready = map(
            sem, ("scores_in_psum", "biased", "max_ready", "shifted", "probs_ready"))
        pt_in_psum, pt_ready, av_in_psum, rsum_ready, attn_ready = map(
            sem, ("pt_in_psum", "pt_ready", "av_in_psum", "rsum_ready", "attn_ready"))
        attnT_in_psum, attnT_ready, wo_in_psum, x1_ready = map(
            sem, ("attnT_in_psum", "attnT_ready", "wo_in_psum", "x1_ready"))
        xn1_kept = sem("xn1_kept")
        xn1_ready, xn1T_in_psum, xn1T_ready, xnT_kept, lg_in_psum, lg_ready = map(
            sem, ("xn1_ready", "xn1T_in_psum", "xn1T_ready", "xnT_kept", "lg_in_psum", "lg_ready"))
        hid_ready, hid_scaled, hid0_added, hid_added, bias_ready, bo_added = map(
            sem, ("hid_ready", "hid_scaled", "hid0_added", "hid_added", "bias_ready", "bo_added"))
        stored = sem("stored")
        x2_ready, bv_ready = sem("x2_ready"), sem("bv_ready")
        zeros_set = sem("zeros_set")
        route_step = sem("route_step")
        rows_zeroed = [sem(f"rows_zeroed{i}") for i in range(2)]
        ffn_in = [sem(f"ffn_in{i}") for i in range(4)]
        centred, exp_ready = sem("centred"), sem("exp_ready")
        picks_ready = [sem(f"picks_ready{i}") for i in range(2)]
        ranks_in_psum = [sem(f"ranks_in_psum{i}") for i in range(2)]
        slots_ready = [sem(f"slots_ready{i}") for i in range(2)]
        experts_ready = [sem(f"experts_ready{i}") for i in range(2)]
        scattered = [sem(f"scattered{i}") for i in range(2)]
        gathered = [sem(f"gathered{i}") for i in range(5)]
        sh_gu_in_psum, sh_silu, sh_hidden, sh_used, sh_added = (
            [sem(f"{name}{i}") for i in range(2)]
            for name in ("sh_gu_in_psum", "sh_silu", "sh_hidden", "sh_used", "sh_added"))
        xs_in = [[sem(f"xs_in{i}{p}") for p in range(2)] for i in range(2)]
        ys_stored = [[sem(f"ys_stored{i}{p}") for p in range(2)] for i in range(2)]
        xsT_in_psum, xsT_ready, gu_in_psum, silu_ready, hs_ready, hsT_in_psum, hsT_ready, ys_in_psum, ys_ready = (
            [sem(f"{name}{i}") for i in range(2)]
            for name in ("xsT_in_psum", "xsT_ready", "gu_in_psum", "silu_ready", "hs_ready", "hsT_in_psum",
                         "hsT_ready", "ys_in_psum", "ys_ready"))
        weighted = sem("weighted")
        out_ready = sem("out_ready")
        waits_ended = sem("waits_ended")

        block = ctx.enter_context(nc.Block())

        def pipeline(eng, body):
            body(0, None, None, None)
            body(1, 0, None, None)
            body(2, 1, 0, None)
            body(3, 2, 1, 0)
            with eng.Fori(3, NB - 1) as n:
                body(n + 1, n, n - 1, n - 2)
            body(None, NB - 1, NB - 2, NB - 3)
            body(None, None, NB - 1, NB - 2)
            body(None, None, None, NB - 1)

        def apart(eng):
            eng.sem_inc(waits_ended, 1)

        SHARED = (((0, 1), (2, 3)), ((0, 1, 2, 3),))

        def shared_steps(layer, groups, body):
            chunks = HC0 if layer == 0 else 1
            for g in groups:
                for c in range(chunks):
                    body(g, c, g * chunks + c)

        def half(layer, g, c):
            return c % 2 if layer == 0 else g % 2

        def at(layer, b):
            return b + NB * layer

        @block.sync
        def _(sp):
            sp.dma_start(x_res[:, 0:2, :], t["x"][:, 0:2, :]).then_inc(x0_in, 16)
            sp.dma_start(cst[:], t["consts"]).then_inc(consts_in, 16)
            sp.dma_start(ctx_k[:], t["ctxT"][:, :, 0:P]).then_inc(ctx_k_in, 16)
            sp.dma_start(w_att[:, 0], t["w_att0"]).then_inc(watt0_in, 16)
            sp.dma_start(ctx_v[:], t["ctxT"][:, :, 0:P]).then_inc(ctx_v_in, 16)
            sp.dma_start(rt[:], t["rt"]).then_inc(small_in, 16)
            sp.dma_start(x_res[:, 2:NB, :], t["x"][:, 2:NB, :]).then_inc(x_in, 16)

            ZERO = (T0 // NB, (T1 + NB) // NB)

            def zero(i, start, tiles):
                sp.dma_start(rows[i][bass.ds(start * P, tiles * P)].rearrange("(t p) d -> p t d", p=P),
                             zeros[:].unsqueeze(1).broadcast_to([P, tiles, D])).then_inc(rows_zeroed[i], 16)

            def attention(layer):
                def load_k(n):
                    sp.wait_ge(k_in_psum, at(layer, n))
                    sp.dma_start(ctx_k[:], t["ctxT"][:, :, bass.ds(n * P, P)]).then_inc(ctx_k_in, 16)

                def load_v(n):
                    sp.wait_ge(v_in_psum, at(layer, n))
                    sp.dma_start(ctx_v[:], t["ctxT"][:, :, bass.ds(n * P, P)]).then_inc(ctx_v_in, 16)

                if layer:
                    load_k(0)
                    load_v(0)
                    sp.dma_start(w1_ffn, t["w_ffn1"]).then_inc(ffn_in[3], 16)
                load_k(1)
                with sp.Fori(1, NB - 1) as n:
                    load_k(n + 1)
                    load_v(n)
                    if layer == 0:
                        for i in range(2):
                            zero(i, n * ZERO[i], ZERO[i])
                if layer == 0:
                    sp.dma_start(w_sh[:], t["w_sh0"]).then_inc(ffn_in[0], 16)
                    for i, tiles in ((0, T0), (1, T1 + NB)):
                        zero(i, 0, ZERO[i])
                        zero(i, (NB - 1) * ZERO[i], tiles - (NB - 1) * ZERO[i])
                load_v(NB - 1)
                if layer:
                    sp.wait_ge(sh_used[0], NB)
                    sp.dma_start(w_sh[:, 0:t["w_sh1"].shape[1]], t["w_sh1"]).then_inc(ffn_in[3], 16)
                if layer == 0:
                    for e in range(3):
                        sp.dma_start(w_ffn[:, e, :], t["w_ffn0"][:, e, :]).then_inc(ffn_in[1], 16)

            sp.wait_ge(zeros_set, 1)
            attention(0)

            def sorted_tiles(layer):
                tiles = rows[layer][0:NS * JT[layer] * P].rearrange("(n j p) d -> n p j d", j=JT[layer], p=P)
                nj = JT[layer]

                def load(n, p):
                    if not (static(n) and n < 2):
                        sp.wait_ge(xsT_in_psum[layer], n - 1)
                    sp.dma_start(xs[:, p, 0:nj, :], tiles[n]).then_inc(xs_in[layer][p], 16)

                def store(b, p):
                    sp.wait_ge(ys_ready[layer], b + 1)
                    sp.dma_start(tiles[b], ys[:, p, 0:nj, :]).then_inc(ys_stored[layer][p], 16)

                sp.wait_ge(scattered[layer], 16 * NB * (1 + layer))
                sp.wait_ge(experts_ready[layer], 1)
                load(0, 0)
                load(1, 1)

                def body(n, b, p):
                    if n is not None and not (static(n) and n + 2 >= NS):
                        load(n + 2, p)
                    if b is not None:
                        store(b, 1 - p)

                body(0, None, 0)
                body(1, 0, 1)
                body(2, 1, 0)
                with sp.Fori(1, (NS - 3) // 2) as i:
                    body(i * 2 + 1, i * 2, 1)
                    body(i * 2 + 2, i * 2 + 1, 0)
                body(NS - 2, NS - 3, 1)
                store(NS - 2, 1)
                store(NS - 1, 0)

            sp.wait_ge(lg_ready, NB)
            sp.wait_ge(av_in_psum, NB)
            sp.wait_ge(bias_ready, NB // MG)
            for e in range(3, E0):
                sp.dma_start(w_ffn[:, e, :], t["w_ffn0"][:, e, :]).then_inc(ffn_in[2], 16)
            sp.dma_start(w_att[:, 1], t["w_att1"]).then_inc(watt1_in, 16)
            sorted_tiles(0)
            sp.wait_ge(ys_in_psum[0], NS)
            attention(1)
            sorted_tiles(1)
            for g in range(NB // MG):
                sp.wait_ge(out_ready, g + 1)
                sp.dma_start(out[g * MG:(g + 1) * MG].rearrange("b t c -> t b c"), x_res[:, g * MG:(g + 1) * MG])\
                    .then_inc(stored, 16)
            sp.wait_ge(stored, 16 * (NB // MG))

        @block.gpsimd
        def _(pool):
            nc.gpsimd.memset(zeros[:], 0.0).then_inc(zeros_set, 1)
            nc.gpsimd.memset(mhalf[:], -0.5).then_inc(setup_pool, 1)
            nc.gpsimd.memset(va[:], 1.0).then_inc(setup_pool, 1)
            nc.gpsimd.memset(xnT_all[:, :, :, 0:2], 0.0).then_inc(setup_pool, 1)
            pool.wait_ge(setup_pool, 1)

            def mlp_units(group, quarter, done, which):
                scaled = (group - 1) * (KB - 1) + 4 * quarter
                for i in which:
                    k = 4 * quarter + i
                    coef = c_bc[:, k:k + 1]
                    pool.wait_ge(hid_ready, done + i + 1)
                    apart(pool)
                    if k == 0:
                        if not (static(group) and group == 1):
                            pool.wait_ge(bias_ready, group)
                            apart(pool)
                        nc.gpsimd.tensor_scalar(acc[:], hid[i], coef, bb2, ALU.mult, ALU.add).then_inc(hid_added, 1)
                    else:
                        nc.gpsimd.tensor_scalar(hid[i], hid[i], coef, 0.0, ALU.mult, ALU.add).then_inc(hid_scaled, 1)
                        pool.wait_ge(hid_scaled, scaled + i)
                        pool.wait_ge(hid_added, done + i - KB)
                        apart(pool)
                        nc.gpsimd.tensor_tensor(acc[:], acc[:], hid[i], ALU.add).then_inc(hid_added, 1)
                if quarter == 3 and 3 in which:
                    if static(group):
                        pool.wait_ge(dist_in, 32)
                    pool.wait_ge(hid_added, done + 4 - KB)
                    four = bias_all[:, bass.ds(group * MG, MG), :].rearrange("p b s -> p (b s)")
                    apart(pool)
                    nc.gpsimd.tensor_tensor(four, four, acc[:], ALU.add).then_inc(bias_ready, 1)

            def rstd(layer, n):
                pool.wait_ge(var_ready, at(layer, n) + 1)
                nc.gpsimd.tensor_tensor(ln_rs[:, 0:1], ln_ve[:, 0:1], mhalf[:], ALU.pow).then_inc(rstd_ready, 1)

            def rstd1(layer, b):
                pool.wait_ge(var1_ready, at(layer, b) + 1)
                nc.gpsimd.tensor_tensor(ln_rs[:, 1:2], ln_ve[:, 1:2], mhalf[:], ALU.pow).then_inc(rstd1_ready, 1)

            def keep(layer, b):
                pool.wait_ge(xn1_ready, at(layer, b) + 1)
                apart(pool)
                nc.gpsimd.tensor_copy(xn_all[:, b, :], xn1[:]).then_inc(xn1_kept, 1)

            def first(m, n, b, c, quarter, mlp_on=True):
                if m is not None:
                    rstd(0, m)
                    if mlp_on:
                        mlp_units((m - quarter) // 4 + 1, quarter, m * 4 + KB, (0,))
                if c is not None:
                    rstd1(0, c)
                if m is not None and mlp_on:
                    mlp_units((m - quarter) // 4 + 1, quarter, m * 4 + KB, (1, 2, 3))
                if c is not None:
                    keep(0, c)

            first(0, None, None, None, 0)
            first(1, 0, None, None, 1)
            first(2, 1, 0, None, 2)
            first(3, 2, 1, 0, 3)
            with pool.Fori(1, NB // 4 - 1) as i:
                for r in range(4):
                    first(i * 4 + r, i * 4 + (r - 1), i * 4 + (r - 2), i * 4 + (r - 3), r)
            with pool.Fori(NB - 4, NB) as m:
                first(m, m - 1, m - 2, m - 3, 0, False)
            first(None, NB - 1, NB - 2, NB - 3, 0)
            first(None, None, NB - 1, NB - 2, 0)
            first(None, None, None, NB - 1, 0)

            def scatter(layer):
                pool.wait_ge(rows_zeroed[layer], 16 * NB)
                pool.wait_ge(xn1_kept, NB * (layer + 1))
                for a in range(1 + layer):
                    pool.wait_ge(slots_ready[layer], a + 1)
                    for b in range(NB):
                        nc.gpsimd.indirect_dma_start(
                            rows[layer], bass.IndirectOffsetOnAxis(ap=slot[:, a, b:b + 1], axis=0),
                            xn_all[:, b, :], None).then_inc(scattered[layer], 16)

            def gather(layer, a, b, to, signal):
                nc.gpsimd.indirect_dma_start(
                    to, None, rows[layer], bass.IndirectOffsetOnAxis(ap=slot[:, a, b:b + 1], axis=0))\
                    .then_inc(signal, 16)

            def tiles_stored(layer):
                for p in range(2):
                    pool.wait_ge(ys_stored[layer][p], 16 * ((NS + 1 - p) // 2))

            scatter(0)
            tiles_stored(0)
            for b in range(NB):
                gather(0, 0, b, xn_all[:, b, :], gathered[4])
            pool.wait_ge(gathered[4], 16 * NB)
            pool.wait_ge(sh_added[0], MG)

            def add_ffn(n):
                nc.gpsimd.tensor_tensor(x_res[:, n, :], x_res[:, n, :], xn_all[:, n, :], ALU.add).then_inc(x2_ready, 1)

            def second(m, n, b, c):
                if m is not None:
                    rstd(1, m)
                    if not (static(m) and m == NB - 1):
                        add_ffn(m + 1)
                    pool.wait_ge(xn_ready, at(1, m) + 1)
                    apart(pool)
                    nc.gpsimd.tensor_tensor(x_res[:, m, :], x_res[:, m, :], bvo[:, 1, :], ALU.add).then_inc(bo_added, 1)
                if c is not None:
                    rstd1(1, c)
                    keep(1, c)

            add_ffn(0)
            second(0, None, None, None)
            pool.wait_ge(sh_added[0], NB)
            second(1, 0, None, None)
            second(2, 1, 0, None)
            second(3, 2, 1, 0)
            with pool.Fori(3, NB - 2) as n:
                second(n + 1, n, n - 1, n - 2)
            second(NB - 1, NB - 2, NB - 3, NB - 4)
            second(None, NB - 1, NB - 2, NB - 3)
            second(None, None, NB - 1, NB - 2)
            second(None, None, None, NB - 1)
            scatter(1)
            tiles_stored(1)
            pool.wait_ge(sh_used[1], NB // MG)
            for b in range(NB):
                gather(1, 0, b, xn_all[:, b, :], gathered[b // MG])
                gather(1, 1, b, rows_b[:, b, :], gathered[b // MG])

        @block.scalar
        def _(act):
            A = nc.scalar.activation

            def unit(group, k, done, i, used):
                if not static(used) or used > 0:
                    act.wait_ge(hid0_added if static(done) and done + i < KB + 4 else hid_added, used)
                A(hid[i], dist[:, bass.ds(group * MG, MG), :].rearrange("p b s -> p (b s)"), ACT.Relu,
                  bias=b_bc[:, bass.ds(k, 1)], scale=a_bc[:, bass.ds(k, 1)]).then_inc(hid_ready, 1)

            def attention(layer):
                def keys(m):
                    act.wait_ge(k_in_psum, at(layer, m) + 1)
                    pk = ps_pm[:, 0:KC * P].rearrange("p (k s) -> p k s", k=KC)
                    for h in range(2):
                        if layer == 0:
                            last = A(kz[:, :, h, :], pk, ACT.Copy, scale=par[:, h:h + 1])
                        else:
                            for k in range(KC):
                                last = A(kz[:, k, h, :], pk[:, k, :], ACT.Identity, scale=par[:, h:h + 1],
                                         bias=kbm[:, k, h:h + 1])
                    last.then_inc(kz_ready, 1)

                def body(m, n, b, c, mlp_on=True):
                    mlp_here = layer == 0 and mlp_on and m is not None

                    def units(which):
                        for i in which:
                            used = m * 4 + i - 3
                            unit(m // 4 + 1, (m % 4) * 4 + i, m * 4 + KB, i, used)

                    def weightsT(j):
                        act.wait_ge(pt_in_psum, at(layer, b) * 4 + j + 1)
                        if j == 0 and not (layer == 0 and static(b) and b == 0):
                            act.wait_ge(av_in_psum, at(layer, b))
                        bank = ps_pb if j % 2 == 0 else ps_pa
                        A(pt[:, j].rearrange("p i s -> p (i s)"), bank[:, :], ACT.Copy).then_inc(pt_ready, 1)

                    def probs(j):
                        act.wait_ge(shifted, at(layer, n) * 4 + j + 1)
                        if not (layer == 0 and static(n) and n == 0):
                            act.wait_ge(pt_in_psum, at(layer, n) * 4 - 3 + j)
                        A(pr[:, j], sc[:, j], ACT.Exp).then_inc(probs_ready, 1)

                    if c is not None:
                        act.wait_ge(attnT_in_psum, at(layer, c) + 1)
                        A(attnT[:].rearrange("p k s -> p (k s)"), ps_pa[:, 0:D], ACT.Copy).then_inc(attnT_ready, 1)
                    if b is not None:
                        weightsT(0)
                    if mlp_here:
                        units((0,))
                    if b is not None:
                        weightsT(1)
                    if m is not None:
                        if n is not None:
                            act.wait_ge(scores_in_psum, at(layer, n) * 2 + 2)
                        keys(m)
                    if n is not None:
                        probs(0)
                    if b is not None:
                        weightsT(2)
                    if m is not None:
                        act.wait_ge(xnT_in_psum, at(layer, m) + 1)
                        A(xnT[:].rearrange("p k s -> p (k s)"), ps_pm[:, 0:D], ACT.Copy).then_inc(xnT_ready, 1)
                    if n is not None:
                        probs(1)
                    if mlp_here:
                        units((1,))
                    if b is not None:
                        weightsT(3)
                    if m is not None:
                        act.wait_ge(q_in_psum, at(layer, m) + 1)
                        if layer == 0:
                            A(qT[:].rearrange("p k s -> p (k s)"), ps_pm[:, 0:D], ACT.Copy, scale=0.25)\
                                .then_inc(q_ready, 1)
                        else:
                            for k in range(KC):
                                last = A(qT[:, k, :], ps_pm[:, k * P:(k + 1) * P], ACT.Identity, scale=0.25,
                                         bias=qb4[:, k:k + 1])
                            last.then_inc(q_ready, 1)
                    if mlp_here:
                        units((2, 3))
                    if n is not None and layer:
                        probs(2)
                    if c is not None:
                        act.wait_ge(xn1T_in_psum, at(layer, c) + 1)
                        A(xn1T[:].rearrange("p k s -> p (k s)"), ps_pb[:, 0:D], ACT.Copy).then_inc(xn1T_ready, 1)
                        A(xnT_all[:, :, c, 2:PADW], ps_pb[:, 0:D].rearrange("p (k s) -> p k s", k=KC), ACT.Copy)\
                            .then_inc(xnT_kept, 1)
                    if n is not None and layer == 0:
                        probs(2)
                        act.wait_ge(v_in_psum, at(layer, n) + 1)
                        if b is not None:
                            act.wait_ge(av_in_psum, at(layer, b) + 1)
                        A(va[:, :, 0:HD], ps_pm[:, 0:D].rearrange("p (h d) -> p h d", h=NH), ACT.Copy)\
                            .then_inc(v_ready, 1)
                    if n is not None:
                        probs(3)
                    if c is not None:
                        act.wait_ge(lg_in_psum, at(layer, c) + 1)
                        ne = E1 if layer else E0
                        A(lg[:, c, 0:ne], ps_po[:, 0:ne], ACT.Copy).then_inc(lg_ready, 1)

                if layer:
                    pipeline(act, body)
                else:
                    body(0, None, None, None, False)
                    for k in range(10, KB):
                        unit(0, k, 0, k % 4, k - 3)
                    act.wait_ge(dist_in, 32)
                    for k in range(4):
                        unit(1, k, KB, k, KB + k - 3)
                    body(1, 0, None, None)
                    body(2, 1, 0, None)
                    body(3, 2, 1, 0)
                    with act.Fori(3, NB - MG - 1) as n:
                        body(n + 1, n, n - 1, n - 2)
                    with act.Fori(NB - MG - 1, NB - 1) as n:
                        body(n + 1, n, n - 1, n - 2, False)
                    body(None, NB - 1, NB - 2, NB - 3)
                    body(None, None, NB - 1, NB - 2)
                    body(None, None, None, NB - 1)

            act.dma_start(mlp[:], t["mlp"]).then_inc(mlp_in, 16)
            act.dma_start(dist[:, 0:MG], t["dist"][:, 0:MG]).then_inc(dist0_in, 16)
            act.dma_start(bias_all[:, 0:MG], t["mask"][:, 0:MG]).then_inc(mask0_in, 16)
            act.dma_start(qkb[:], t["qkb"]).then_inc(small_in, 16)
            act.dma_start(bvo[:], t["bvo"]).then_inc(small_in, 16)
            act.dma_start(rbias[:], t["rbias"]).then_inc(small_in, 16)
            act.dma_start(dist[:, MG:], t["dist"][:, MG:]).then_inc(dist_in, 16)
            act.dma_start(bias_all[:, MG:], t["mask"][:, MG:]).then_inc(dist_in, 16)
            act.wait_ge(mlp_in, 16)
            act.wait_ge(dist0_in, 16)
            for k in range(10):
                unit(0, k, 0, k % 4, k - 3)
            act.wait_ge(consts_in, 16)
            act.wait_ge(setup_pool, 3)
            attention(0)

            def shared(layer, groups):
                def body(g, c, q):
                    h = half(layer, g, c)
                    act.wait_ge(sh_gu_in_psum[layer], q + 1)
                    if not static(q) or q >= 2:
                        act.wait_ge(sh_hidden[layer], q - 1)
                    A(sg[:, h, :], ps[h][:, :], ACT.Silu).then_inc(sh_silu[layer], 1)
                shared_steps(layer, groups, body)

            def sorted_tiles(layer):
                def body(n, b, p):
                    def rowsT(n):
                        act.wait_ge(xsT_in_psum[layer], n + 1)
                        w = D * JT[layer]
                        if not (static(n) and n == 0):
                            act.wait_ge(gu_in_psum[layer], n)
                        A(xsT[:, 0:w], ps[4][:, 0:w], ACT.Copy).then_inc(xsT_ready[layer], 1)

                    if b is not None:
                        w = HC0 * P if layer == 0 else 2 * P
                        act.wait_ge(hsT_in_psum[layer], b + 1)
                        if not (static(b) and b == 0):
                            act.wait_ge(ys_in_psum[layer], b)
                        A(hsT[:, 0:w], ps[2][:, 0:w], ACT.Copy).then_inc(hsT_ready[layer], 1)
                    if n is not None:
                        if static(n) and n == 0:
                            rowsT(0)
                        act.wait_ge(gu_in_psum[layer], n + 1)
                        if not (static(n) and n == 0):
                            act.wait_ge(hs_ready[layer], n)
                        if layer == 0:
                            A(sgs[:, 0:H0], ps[0][:, 0:H0], ACT.Silu).then_inc(silu_ready[layer], 1)
                        else:
                            A(sgs[:, 0:2 * H1].rearrange("p (j h) -> p j h", j=2),
                              ps[0][:, :].rearrange("p (j a h) -> p j a h", j=2, a=2)[:, :, 0, :], ACT.Silu)\
                                .then_inc(silu_ready[layer], 1)
                        if not (static(n) and n == NS - 1):
                            rowsT(n + 1)
                    if b is not None:
                        act.wait_ge(ys_in_psum[layer], b + 1)
                        if not (static(b) and b < 2):
                            act.wait_ge(ys_stored[layer][1 - p], (b // 2) * 16)
                        w = D * JT[layer]
                        A(ys[:, 1 - p, 0:JT[layer], :].rearrange("p j d -> p (j d)"), ps[3][:, 0:w], ACT.Copy)\
                            .then_inc(ys_ready[layer], 1)

                body(0, None, 0)
                body(1, 0, 1)
                body(2, 1, 0)
                with act.Fori(1, (NS - 3) // 2) as i:
                    body(i * 2 + 1, i * 2, 1)
                    body(i * 2 + 2, i * 2 + 1, 0)
                body(NS - 2, NS - 3, 1)
                body(NS - 1, NS - 2, 0)
                body(None, NS - 1, 1)

            act.wait_ge(xn1_kept, NB)
            shared(0, SHARED[0][0])
            sorted_tiles(0)
            shared(0, SHARED[0][1])
            attention(1)
            act.wait_ge(centred, 1)
            A(rw[1], rw[0], ACT.Exp).then_inc(exp_ready, 1)
            act.wait_ge(xn1_kept, 2 * NB)
            shared(1, SHARED[1][0])
            sorted_tiles(1)

        @block.tensor
        def _(pe):
            mm, tr = nc.tensor.matmul, nc.tensor.transpose

            def attention(layer):
                wq, wk, wv, wo = (w_att[:, layer, i] for i in range(4))
                r0 = E0 if layer else 0
                ne = E1 if layer else E0

                def since(signal, count):
                    if not static(count) or count > 0:
                        pe.wait_ge(signal, count)

                def body(m, n, b, c):
                    def scores(half, k):
                        if n is None:
                            return
                        if half == 0 and k == 0:
                            pe.wait_ge(q_ready, at(layer, n) + 1)
                            pe.wait_ge(kz_ready, at(layer, n) + 1)
                        if k == 0:
                            since(shifted, at(layer, n) * 4 - 2 + 2 * half)
                        for j in (2 * half, 2 * half + 1):
                            r = slice(32 * j, 32 * j + 32)
                            last = mm(ps_s[j][:, k * 256:(k + 1) * 256], qT[r, k, :],
                                      kz[r, k].rearrange("p h s -> p (h s)"), start=True, stop=True)
                        if k == KC - 1:
                            last.then_inc(scores_in_psum, 1)

                    def weightsT(j):
                        if b is None:
                            return
                        pe.wait_ge(probs_ready, at(layer, b) * 4 + j + 1)
                        if j == 0:
                            since(pt_ready, at(layer, b) * 4 - 1)
                            since(xn1T_ready, at(layer, b) - 1)
                            since(xnT_kept, at(layer, b) - 1)
                        elif j == 1:
                            since(attnT_ready, at(layer, b))
                        else:
                            pe.wait_ge(pt_ready, at(layer, b) * 4 + j - 1)
                        bank = ps_pb if j % 2 == 0 else ps_pa
                        for i in range(4):
                            last = tr(bank[:, i * P:(i + 1) * P], pr[:, j, i, :], ident)
                        last.then_inc(pt_in_psum, 1)

                    def weighted_values(j):
                        if b is None:
                            return
                        pe.wait_ge(pt_ready, at(layer, b) * 4 + j + 1)
                        if j == 0:
                            pe.wait_ge(v_ready, at(layer, b) + 1)
                            since(x1_ready, at(layer, b))
                            since(lg_ready, at(layer, b) - 1)
                        for i in range(4):
                            h = head_of(j, i)
                            last = mm(ps_po[:, h * VW:(h + 1) * VW], pt[:, j, i, :], va[:, h, :], start=True, stop=True)
                        if j == 3:
                            last.then_inc(av_in_psum, 1)

                    def attended():
                        if c is None:
                            return
                        pe.wait_ge(attn_ready, at(layer, c) + 1)
                        since(pt_ready, at(layer, c) * 4 + 4)
                        for k in range(KC):
                            last = tr(ps_pa[:, k * P:(k + 1) * P], attn[:, k * P:(k + 1) * P], ident)
                        last.then_inc(attnT_in_psum, 1)

                    def keys():
                        if m is None:
                            return
                        pe.wait_ge(ctx_k_in, (at(layer, m) + 1) * 16)
                        since(v_ready, at(layer, m) - 1)
                        since(q_ready, at(layer, m))
                        for o in range(KC):
                            for k in range(KC):
                                last = mm(ps_pm[:, o * P:(o + 1) * P], wk[:, k, o * P:(o + 1) * P], ctx_k[:, k, :],
                                          start=(k == 0), stop=(k == KC - 1))
                        last.then_inc(k_in_psum, 1)

                    def output():
                        if c is None:
                            return
                        pe.wait_ge(attnT_ready, at(layer, c) + 1)
                        since(lg_ready, at(layer, c))
                        for k in range(KC):
                            last = mm(ps_po[:, 0:D], attnT[:, k, :], wo[:, k, :], start=(k == 0), stop=(k == KC - 1))
                        last.then_inc(wo_in_psum, 1)

                    def rows_in():
                        if m is None:
                            return
                        pe.wait_ge(xn_ready, at(layer, m) + 1)
                        pe.wait_ge(kz_ready, at(layer, m) + 1)
                        for k in range(KC):
                            last = tr(ps_pm[:, k * P:(k + 1) * P], xn[:, k * P:(k + 1) * P], ident)
                        last.then_inc(xnT_in_psum, 1)

                    def queries():
                        if m is None:
                            return
                        pe.wait_ge(xnT_ready, at(layer, m) + 1)
                        for o in range(KC):
                            for k in range(KC):
                                last = mm(ps_pm[:, o * P:(o + 1) * P], wq[:, k, o * P:(o + 1) * P], xnT[:, k, :],
                                          start=(k == 0), stop=(k == KC - 1))
                        last.then_inc(q_in_psum, 1)

                    def rows_out():
                        if c is None:
                            return
                        pe.wait_ge(xn1_ready, at(layer, c) + 1)
                        if b is None:
                            pe.wait_ge(xn1T_ready, at(layer, c))
                            pe.wait_ge(xnT_kept, at(layer, c))
                        for k in range(KC):
                            last = tr(ps_pb[:, k * P:(k + 1) * P], xn1[:, k * P:(k + 1) * P], ident)
                        last.then_inc(xn1T_in_psum, 1)

                    def values():
                        if n is None:
                            return
                        pe.wait_ge(ctx_v_in, (at(layer, n) + 1) * 16)
                        if m is not None:
                            pe.wait_ge(q_ready, at(layer, m) + 1)
                        else:
                            pe.wait_ge(v_ready, at(layer, n))
                        for k in range(KC):
                            last = mm(ps_pm[:, 0:D], ctx_v[:, k, :], wv[:, k, :], start=(k == 0), stop=(k == KC - 1))
                        last.then_inc(v_in_psum, 1)

                    def logits():
                        if c is None:
                            return
                        pe.wait_ge(xn1T_ready, at(layer, c) + 1)
                        if b is not None:
                            pe.wait_ge(attn_ready, at(layer, b) + 1)
                        for k in range(KC):
                            last = mm(ps_po[:, 0:ne], xn1T[:, k, :], rt[:, k, r0:r0 + ne], start=(k == 0), stop=(k == KC - 1))
                        last.then_inc(lg_in_psum, 1)

                    if layer == 0:
                        attended()
                        weightsT(0)
                        scores(0, 0)
                        scores(0, 1)
                        keys()
                        weightsT(1)
                        scores(1, 0)
                        output()
                        scores(1, 1)
                        weightsT(2)
                        weightsT(3)
                        weighted_values(0)
                        rows_in()
                        weighted_values(1)
                        queries()
                        weighted_values(2)
                        weighted_values(3)
                        rows_out()
                        values()
                        logits()
                    else:
                        attended()
                        weightsT(0)
                        keys()
                        weightsT(1)
                        scores(0, 0)
                        scores(0, 1)
                        scores(1, 0)
                        scores(1, 1)
                        output()
                        weightsT(2)
                        weightsT(3)
                        weighted_values(0)
                        rows_in()
                        weighted_values(1)
                        queries()
                        weighted_values(2)
                        weighted_values(3)
                        rows_out()
                        values()
                        logits()
                pipeline(pe, body)

            pe.wait_ge(consts_in, 16)
            pe.wait_ge(watt0_in, 16)
            pe.wait_ge(small_in, 64)
            attention(0)

            def ranks(layer):
                w = NB * (E1 if layer else E0)
                pe.wait_ge(picks_ready[layer], 1)
                mm(ps_pm[:, 0:w], tri, picks[:, 0:w], start=True, stop=True)
                mm(ps_po[:, 0:w], ones, picks[:, 0:w], start=True, stop=True).then_inc(ranks_in_psum[layer], 1)

            def shared(layer, groups):
                wd = 2 * KC * H0 if layer == 0 else (CONV + 1) * KC * H1

                def down(g, c, q):
                    h = half(layer, g, c)
                    pe.wait_ge(sh_hidden[layer], q + 1)
                    if c == 0:
                        if g:
                            pe.wait_ge(sh_added[layer], g * MG)
                        else:
                            pe.wait_ge(slots_ready[layer], 1 + layer)
                    last_c = c == HC0 - 1 or layer == 1
                    for i in range(MG):
                        last = mm(ps[4 + i][:, 0:D], hT[:, h, i * P:(i + 1) * P], w_sh[:, wd + c * D:wd + (c + 1) * D],
                                  start=(c == 0), stop=last_c)
                    last.then_inc(sh_used[layer], 1)

                def body(g, c, q):
                    h = half(layer, g, c)
                    if not static(q) or q >= 2:
                        pe.wait_ge(sh_hidden[layer], q - 1)
                    batches = bass.ds(g * MG, MG)
                    gate, up = ps[h][:, :].rearrange("p (b s) -> p b s", b=MG), \
                        ps[2 + h][:, :].rearrange("p (b s) -> p b s", b=MG)
                    if layer == 0:
                        for o, to in ((0, gate), (H0, up)):
                            for k in range(KC):
                                at_w = k * 2 * H0 + o + c * P
                                last = mm(to, w_sh[:, at_w:at_w + P], xnT_all[:, k, batches, 2:PADW],
                                          start=(k == 0), stop=(k == KC - 1))
                    else:
                        for k in range(KC):
                            for o in range(CONV):
                                at_w = (k * CONV + o) * H1
                                mm(gate, w_sh[:, at_w:at_w + H1], xnT_all[:, k, batches, o:o + P],
                                   start=(k == 0 and o == 0), stop=(k == KC - 1 and o == CONV - 1))
                        for k in range(KC):
                            at_w = (KC * CONV + k) * H1
                            last = mm(up, w_sh[:, at_w:at_w + H1], xnT_all[:, k, batches, 2:PADW],
                                      start=(k == 0), stop=(k == KC - 1))
                    last.then_inc(sh_gu_in_psum[layer], 1)
                    if q == 1:
                        ranks(layer)
                    if c > 0:
                        down(g, c - 1, q - 1)
                    elif g != groups[0]:
                        down(g - 1, chunks - 1, q - 1)

                chunks = HC0 if layer == 0 else 1
                shared_steps(layer, groups, body)
                down(groups[-1], chunks - 1, (groups[-1] + 1) * chunks - 1)
                pe.wait_ge(sh_added[layer], (groups[-1] + 1) * MG)

            def sorted_tiles(layer):
                nj = JT[layer]

                def rowsT(n, p):
                    pe.wait_ge(xs_in[layer][p], (n // 2 + 1) * 16)
                    if not (static(n) and n == 0):
                        pe.wait_ge(xsT_ready[layer], n)
                    for j in range(nj):
                        for k in range(KC):
                            last = tr(ps[4][:, (j * KC + k) * P:(j * KC + k + 1) * P], xs[:, p, j, k * P:(k + 1) * P],
                                      ident)
                    last.then_inc(xsT_in_psum[layer], 1)

                base = R1 if layer else E0

                def experts_of(n):
                    code = pe.value_load(step_experts[0:1, bass.ds(n, 1)], min_val=0, max_val=base ** (2 * nj) - 1)
                    return [(code // base ** i) % base for i in range(nj)], [(code // base ** i) % base for i in range(nj, 2 * nj)]

                def body(n, b, p):
                    if n is not None:
                        experts_n, experts_b = experts_of(n)
                    else:
                        experts_b, _ = experts_of(b)
                    if b is not None:
                        pe.wait_ge(hs_ready[layer], b + 1)
                        if not (static(b) and b == 0):
                            pe.wait_ge(hsT_ready[layer], b)
                        for k in range(HC0 if layer == 0 else 2):
                            last = tr(ps[2][:, k * P:(k + 1) * P], hs[:, k * P:(k + 1) * P], ident)
                        last.then_inc(hsT_in_psum[layer], 1)
                    if n is not None:
                        if static(n) and n == 0:
                            rowsT(0, 0)
                        pe.wait_ge(xsT_ready[layer], n + 1)
                        for j in range(nj):
                            e = experts_n[j]
                            if layer == 0:
                                for o in range(2):
                                    for k in range(KC):
                                        at_w = k * 2 * H0 + o * H0
                                        last = mm(ps[o][:, :], xsT[:, k * P:(k + 1) * P], w_ffn[:, e, at_w:at_w + H0],
                                                  start=(k == 0), stop=(k == KC - 1))
                            else:
                                for k in range(KC):
                                    last = mm(ps[0][:, j * 256:(j + 1) * 256],
                                              xsT[:, (j * KC + k) * P:(j * KC + k + 1) * P],
                                              w1_ffn[:, e, k * 256:(k + 1) * 256], start=(k == 0), stop=(k == KC - 1))
                        last.then_inc(gu_in_psum[layer], 1)
                        if not (static(n) and n == NS - 1):
                            rowsT(n + 1, 1 - p)
                    if b is not None:
                        pe.wait_ge(hsT_ready[layer], b + 1)
                        if not (static(b) and b == 0):
                            pe.wait_ge(ys_ready[layer], b)
                        for j in range(nj):
                            e = experts_b[j]
                            if layer == 0:
                                for k in range(HC0):
                                    at_w = 2 * KC * H0 + k * D
                                    last = mm(ps[3][:, 0:D], hsT[:, k * P:(k + 1) * P], w_ffn[:, e, at_w:at_w + D],
                                              start=(k == 0), stop=(k == HC0 - 1))
                            else:
                                last = mm(ps[3][:, j * D:(j + 1) * D], hsT[:, j * P:(j + 1) * P],
                                          w1_ffn[:, e, 512:768], start=True, stop=True)
                        last.then_inc(ys_in_psum[layer], 1)

                body(0, None, 0)
                body(1, 0, 1)
                body(2, 1, 0)
                with pe.Fori(1, (NS - 3) // 2) as i:
                    body(i * 2 + 1, i * 2, 1)
                    body(i * 2 + 2, i * 2 + 1, 0)
                body(NS - 2, NS - 3, 1)
                body(NS - 1, NS - 2, 0)
                body(None, NS - 1, 1)

            def ffn(layer):
                pe.wait_ge(lg_ready, NB * (layer + 1))
                pe.wait_ge(x1_ready, NB * (layer + 1))
                pe.wait_ge(ffn_in[0] if layer == 0 else ffn_in[3], 16 if layer == 0 else 32)
                shared(layer, SHARED[layer][0])
                pe.wait_ge(experts_ready[layer], 1)
                if layer == 0:
                    pe.wait_ge(ffn_in[1], 48)
                    pe.wait_ge(ffn_in[2], 80)
                sorted_tiles(layer)

            ffn(0)
            pe.wait_ge(ys_ready[0], NS)
            shared(0, SHARED[0][1])
            pe.wait_ge(watt1_in, 16)
            attention(1)
            ffn(1)

        @block.vector
        def _(dve):
            V = nc.vector

            def attention(layer):
                def stats(n):
                    if layer:
                        dve.wait_ge(x2_ready, n + 1)
                        apart(dve)
                    apart(dve)
                    V.bn_stats(ln_st[:, 0, :], x_res[:, n, :]).then_inc(stats_done, 1)
                    dve.wait_ge(stats_done, at(layer, n) + 1)
                    apart(dve)
                    V.bn_aggr(ln_mv[:, 0, :], ln_st[:, 0, :]).then_inc(aggr_done, 1)
                    dve.wait_ge(aggr_done, at(layer, n) + 1)
                    V.tensor_scalar(ln_ve[:, 0:1], ln_mv[:, 0, 1:2], EPS, None, ALU.add).then_inc(var_ready, 1)

                def normalise(n):
                    dve.wait_ge(rstd_ready, at(layer, n) + 1)
                    if not (layer == 0 and static(n) and n == 0):
                        dve.wait_ge(xnT_in_psum, at(layer, n))
                    V.tensor_scalar(xn[:], x_res[:, n, :], ln_mv[:, 0, 0:1], ln_rs[:, 0:1], ALU.subtract, ALU.mult)\
                        .then_inc(xn_ready, 1)

                def shift(n, half, between=None, before=None):
                    first = layer == 0 and static(n) and n == 0
                    banks = (2 * half, 2 * half + 1)
                    s4 = {j: ps_s[j][:, :].rearrange("p (i s) -> p i s", i=4) for j in banks}
                    dve.wait_ge(scores_in_psum, at(layer, n) * 2 + half + 1)
                    if layer == 0:
                        for j in banks:
                            if not first:
                                dve.wait_ge(probs_ready, at(layer, n) * 4 - 3 + j)
                            V.tensor_tensor(sc[:, j], s4[j], bias_all[:, n, :].unsqueeze(1).broadcast_to([P, 4, P]),
                                            ALU.add).then_inc(biased, 1)
                            s4[j] = sc[:, j]
                    if between and layer == 0:
                        between()
                    for j in banks:
                        if layer == 0:
                            dve.wait_ge(biased, at(layer, n) * 4 + j + 1)
                        V.tensor_reduce(mx[:, j, :], s4[j], AX.X, ALU.max).then_inc(max_ready, 1)
                    if between and layer:
                        between()
                    if before:
                        before()
                    for j in banks:
                        dve.wait_ge(max_ready, at(layer, n) * 4 + j + 1)
                        if layer and not first:
                            dve.wait_ge(probs_ready, at(layer, n) * 4 - 3 + j)
                        V.tensor_tensor(sc[:, j], s4[j], mx[:, j, :].unsqueeze(2).broadcast_to([P, 4, P]), ALU.subtract)\
                            .then_inc(shifted, 1)

                def body(m, n, b, c):
                    def residual():
                        dve.wait_ge(wo_in_psum, at(layer, c) + 1)
                        if layer:
                            dve.wait_ge(bo_added, c + 1)
                        V.tensor_tensor(x_res[:, c, :], ps_po[:, 0:D], x_res[:, c, :], ALU.add).then_inc(x1_ready, 1)

                    if m is not None:
                        stats(m)
                    if n is not None:
                        if layer == 0:
                            dve.wait_ge(bias_ready, n // MG + 1)
                        shift(n, 0, before=residual if c is not None and layer == 0 else None)
                    if m is not None:
                        normalise(m)
                    if c is not None and (layer or n is None):
                        residual()
                    if c is not None:
                        dve.wait_ge(x1_ready, at(layer, c) + 1)
                        apart(dve)
                        V.bn_stats(ln_st[:, 1, :], x_res[:, c, :]).then_inc(stats1_done, 1)
                        dve.wait_ge(stats1_done, at(layer, c) + 1)
                        apart(dve)
                        V.bn_aggr(ln_mv[:, 1, :], ln_st[:, 1, :]).then_inc(aggr1_done, 1)
                        dve.wait_ge(aggr1_done, at(layer, c) + 1)
                        V.tensor_scalar(ln_ve[:, 1:2], ln_mv[:, 1, 1:2], EPS, None, ALU.add).then_inc(var1_ready, 1)

                    def normalise1():
                        dve.wait_ge(rstd1_ready, at(layer, c) + 1)
                        if not (layer == 0 and static(c) and c == 0):
                            dve.wait_ge(xn1T_in_psum, at(layer, c))
                            dve.wait_ge(xn1_kept, at(layer, c))
                        V.tensor_scalar(xn1[:], x_res[:, c, :], ln_mv[:, 1, 0:1], ln_rs[:, 1:2],
                                        ALU.subtract, ALU.mult).then_inc(xn1_ready, 1)


                    def weighted_rows():
                        dve.wait_ge(av_in_psum, at(layer, b) + 1)
                        po = ps_po[:, 0:NH * VW].rearrange("p (h d) -> p h d", h=NH)
                        V.reciprocal(rsum[:].unsqueeze(2), po[:, :, HD:VW]).then_inc(rsum_ready, 1)
                        dve.wait_ge(rsum_ready, at(layer, b) + 1)
                        if not (layer == 0 and static(b) and b == 0):
                            dve.wait_ge(attnT_in_psum, at(layer, b))
                        V.tensor_tensor(attn[:].rearrange("p (h d) -> p h d", h=NH), po[:, :, 0:HD],
                                        rsum[:].unsqueeze(2).broadcast_to([P, NH, HD]), ALU.mult).then_inc(attn_ready, 1)

                    within = layer == 0 and n is not None
                    if n is not None:
                        shift(n, 1, normalise1 if c is not None else None, weighted_rows if b is not None and within else None)
                    elif c is not None:
                        normalise1()
                    if b is not None and not within:
                        weighted_rows()
                    if n is not None and layer:
                        dve.wait_ge(v_in_psum, at(layer, n) + 1)
                        V.tensor_tensor(va[:, :, 0:HD], ps_pm[:, 0:D].rearrange("p (h d) -> p h d", h=NH),
                                        bvo[:, 0, :].rearrange("p (h d) -> p h d", h=NH), ALU.add).then_inc(v_ready, 1)

                pipeline_start(layer, body)

            def pipeline_start(layer, body):
                if layer:
                    pipeline(dve, body)
                    return
                body(0, None, None, None)
                for k in range(KB):
                    dve.wait_ge(hid_ready, k + 1)
                    if k == 0:
                        V.tensor_scalar(acc0[:], hid[0], c_bc[:, 0:1], bb2, ALU.mult, ALU.add).then_inc(hid0_added, 1)
                    else:
                        dve.wait_ge(hid0_added, k)
                        V.scalar_tensor_tensor(acc0[:], hid[k % 4], c_bc[:, k:k + 1], acc0[:], ALU.mult, ALU.add)\
                            .then_inc(hid0_added, 1)
                dve.wait_ge(hid0_added, KB)
                dve.wait_ge(mask0_in, 16)
                four = bias_all[:, 0:MG, :].rearrange("p b s -> p (b s)")
                V.tensor_tensor(four, four, acc0[:], ALU.add).then_inc(bias_ready, 1)
                dve.wait_ge(x_in, 16)
                dve.wait_ge(small_in, 64)
                dve.wait_ge(consts_in, 16)
                V.tensor_scalar(qb4[:], qkb[:, 0, :], 0.25, None, ALU.mult).then_inc(setup_dve, 1)
                for k in range(KC):
                    V.tensor_scalar(kbm[:, k, :], par, qkb[:, 1, k:k + 1], None, ALU.mult).then_inc(setup_dve, 1)
                body(1, 0, None, None)
                body(2, 1, 0, None)
                body(3, 2, 1, 0)
                with dve.Fori(3, NB - 1) as n:
                    body(n + 1, n, n - 1, n - 2)
                body(None, NB - 1, NB - 2, NB - 3)
                body(None, None, NB - 1, NB - 2)
                body(None, None, None, NB - 1)

            dve.wait_ge(x0_in, 16)
            dve.wait_ge(mlp_in, 16)
            attention(0)

            chain = [0]

            def then(instruction):
                chain[0] += 1
                instruction.then_inc(route_step, 1)
                dve.wait_ge(route_step, chain[0])

            def routing(layer):
                ne = E1 if layer else E0
                w = NB * ne
                be = lambda v: v[:, 0:w].rearrange("p (b e) -> p b e", b=NB)
                eb = lambda v: v[:, 0:w].rearrange("p (e b) -> p e b", e=ne)
                over_e = lambda v: v.unsqueeze(2).broadcast_to([P, NB, ne])
                over_b = lambda v: v.unsqueeze(1).broadcast_to([P, NB, ne])
                prio = cst[:, C_PRI:C_PRI + ne]
                dve.wait_ge(lg_ready, NB * (layer + 1))
                dve.wait_ge(xn1_kept, NB * (layer + 1))

                def pick(values, to, best):
                    then(V.tensor_reduce(best, values, AX.X, ALU.max))
                    then(V.tensor_tensor(be(rw[7]), values, over_e(best), ALU.is_equal))
                    then(V.tensor_tensor(be(rw[7]), be(rw[7]), over_b(prio), ALU.mult))
                    then(V.tensor_reduce(small[:, 7, :], be(rw[7]), AX.X, ALU.max))
                    then(V.tensor_tensor(to, be(rw[7]), over_e(small[:, 7, :]), ALU.is_equal))

                if layer == 0:
                    pick(lg[:, :, 0:ne], be(rw[3]), small[:, 0, :])
                    then(V.tensor_copy(picks[:, 0:w], rw[3][:, 0:w]))
                    chosen = [rw[3]]
                else:
                    then(V.tensor_tensor(be(rw[0]), lg[:], over_b(rbias[:]), ALU.add))
                    then(V.tensor_reduce(small[:, 0, :], be(rw[0]), AX.X, ALU.max))
                    V.tensor_tensor(be(rw[0]), be(rw[0]), over_e(small[:, 0, :]), ALU.subtract).then_inc(centred, 1)
                    dve.wait_ge(exp_ready, 1)
                    then(V.tensor_reduce(small[:, 1, :], be(rw[1]), AX.X, ALU.add))
                    then(V.reciprocal(small[:, 2, :], small[:, 1, :]))
                    then(V.tensor_tensor(be(rw[2]), be(rw[1]), over_e(small[:, 2, :]), ALU.mult))
                    pick(be(rw[2]), be(rw[3]), small[:, 3, :])
                    then(V.scalar_tensor_tensor(rw[4], rw[3], -2.0, rw[2], ALU.mult, ALU.add))
                    pick(be(rw[4]), be(rw[5]), small[:, 4, :])
                    then(V.tensor_tensor(picks[:, 0:w], rw[3], rw[5], ALU.add))
                    then(V.tensor_tensor(small[:, 5, :], small[:, 3, :], small[:, 4, :], ALU.add))
                    then(V.tensor_scalar(small[:, 5, :], small[:, 5, :], 1e-6, None, ALU.add))
                    then(V.reciprocal(small[:, 6, :], small[:, 5, :]))
                    then(V.tensor_tensor(wgt[:, 0, :], small[:, 3, :], small[:, 6, :], ALU.mult))
                    then(V.tensor_tensor(wgt[:, 1, :], small[:, 4, :], small[:, 6, :], ALU.mult))
                    chosen = [rw[3], rw[5]]
                then(V.tensor_copy(small[:, 7, :], small[:, 0, :]))
                V.tensor_copy(small[:, 6, :], small[:, 0, :]).then_inc(picks_ready[layer], 1)
                dve.wait_ge(ranks_in_psum[layer], 1)
                then(V.tensor_copy(eb(rw[8]), be(ps_po).rearrange("p b e -> p e b")))
                then(V.tensor_tensor_scan(rw[9][:, 0:w], seg[:, 0:w], rw[8][:, 0:w], 0.0, ALU.mult, ALU.add))
                total = eb(rw[9])[:, :, NB - 1]
                need, upto = small[:, 1, 0:ne], small[:, 2, 0:ne]
                then(V.tensor_scalar(need_i[:, 0:ne], total, float(P - 1), None, ALU.add))
                then(V.tensor_scalar(need_i[:, 0:ne], need_i[:, 0:ne], P.bit_length() - 1, None, ALU.arith_shift_right))
                then(V.tensor_copy(need, need_i[:, 0:ne]))
                then(V.tensor_tensor_scan(upto, ones[:, 0:ne], need, 0.0, ALU.mult, ALU.add))
                then(V.tensor_tensor(small[:, 3, 0:ne], upto, need, ALU.subtract))
                if layer:
                    then(V.memset(small[:, 3, R1:E1], float(T1)))
                then(V.tensor_scalar(small[:, 3, 0:ne], small[:, 3, 0:ne], float(P), None, ALU.mult))
                then(V.tensor_tensor(rw[9][:, 0:w], rw[9][:, 0:w], rw[8][:, 0:w], ALU.subtract))
                then(V.tensor_tensor(be(rw[10]), be(ps_pm), eb(rw[9]).rearrange("p e b -> p b e"), ALU.add))
                then(V.tensor_tensor(be(rw[10]), be(rw[10]), over_b(small[:, 3, 0:ne]), ALU.add))
                for a, one in enumerate(chosen):
                    then(V.tensor_tensor(be(rw[11]), be(rw[10]), be(one), ALU.mult))
                    then(V.tensor_reduce(small[:, 4 + a, :], be(rw[11]), AX.X, ALU.add))
                    V.tensor_copy(slot[:, a, :], small[:, 4 + a, :]).then_inc(slots_ready[layer], 1)
                nt, nr = (T1, R1) if layer else (T0, E0)
                big = work[:, 0:nt * nr].rearrange("p (t e) -> p t e", t=nt)
                then(V.tensor_tensor(big, upto[:, 0:nr].unsqueeze(1).broadcast_to([P, nt, nr]),
                                     cst[:, C_TIL:C_TIL + nt].unsqueeze(2).broadcast_to([P, nt, nr]), ALU.is_le))
                then(V.tensor_reduce(te_f[:, 0:nt], big, AX.X, ALU.add))
                then(V.tensor_scalar(te_f[:, 0:nt], te_f[:, 0:nt], float(nr - 1), None, ALU.min))
                digits = te_f[:, 0:NS]
                if layer:
                    pairs = te_f[:].rearrange("p (n j) -> p n j", j=2)
                    digits = small[:].rearrange("p a b -> p (a b)")[:, 0:NS]
                    then(V.scalar_tensor_tensor(digits, pairs[:, :, 1], float(nr), pairs[:, :, 0], ALU.mult, ALU.add))
                then(V.scalar_tensor_tensor(rw[11][:, 1:NS], digits[:, 0:NS - 1], float(nr ** JT[layer]),
                                            digits[:, 1:NS], ALU.mult, ALU.add))
                then(V.tensor_copy(rw[11][:, 0:1], digits[:, 0:1]))
                V.tensor_copy(step_experts[:], rw[11][:, 0:NS]).then_inc(experts_ready[layer], 1)

            def shared(layer, groups):
                def add(g):
                    dve.wait_ge(sh_used[layer], g * HC0 + HC0 if layer == 0 else g + 1)
                    for i in range(MG):
                        V.tensor_tensor(x_res[:, g * MG + i, :], ps[4 + i][:, 0:D], x_res[:, g * MG + i, :], ALU.add)\
                            .then_inc(sh_added[layer], 1)

                def body(g, c, q):
                    h = half(layer, g, c)
                    dve.wait_ge(sh_silu[layer], q + 1)
                    if not static(q) or q >= 2:
                        dve.wait_ge(sh_used[layer], q - 1)
                    V.tensor_tensor(hT[:, h, :], ps[2 + h][:, :], sg[:, h, :], ALU.mult).then_inc(sh_hidden[layer], 1)
                    if c == 0 and g != groups[0]:
                        add(g - 1)

                shared_steps(layer, groups, body)
                add(groups[-1])

            def sorted_tiles(layer):
                def body(n):
                    dve.wait_ge(silu_ready[layer], n + 1)
                    if not (static(n) and n == 0):
                        dve.wait_ge(hsT_in_psum[layer], n)
                    if layer == 0:
                        V.tensor_tensor(hs[:, 0:H0], ps[1][:, :], sgs[:, 0:H0], ALU.mult).then_inc(hs_ready[layer], 1)
                    else:
                        V.tensor_tensor(hs[:, 0:2 * H1].rearrange("p (j h) -> p j h", j=2),
                                        ps[0][:, :].rearrange("p (j a h) -> p j a h", j=2, a=2)[:, :, 1, :],
                                        sgs[:, 0:2 * H1].rearrange("p (j h) -> p j h", j=2), ALU.mult)\
                            .then_inc(hs_ready[layer], 1)
                body(0)
                with dve.Fori(1, NS) as n:
                    body(n)

            routing(0)
            shared(0, SHARED[0][0])
            sorted_tiles(0)
            for p in range(2):
                dve.wait_ge(ys_stored[0][p], 16 * ((NS + 1 - p) // 2))
            shared(0, SHARED[0][1])
            attention(1)
            routing(1)
            shared(1, SHARED[1][0])
            sorted_tiles(1)
            for g in range(NB // MG):
                dve.wait_ge(gathered[g], 2 * MG * 16)
                for b in range(g * MG, (g + 1) * MG):
                    V.scalar_tensor_tensor(x_res[:, b, :], xn_all[:, b, :], wgt[:, 0, b:b + 1], x_res[:, b, :],
                                           ALU.mult, ALU.add).then_inc(weighted, 1)
                for b in range(g * MG, (g + 1) * MG):
                    dve.wait_ge(weighted, b + 1)
                    last = V.scalar_tensor_tensor(x_res[:, b, :], rows_b[:, b, :], wgt[:, 1, b:b + 1], x_res[:, b, :],
                                                  ALU.mult, ALU.add)
                last.then_inc(out_ready, 1)


def static(i):
    return isinstance(i, int)


def kernel(**inputs):
    import numpy as _np
    import concourse.bacc as _bacc
    from concourse import mybir as _mybir
    from concourse.bass_utils import run_bass_kernel_spmd as _run

    a = {k: _np.asarray(v) for k, v in inputs.items()}

    def chunks(w):
        return w.reshape(w.shape[0] // P, P, -1).transpose(1, 0, 2)

    cst = _np.zeros((P, C_END), _np.float32)
    i = _np.arange(P)
    cst[:, C_ID:C_ID + P] = i[:, None] == i[None, :]
    cst[:, C_TRI:C_TRI + P] = i[:, None] < i[None, :]
    cst[:, C_ONE:C_ONE + P] = 1
    cst[:, C_PAR] = i % 32 < HD
    cst[:, C_PAR + 1] = i % 32 >= HD
    cst[:, C_PRI:C_PRI + E1] = E1 - _np.arange(E1)
    cst[:, C_TIL:C_SEG] = _np.arange(C_SEG - C_TIL)
    cst[:, C_SEG:C_END] = _np.arange(NB * E1) % NB > 0
    bc = lambda v: _np.ascontiguousarray(_np.broadcast_to(v.reshape(1, -1), (P, v.size)))
    host = {
        "consts": cst,
        "x": a["x"].transpose(1, 0, 2),
        "ctxT": chunks(a["ctx_1024"].reshape(NB * P, D).T),
        "dist": a["fside_BxSxS2_0"].transpose(1, 0, 2),
        "mask": a["mask_Bx1xSxS2_ff0"][:, 0].transpose(1, 0, 2),
        "w_att0": _np.stack([chunks(a["L0_xattn_Wq"].reshape(D, D)), chunks(a["L0_xattn_Wk"].reshape(D, D)),
                             chunks(a["L0_xattn_Wv"].reshape(D, D)), chunks(a["L0_xattn_Wo"].reshape(D, D))], 1),
        "w_att1": _np.stack([chunks(a["L1_xattn_W" + x].T) for x in "qkvo"], 1),
        "rt": chunks(_np.concatenate([a["L0_ffn_router"].T, a["L1_ffn_router_w"]], 1)),
        "mlp": bc(_np.concatenate([a["L0_xattn_Wb1"][0], a["L0_xattn_bb1"], a["L0_xattn_Wb2"][:, 0],
                                   a["L0_xattn_bb2"]])),
        "qkb": _np.stack([a["L1_xattn_bq"].reshape(KC, P).T, a["L1_xattn_bk"].reshape(KC, P).T], 1),
        "bvo": bc(_np.concatenate([a["L1_xattn_bv"], a["L1_xattn_bo"]])).reshape(P, 2, D),
        "w_ffn0": _np.concatenate([
            _np.concatenate([a["L0_ffn_gate"], a["L0_ffn_up"]], 1).transpose(2, 0, 1)
            .reshape(KC, P, E0, 2 * H0).transpose(1, 2, 0, 3).reshape(P, E0, -1),
            a["L0_ffn_down"].transpose(2, 0, 1).reshape(HC0, P, E0, D).transpose(1, 2, 0, 3).reshape(P, E0, -1)], 2),
        "w_sh0": _np.concatenate([
            chunks(_np.concatenate([a["L0_ffn_w_gate_s"], a["L0_ffn_w_up_s"]], 0).T).reshape(P, -1),
            chunks(a["L0_ffn_w_down_s"].T).reshape(P, -1)], 1),
        "w_ffn1": _np.concatenate([
            _np.concatenate([a["L1_ffn_expert_gate_w"], a["L1_ffn_expert_up_w"]], 2).transpose(1, 0, 2)
            .reshape(KC, P, R1, 2 * H1).transpose(1, 2, 0, 3).reshape(P, R1, -1),
            a["L1_ffn_expert_down_w"].transpose(1, 0, 2)], 2),
        "w_sh1": _np.concatenate([
            a["L1_ffn_conv_w"].transpose(1, 2, 0).reshape(KC, P, CONV * H1).transpose(1, 0, 2).reshape(P, -1),
            chunks(a["L1_ffn_shared_up_w"]).reshape(P, -1), a["L1_ffn_shared_down_w"]], 1),
        "rbias": bc(a["L1_ffn_router_bias"]),
    }
    nc = _bacc.Bacc("TRN2", target_bir_lowering=False, num_devices=1)
    arrays, aps = {}, {}
    for name, v in host.items():
        v = _np.ascontiguousarray(v)
        arrays[f"in_{name}"] = v
        aps[name] = nc.dram_tensor(f"in_{name}", v.shape, _mybir.dt.from_np(v.dtype), kind="ExternalInput").ap()
    out = nc.dram_tensor("out_0", (NB, P, D), _mybir.dt.float32, kind="ExternalOutput").ap()
    rows = [nc.dram_tensor("rows0", (T0 * P, D), _mybir.dt.float32).ap(),
            nc.dram_tensor("rows1", ((T1 + NB) * P, D), _mybir.dt.float32).ap()]
    build_program(nc, aps, out, rows)
    r = _run(nc, [arrays], core_ids=[0])
    return r.results[0]["out_0"]
```

```python
from contextlib import ExitStack

import numpy as np
import concourse.bass as bass
from concourse import mybir

F32 = mybir.dt.float32
I32 = mybir.dt.int32
U32 = mybir.dt.uint32
ALU = mybir.AluOpType
ACT = mybir.ActivationFunctionType
AX = mybir.AxisListType

P = 128
NB = 16
D = 256
KC = D // P
NH, HD = 16, 16
NBANK = 4
VW = HD + 1
KB = 16
MG = 4
PADW = P + 2
EPS = 1e-5

E0, H0 = 8, 512
HC0 = H0 // P
T0 = (NB * P + E0 * (P - 1)) // P
W0 = KC * 2 * H0 + HC0 * D

E1, H1 = 16, 128
R1 = E1 - 1
T1 = (2 * NB * P + R1 * (P - 1)) // P
W1 = KC * 2 * H1 + D
CONV = 3

JT = (1, 2)
NS = T0
assert NS * JT[0] == T0 and NS * JT[1] == T1 and NS % 2 == 1

C_ID, C_TRI, C_ONE, C_PAR, C_PRI, C_TIL = 0, 128, 256, 384, 386, 402
C_SEG = C_TIL + 48
C_OUT = C_SEG + NB * E1
C_OWN = C_OUT + NB
C_END = C_OWN + T1

RESULTS = T1 * P
SECOND = NB * P


def head_of(bank, i):
    return (i // 2) * 8 + 2 * bank + i % 2


def build_program(nc, t, out, rows):
    with ExitStack() as ctx:
        def sb(name, shape, dt=F32):
            return ctx.enter_context(nc.sbuf_tensor(name, shape, dt))

        def sem(name):
            return ctx.enter_context(nc.semaphore(name))

        ps = [ctx.enter_context(nc.psum_tensor(f"bank{i}", [P, 512], F32)) for i in range(8)]
        ps_s, ps_pa, ps_pb, ps_pm, ps_po = ps[0:4], ps[4], ps[5], ps[6], ps[7]

        cst = sb("cst", [P, C_END])
        ident, tri, ones = cst[:, C_ID:C_ID + P], cst[:, C_TRI:C_TRI + P], cst[:, C_ONE:C_ONE + P]
        par = cst[:, C_PAR:C_PAR + 2]
        x_res = sb("x_res", [P, NB, D])
        xn_full = sb("xn_full", [P, NB, D + 1])
        xn_all = xn_full[:, :, 0:D]
        xnT_all = sb("xnT_all", [P, KC, NB, PADW])
        w_att = sb("w_att", [P, 2, 4, KC, D])
        rt = sb("rt", [P, KC, E0 + E1])
        w_ffn = sb("w_ffn", [P, E0, W0])
        w_sh = sb("w_sh", [P, W0])
        sc = w_ffn[:, 7, 0:2048].rearrange("p (g i s) -> p g i s", g=NBANK, i=4)
        pr = w_ffn[:, 6, 0:2048].rearrange("p (g i s) -> p g i s", g=NBANK, i=4)
        pt = w_ffn[:, 5, 0:2048].rearrange("p (g i s) -> p g i s", g=NBANK, i=4)
        dist = w_ffn[:, 4, 0:2048].rearrange("p (b s) -> p b s", b=NB)
        bias_all = w_ffn[:, 3, 0:2048].rearrange("p (b s) -> p b s", b=NB)
        hid = [w_ffn[:, 4 + i, 2048:2560] for i in range(4)]

        mlp = sb("mlp", [P, 3 * KB + 1])
        a_bc, b_bc, c_bc, bb2 = mlp[:, 0:KB], mlp[:, KB:2 * KB], mlp[:, 2 * KB:3 * KB], mlp[:, 3 * KB:3 * KB + 1]
        qkb = sb("qkb", [P, 2, KC])
        qb4 = sb("qb4", [P, KC])
        kbm = sb("kbm", [P, KC, 2])
        bvo = sb("bvo", [P, 2, D])
        rbias = sb("rbias", [P, E1])
        work = sb("work", [P, 5120])

        def attention_tile(at_column, *shape):
            n = int(np.prod(shape))
            return work[:, at_column:at_column + n], at_column + n

        col = 0
        ctx_k, col = attention_tile(col, KC, P)
        ctx_v, col = attention_tile(col, KC, P)
        xn, col = attention_tile(col, D)
        xnT, col = attention_tile(col, KC, P)
        qT, col = attention_tile(col, KC, P)
        kz, col = attention_tile(col, KC, 2, P)
        attn, col = attention_tile(col, D)
        attnT, col = attention_tile(col, KC, P)
        xn1, col = attention_tile(col, D)
        xn1T, col = attention_tile(col, KC, P)
        ctx_k, ctx_v, xnT, qT, attnT, xn1T = (
            v.rearrange("p (k s) -> p k s", k=KC) for v in (ctx_k, ctx_v, xnT, qT, attnT, xn1T))
        kz = kz.rearrange("p (k h s) -> p k h s", k=KC, h=2)
        acc0, col = attention_tile(col, MG * P)
        acc, col = attention_tile(col, MG * P)
        sg = work[:, 3072:4096].rearrange("p (a s) -> p a s", a=2)
        hT = work[:, 4096:5120].rearrange("p (a s) -> p a s", a=2)
        xs = work[:, 3072 - 4 * (D + 1):3072].rearrange("p (a j d) -> p a j d", a=2, j=2)
        xsT = work[:, 3072:3584]
        hs = work[:, 3584:4096]
        hsT = work[:, 0:512]
        sgs = work[:, 512:1024]
        ys = work[:, 4096:5120].rearrange("p (a j d) -> p a j d", a=2, j=2)
        rw = [work[:, 256 * i:256 * (i + 1)] for i in range(12)]
        va = sb("va", [P, NH, VW])
        mx = sb("mx", [P, NBANK, 4])
        rsum = sb("rsum", [P, NH])
        lg = sb("lg", [P, NB, E1])
        picks = rw[6]
        slot = sb("slot", [P, 2, NB], I32)
        step_experts = sb("step_experts", [P, NS], I32)
        wgt = sb("wgt", [P, 2, NB])
        small = sb("small", [P, 8, NB])
        need_i = sb("need_i", [P, E1], I32)
        te_f = sb("te_f", [P, T1])
        seg, result_rows, own_rows = cst[:, C_SEG:C_OUT], cst[:, C_OUT:C_OUT + NB], cst[:, C_OWN:C_END]
        zeros = sb("zeros", [P, D + 1])
        row_ids = sb("row_ids", [P, NS, JT[1]])
        result_at = sb("result_at", [P, 2, JT[1]], I32)
        rows_b = xnT_all[:].rearrange("p k b s -> p (k b s)")[:, 0:NB * D].rearrange("p (b d) -> p b d", b=NB)
        w1_ffn = w_ffn[:, 0:4, :].rearrange("p a w -> p (a w)")[:, 0:R1 * W1].rearrange("p (e w) -> p e w", e=R1)
        ln_st = sb("ln_st", [P, 2, 6])
        ln_mv = sb("ln_mv", [P, 2, 2])
        ln_ve = sb("ln_ve", [P, 2])
        ln_rs = sb("ln_rs", [P, 2])
        mhalf = sb("mhalf", [P, 1])
        unread = sb("unread", [P, 1])

        consts_in, x_in, mlp_in, dist_in, watt0_in, watt1_in, small_in = map(
            sem, ("consts_in", "x_in", "mlp_in", "dist_in", "watt0_in", "watt1_in", "small_in"))
        ctx_k_in, ctx_v_in = sem("ctx_k_in"), sem("ctx_v_in")
        x0_in, dist0_in, mask0_in, watt0b_in = map(sem, ("x0_in", "dist0_in", "mask0_in", "watt0b_in"))
        setup_pool, setup_dve = sem("setup_pool"), sem("setup_dve")
        stats_done, aggr_done, var_ready, rstd_ready = map(sem, ("stats_done", "aggr_done", "var_ready", "rstd_ready"))
        stats1_done, aggr1_done, var1_ready, rstd1_ready = map(
            sem, ("stats1_done", "aggr1_done", "var1_ready", "rstd1_ready"))
        xn_ready, xnT_in_psum, xnT_ready = map(sem, ("xn_ready", "xnT_in_psum", "xnT_ready"))
        k_in_psum, kz_ready, q_in_psum, q_ready = map(sem, ("k_in_psum", "kz_ready", "q_in_psum", "q_ready"))
        v_in_psum, v_ready = sem("v_in_psum"), sem("v_ready")
        scores_in_psum, biased, max_ready, shifted, probs_ready = map(
            sem, ("scores_in_psum", "biased", "max_ready", "shifted", "probs_ready"))
        pt_in_psum, pt_ready, av_in_psum, rsum_ready, attn_ready = map(
            sem, ("pt_in_psum", "pt_ready", "av_in_psum", "rsum_ready", "attn_ready"))
        attnT_in_psum, attnT_ready, wo_in_psum, x1_ready = map(
            sem, ("attnT_in_psum", "attnT_ready", "wo_in_psum", "x1_ready"))
        xn1_kept = sem("xn1_kept")
        xn1_ready, xn1T_in_psum, xn1T_ready, xnT_kept, lg_in_psum, lg_ready = map(
            sem, ("xn1_ready", "xn1T_in_psum", "xn1T_ready", "xnT_kept", "lg_in_psum", "lg_ready"))
        hid_ready, hid_scaled, hid0_added, hid_added, bias_ready, bo_added = map(
            sem, ("hid_ready", "hid_scaled", "hid0_added", "hid_added", "bias_ready", "bo_added"))
        stored = sem("stored")
        x2_ready = sem("x2_ready")
        zeros_set, out_rows_set = sem("zeros_set"), sem("out_rows_set")
        first_scattered = [sem(f"first_scattered{i}") for i in range(2)]
        ids_kept, ids_placed = sem("ids_kept"), sem("ids_placed")
        route_step = sem("route_step")
        rows_zeroed = [sem(f"rows_zeroed{i}") for i in range(2)]
        ffn_in = [sem(f"ffn_in{i}") for i in range(4)]
        centred, exp_ready = sem("centred"), sem("exp_ready")
        picks_ready = [sem(f"picks_ready{i}") for i in range(2)]
        ranks_in_psum = [sem(f"ranks_in_psum{i}") for i in range(2)]
        slots_ready = [sem(f"slots_ready{i}") for i in range(2)]
        experts_ready = [sem(f"experts_ready{i}") for i in range(2)]
        scattered = [sem(f"scattered{i}") for i in range(2)]
        gathered = sem("gathered")
        results_loaded = [sem(f"results_loaded{g}") for g in range(NB // MG)]
        sh_gu_in_psum, sh_silu, sh_hidden, sh_used, sh_added = (
            [sem(f"{name}{i}") for i in range(2)]
            for name in ("sh_gu_in_psum", "sh_silu", "sh_hidden", "sh_used", "sh_added"))
        xs_in = [[sem(f"xs_in{i}{p}") for p in range(2)] for i in range(2)]
        ys_stored = [[sem(f"ys_stored{i}{p}") for p in range(2)] for i in range(2)]
        xsT_in_psum, xsT_ready, gu_in_psum, silu_ready, hs_ready, hsT_in_psum, hsT_ready, ys_in_psum, ys_ready = (
            [sem(f"{name}{i}") for i in range(2)]
            for name in ("xsT_in_psum", "xsT_ready", "gu_in_psum", "silu_ready", "hs_ready", "hsT_in_psum",
                         "hsT_ready", "ys_in_psum", "ys_ready"))
        weighted = sem("weighted")
        out_ready = sem("out_ready")
        waits_ended = sem("waits_ended")

        block = ctx.enter_context(nc.Block())

        def pipeline(eng, body):
            body(0, None, None, None)
            body(1, 0, None, None)
            body(2, 1, 0, None)
            body(3, 2, 1, 0)
            with eng.Fori(3, NB - 1) as n:
                body(n + 1, n, n - 1, n - 2)
            body(None, NB - 1, NB - 2, NB - 3)
            body(None, None, NB - 1, NB - 2)
            body(None, None, None, NB - 1)

        def apart(eng):
            eng.sem_inc(waits_ended, 1)

        SHARED = (((0, 1), (2, 3)), ((0, 1, 2, 3),))

        EARLY = (1, 1)

        def shared_steps(layer, groups):
            chunks = HC0 if layer == 0 else 1
            return [(g, c, g * chunks + c) for g in groups for c in range(chunks)]

        def half(layer, g, c):
            return c % 2 if layer == 0 else g % 2

        def at(layer, b):
            return b + NB * layer

        def results_in(eng, a, to):
            for p in range(2):
                eng.wait_ge(ys_stored[1][p], 16 * JT[1] * ((NS + 1 - p) // 2))
            for g in range(NB // MG):
                start = RESULTS + a * SECOND + g * MG * P
                eng.dma_start(to[:, g * MG:(g + 1) * MG, :],
                              rows[1][start:start + MG * P, 0:D].rearrange("(b p) d -> p b d", p=P))\
                    .then_inc(results_loaded[g], 16)

        @block.sync
        def _(sp):
            sp.dma_start(x_res[:, 0:2, :], t["x"][:, 0:2, :]).then_inc(x0_in, 16)
            sp.dma_start(cst[:], t["consts"]).then_inc(consts_in, 16)
            sp.dma_start(ctx_k[:], t["ctxT"][:, :, 0:P]).then_inc(ctx_k_in, 16)
            sp.wait_ge(dist0_in, 16)
            sp.dma_start(w_att[:, 0, 0:2], t["w_att0"][:, 0:2]).then_inc(watt0_in, 16)
            sp.dma_start(ctx_v[:], t["ctxT"][:, :, 0:P]).then_inc(ctx_v_in, 16)
            sp.dma_start(w_att[:, 0, 2:4], t["w_att0"][:, 2:4]).then_inc(watt0b_in, 16)
            sp.dma_start(rt[:], t["rt"]).then_inc(small_in, 16)
            sp.dma_start(x_res[:, 2:NB, :], t["x"][:, 2:NB, :]).then_inc(x_in, 16)

            ZERO = (T0 // NB, T1 // NB)

            def zero(i, start, tiles):
                sp.dma_start(rows[i][bass.ds(start * P, tiles * P)].rearrange("(t p) d -> p t d", p=P),
                             zeros[:, 0:D + i].unsqueeze(1).broadcast_to([P, tiles, D + i]))\
                    .then_inc(rows_zeroed[i], 16)

            def attention(layer):
                def load_k(n):
                    sp.wait_ge(k_in_psum, at(layer, n))
                    sp.dma_start(ctx_k[:], t["ctxT"][:, :, bass.ds(n * P, P)]).then_inc(ctx_k_in, 16)

                def load_v(n):
                    sp.wait_ge(v_in_psum, at(layer, n))
                    sp.dma_start(ctx_v[:], t["ctxT"][:, :, bass.ds(n * P, P)]).then_inc(ctx_v_in, 16)

                if layer:
                    load_k(0)
                    load_v(0)
                load_k(1)
                with sp.Fori(1, NB - 1) as n:
                    load_k(n + 1)
                    load_v(n)
                    if layer == 0:
                        for i in range(2):
                            zero(i, n * ZERO[i], ZERO[i])
                    else:
                        e = n - 1
                        sp.dma_start(w1_ffn[:, bass.ds(e, 1), :], t["w_ffn1"][:, bass.ds(e, 1), :])\
                            .then_inc(ffn_in[3], 16)
                if layer == 0:
                    sp.dma_start(w_sh[:], t["w_sh0"]).then_inc(ffn_in[0], 16)
                    for i, tiles in ((0, T0), (1, T1)):
                        zero(i, 0, ZERO[i])
                        zero(i, (NB - 1) * ZERO[i], tiles - (NB - 1) * ZERO[i])
                load_v(NB - 1)
                if layer:
                    for e in range(NB - 2, R1):
                        sp.dma_start(w1_ffn[:, e, :], t["w_ffn1"][:, e, :]).then_inc(ffn_in[3], 16)
                    sp.wait_ge(sh_used[0], NB)
                    sp.dma_start(w_sh[:, 0:t["w_sh1"].shape[1]], t["w_sh1"]).then_inc(ffn_in[3], 16)
                if layer == 0:
                    for e in range(3):
                        sp.dma_start(w_ffn[:, e, :], t["w_ffn0"][:, e, :]).then_inc(ffn_in[1], 16)

            sp.wait_ge(zeros_set, 1)
            attention(0)

            def sorted_tiles(layer):
                tiles = rows[layer][0:NS * JT[layer] * P].rearrange("(n j p) d -> n p j d", j=JT[layer], p=P)
                nj = JT[layer]

                def load(n, p):
                    if not (static(n) and n < 2):
                        sp.wait_ge(xsT_in_psum[layer], n - 1)
                        if layer:
                            sp.wait_ge(ids_kept, n - 1)
                    sp.dma_start(xs[:, p, 0:nj, 0:D + layer], tiles[n]).then_inc(xs_in[layer][p], 16)

                def store(b, p):
                    sp.wait_ge(ys_ready[layer], b + 1)
                    sp.dma_start(tiles[b], ys[:, p, 0:nj, :]).then_inc(ys_stored[layer][p], 16)

                sp.wait_ge(scattered[layer], 16 * NB)
                sp.wait_ge(experts_ready[layer], 1)
                load(0, 0)
                load(1, 1)

                def body(n, b, p):
                    if n is not None and not (static(n) and n + 2 >= NS):
                        load(n + 2, p)
                    if b is not None and layer == 0:
                        store(b, 1 - p)

                body(0, None, 0)
                body(1, 0, 1)
                body(2, 1, 0)
                with sp.Fori(1, (NS - 3) // 2) as i:
                    body(i * 2 + 1, i * 2, 1)
                    body(i * 2 + 2, i * 2 + 1, 0)
                body(NS - 2, NS - 3, 1)
                if layer == 0:
                    store(NS - 2, 1)
                    store(NS - 1, 0)

            sp.wait_ge(lg_ready, NB)
            sp.wait_ge(av_in_psum, NB)
            sp.wait_ge(bias_ready, NB // MG)
            for e in range(3, E0):
                sp.dma_start(w_ffn[:, e, :], t["w_ffn0"][:, e, :]).then_inc(ffn_in[2], 16)
            sp.dma_start(w_att[:, 1], t["w_att1"]).then_inc(watt1_in, 16)
            sorted_tiles(0)
            sp.wait_ge(ys_in_psum[0], NS)
            attention(1)
            sorted_tiles(1)
            results_in(sp, 0, xn_all)
            for g in range(NB // MG):
                sp.wait_ge(out_ready, g + 1)
                sp.dma_start(out[g * MG:(g + 1) * MG].rearrange("b t c -> t b c"), x_res[:, g * MG:(g + 1) * MG])\
                    .then_inc(stored, 16)
            sp.wait_ge(stored, 16 * (NB // MG))

        @block.gpsimd
        def _(pool):
            nc.gpsimd.memset(zeros[:], 0.0).then_inc(zeros_set, 1)
            nc.gpsimd.memset(mhalf[:], -0.5).then_inc(setup_pool, 1)
            nc.gpsimd.memset(va[:], 1.0).then_inc(setup_pool, 1)
            nc.gpsimd.memset(xnT_all[:, :, :, 0:2], 0.0).then_inc(setup_pool, 1)
            pool.wait_ge(consts_in, 16)
            nc.gpsimd.tensor_copy(xn_full[:, :, D], result_rows).then_inc(out_rows_set, 1)
            pool.wait_ge(setup_pool, 1)

            def mlp_units(group, quarter, done, which):
                scaled = (group - 1) * (KB - 1) + 4 * quarter
                for i in which:
                    k = 4 * quarter + i
                    coef = c_bc[:, k:k + 1]
                    pool.wait_ge(hid_ready, done + i + 1)
                    apart(pool)
                    if k == 0:
                        if not (static(group) and group == 1):
                            pool.wait_ge(bias_ready, group)
                            apart(pool)
                        nc.gpsimd.tensor_scalar(acc[:], hid[i], coef, bb2, ALU.mult, ALU.add).then_inc(hid_added, 1)
                    else:
                        nc.gpsimd.tensor_scalar(hid[i], hid[i], coef, 0.0, ALU.mult, ALU.add).then_inc(hid_scaled, 1)
                        pool.wait_ge(hid_scaled, scaled + i)
                        pool.wait_ge(hid_added, done + i - KB)
                        apart(pool)
                        nc.gpsimd.tensor_tensor(acc[:], acc[:], hid[i], ALU.add).then_inc(hid_added, 1)
                if quarter == 3 and 3 in which:
                    if static(group):
                        pool.wait_ge(dist_in, 32)
                    pool.wait_ge(hid_added, done + 4 - KB)
                    four = bias_all[:, bass.ds(group * MG, MG), :].rearrange("p b s -> p (b s)")
                    apart(pool)
                    nc.gpsimd.tensor_tensor(four, four, acc[:], ALU.add).then_inc(bias_ready, 1)

            def rstd(layer, n):
                pool.wait_ge(var_ready, at(layer, n) + 1)
                nc.gpsimd.tensor_tensor(ln_rs[:, 0:1], ln_ve[:, 0:1], mhalf[:], ALU.pow).then_inc(rstd_ready, 1)

            def rstd1(layer, b):
                pool.wait_ge(var1_ready, at(layer, b) + 1)
                nc.gpsimd.tensor_tensor(ln_rs[:, 1:2], ln_ve[:, 1:2], mhalf[:], ALU.pow).then_inc(rstd1_ready, 1)

            def keep(layer, b):
                pool.wait_ge(xn1_ready, at(layer, b) + 1)
                apart(pool)
                nc.gpsimd.tensor_copy(xn_all[:, b, :], xn1[:]).then_inc(xn1_kept, 1)

            def first(m, n, b, c, quarter, mlp_on=True):
                if m is not None:
                    if not (static(m) and m == 1):
                        rstd(0, m)
                    if static(m) and m == 0:
                        rstd(0, 1)
                    if mlp_on:
                        mlp_units((m - quarter) // 4 + 1, quarter, m * 4 + KB, (0,))
                if c is not None:
                    rstd1(0, c)
                if m is not None and mlp_on:
                    mlp_units((m - quarter) // 4 + 1, quarter, m * 4 + KB, (1, 2, 3))
                if c is not None:
                    keep(0, c)

            first(0, None, None, None, 0)
            first(1, 0, None, None, 1)
            first(2, 1, 0, None, 2)
            first(3, 2, 1, 0, 3)
            with pool.Fori(1, NB // 4 - 1) as i:
                for r in range(4):
                    first(i * 4 + r, i * 4 + (r - 1), i * 4 + (r - 2), i * 4 + (r - 3), r)
            with pool.Fori(NB - 4, NB) as m:
                first(m, m - 1, m - 2, m - 3, 0, False)
            first(None, NB - 1, NB - 2, NB - 3, 0)
            first(None, None, NB - 1, NB - 2, 0)
            first(None, None, None, NB - 1, 0)

            def scatter(layer):
                pool.wait_ge(rows_zeroed[layer], 16 * NB)
                pool.wait_ge(xn1_kept, NB * (layer + 1))
                if layer:
                    pool.wait_ge(out_rows_set, 1)
                for a in range(1 + layer):
                    pool.wait_ge(slots_ready[layer], a + 1)
                    for b in range(NB):
                        if a and b % (NB // 2) == 0:
                            pool.wait_ge(first_scattered[b // (NB // 2)], 16 * (NB // 2))
                            out_rows = xn_full[:, b:b + NB // 2, D]
                            nc.gpsimd.tensor_scalar(out_rows, out_rows, float(SECOND), None, ALU.add)\
                                .then_inc(out_rows_set, 1)
                            pool.wait_ge(out_rows_set, 2 + b // (NB // 2))
                        done = first_scattered[b // (NB // 2)] if layer and a == 0 else scattered[layer]
                        nc.gpsimd.indirect_dma_start(
                            rows[layer], bass.IndirectOffsetOnAxis(ap=slot[:, a, b:b + 1], axis=0),
                            xn_full[:, b, 0:D + layer], None).then_inc(done, 16)

            scatter(0)
            for p in range(2):
                pool.wait_ge(ys_stored[0][p], 16 * ((NS + 1 - p) // 2))
            for b in range(NB):
                nc.gpsimd.indirect_dma_start(
                    xn_all[:, b, :], None, rows[0], bass.IndirectOffsetOnAxis(ap=slot[:, 0, b:b + 1], axis=0))\
                    .then_inc(gathered, 16)
            pool.wait_ge(gathered, 16 * NB)
            pool.wait_ge(sh_added[0], MG)

            def add_ffn(n):
                nc.gpsimd.tensor_tensor(x_res[:, n, :], x_res[:, n, :], xn_all[:, n, :], ALU.add).then_inc(x2_ready, 1)

            def second(m, n, b, c):
                if m is not None:
                    rstd(1, m)
                    if not (static(m) and m == NB - 1):
                        add_ffn(m + 1)
                    pool.wait_ge(xn_ready, at(1, m) + 1)
                    apart(pool)
                    nc.gpsimd.tensor_tensor(x_res[:, m, :], x_res[:, m, :], bvo[:, 1, :], ALU.add).then_inc(bo_added, 1)
                if c is not None:
                    rstd1(1, c)
                    keep(1, c)

            add_ffn(0)
            second(0, None, None, None)
            pool.wait_ge(sh_added[0], NB)
            second(1, 0, None, None)
            second(2, 1, 0, None)
            second(3, 2, 1, 0)
            with pool.Fori(3, NB - 2) as n:
                second(n + 1, n, n - 1, n - 2)
            second(NB - 1, NB - 2, NB - 3, NB - 4)
            second(None, NB - 1, NB - 2, NB - 3)
            second(None, None, NB - 1, NB - 2)
            second(None, None, None, NB - 1)
            scatter(1)

            def store_results(b, p):
                if not (static(b) and b < 2):
                    pool.wait_ge(ys_stored[1][p], (b // 2) * 16 * JT[1])
                pool.wait_ge(ids_kept, b + 1)
                apart(pool)
                nc.gpsimd.tensor_copy(result_at[:, p:p + 1, :], row_ids[:, bass.ds(b, 1), :]).then_inc(ids_placed, 1)
                pool.wait_ge(ids_placed, b + 1)
                pool.wait_ge(ys_ready[1], b + 1)
                apart(pool)
                for j in range(JT[1]):
                    nc.gpsimd.indirect_dma_start(
                        rows[1], bass.IndirectOffsetOnAxis(ap=result_at[:, p, j:j + 1], axis=0),
                        ys[:, p, j, 0:D], None).then_inc(ys_stored[1][p], 16)

            store_results(0, 0)
            store_results(1, 1)
            store_results(2, 0)
            with pool.Fori(2, NS // 2) as i:
                store_results(i * 2 - 1, 1)
                store_results(i * 2, 0)
            store_results(NS - 2, 1)
            store_results(NS - 1, 0)

        @block.scalar
        def _(act):
            A = nc.scalar.activation

            def unit(group, k, done, i, used):
                if not static(used) or used > 0:
                    act.wait_ge(hid0_added if static(done) and done + i < KB + 4 else hid_added, used)
                A(hid[i], dist[:, bass.ds(group * MG, MG), :].rearrange("p b s -> p (b s)"), ACT.Relu,
                  bias=b_bc[:, bass.ds(k, 1)], scale=a_bc[:, bass.ds(k, 1)]).then_inc(hid_ready, 1)

            def attention(layer):
                def keys(m):
                    act.wait_ge(k_in_psum, at(layer, m) + 1)
                    pk = ps_pm[:, 0:KC * P].rearrange("p (k s) -> p k s", k=KC)
                    for h in range(2):
                        if layer == 0:
                            last = A(kz[:, :, h, :], pk, ACT.Copy, scale=par[:, h:h + 1])
                        else:
                            for k in range(KC):
                                last = A(kz[:, k, h, :], pk[:, k, :], ACT.Identity, scale=par[:, h:h + 1],
                                         bias=kbm[:, k, h:h + 1])
                    last.then_inc(kz_ready, 1)

                def body(m, n, b, c, mlp_on=True):
                    mlp_here = layer == 0 and mlp_on and m is not None

                    def units(which):
                        for i in which:
                            used = m * 4 + i - 3
                            unit(m // 4 + 1, (m % 4) * 4 + i, m * 4 + KB, i, used)

                    def weightsT(j):
                        act.wait_ge(pt_in_psum, at(layer, b) * 4 + j + 1)
                        if j == 0 and not (layer == 0 and static(b) and b == 0):
                            act.wait_ge(av_in_psum, at(layer, b))
                        bank = ps_pb if j % 2 == 0 else ps_pa
                        A(pt[:, j].rearrange("p i s -> p (i s)"), bank[:, :], ACT.Copy).then_inc(pt_ready, 1)

                    def probs(j):
                        act.wait_ge(shifted, at(layer, n) * 4 + j + 1)
                        if not (layer == 0 and static(n) and n == 0):
                            act.wait_ge(pt_in_psum, at(layer, n) * 4 - 3 + j)
                        A(pr[:, j], sc[:, j], ACT.Exp).then_inc(probs_ready, 1)

                    if c is not None:
                        act.wait_ge(attnT_in_psum, at(layer, c) + 1)
                        A(attnT[:].rearrange("p k s -> p (k s)"), ps_pa[:, 0:D], ACT.Copy).then_inc(attnT_ready, 1)
                    if b is not None:
                        weightsT(0)
                    if mlp_here:
                        units((0,))
                    if b is not None:
                        weightsT(1)
                    if m is not None:
                        if n is not None:
                            act.wait_ge(scores_in_psum, at(layer, n) * 2 + 2)
                        keys(m)
                    if n is not None:
                        probs(0)
                    if b is not None:
                        weightsT(2)
                    if m is not None:
                        act.wait_ge(xnT_in_psum, at(layer, m) + 1)
                        A(xnT[:].rearrange("p k s -> p (k s)"), ps_pm[:, 0:D], ACT.Copy).then_inc(xnT_ready, 1)
                    if layer == 0 and static(m) and m == 0:
                        for k in (10, 11):
                            unit(0, k, 0, k % 4, k - 3)
                    if n is not None:
                        probs(1)
                    if mlp_here:
                        units((1,))
                    if b is not None:
                        weightsT(3)
                    if m is not None:
                        act.wait_ge(q_in_psum, at(layer, m) + 1)
                        if layer == 0:
                            A(qT[:].rearrange("p k s -> p (k s)"), ps_pm[:, 0:D], ACT.Copy, scale=0.25)\
                                .then_inc(q_ready, 1)
                        else:
                            for k in range(KC):
                                last = A(qT[:, k, :], ps_pm[:, k * P:(k + 1) * P], ACT.Identity, scale=0.25,
                                         bias=qb4[:, k:k + 1])
                            last.then_inc(q_ready, 1)
                    if mlp_here:
                        units((2, 3))
                    if n is not None and layer:
                        probs(2)
                    if c is not None:
                        act.wait_ge(xn1T_in_psum, at(layer, c) + 1)
                        A(xn1T[:].rearrange("p k s -> p (k s)"), ps_pb[:, 0:D], ACT.Copy).then_inc(xn1T_ready, 1)
                        A(xnT_all[:, :, c, 2:PADW], ps_pb[:, 0:D].rearrange("p (k s) -> p k s", k=KC), ACT.Copy)\
                            .then_inc(xnT_kept, 1)
                    if n is not None and layer == 0:
                        probs(2)
                        act.wait_ge(v_in_psum, at(layer, n) + 1)
                        if b is not None:
                            act.wait_ge(av_in_psum, at(layer, b) + 1)
                        A(va[:, :, 0:HD], ps_pm[:, 0:D].rearrange("p (h d) -> p h d", h=NH), ACT.Copy)\
                            .then_inc(v_ready, 1)
                    if n is not None:
                        probs(3)
                    if c is not None:
                        act.wait_ge(lg_in_psum, at(layer, c) + 1)
                        ne = E1 if layer else E0
                        A(lg[:, c, 0:ne], ps_po[:, 0:ne], ACT.Copy).then_inc(lg_ready, 1)

                if layer:
                    pipeline(act, body)
                else:
                    body(0, None, None, None, False)
                    for k in range(12, KB):
                        unit(0, k, 0, k % 4, k - 3)
                    act.wait_ge(dist_in, 32)
                    for k in range(4):
                        unit(1, k, KB, k, KB + k - 3)
                    body(1, 0, None, None)
                    body(2, 1, 0, None)
                    body(3, 2, 1, 0)
                    with act.Fori(3, NB - MG - 1) as n:
                        body(n + 1, n, n - 1, n - 2)
                    with act.Fori(NB - MG - 1, NB - 1) as n:
                        body(n + 1, n, n - 1, n - 2, False)
                    body(None, NB - 1, NB - 2, NB - 3)
                    body(None, None, NB - 1, NB - 2)
                    body(None, None, None, NB - 1)

            act.dma_start(mlp[:], t["mlp"]).then_inc(mlp_in, 16)
            act.dma_start(dist[:, 0:MG], t["dist"][:, 0:MG]).then_inc(dist0_in, 16)
            act.dma_start(bias_all[:, 0:MG], t["mask"][:, 0:MG]).then_inc(mask0_in, 16)
            act.dma_start(qkb[:], t["qkb"]).then_inc(small_in, 16)
            act.dma_start(bvo[:], t["bvo"]).then_inc(small_in, 16)
            act.dma_start(rbias[:], t["rbias"]).then_inc(small_in, 16)
            act.wait_ge(mlp_in, 16)
            act.wait_ge(dist0_in, 16)
            for k in range(10):
                unit(0, k, 0, k % 4, k - 3)
            act.dma_start(dist[:, MG:], t["dist"][:, MG:]).then_inc(dist_in, 16)
            act.dma_start(bias_all[:, MG:], t["mask"][:, MG:]).then_inc(dist_in, 16)
            act.wait_ge(consts_in, 16)
            act.wait_ge(setup_pool, 3)
            attention(0)

            def shared(layer, groups):
                for g, c, q in shared_steps(layer, groups):
                    h = half(layer, g, c)
                    act.wait_ge(sh_gu_in_psum[layer], q + 1)
                    if q >= 2:
                        act.wait_ge(sh_hidden[layer], q - 1)
                    A(sg[:, h, :], ps[h][:, :], ACT.Silu).then_inc(sh_silu[layer], 1)

            def sorted_tiles(layer):
                def body(n, b, p):
                    def rowsT(n):
                        act.wait_ge(xsT_in_psum[layer], n + 1)
                        w = D * JT[layer]
                        if not (static(n) and n == 0):
                            act.wait_ge(gu_in_psum[layer], n)
                        A(xsT[:, 0:w], ps[4][:, 0:w], ACT.Copy).then_inc(xsT_ready[layer], 1)

                    if b is not None:
                        w = HC0 * P if layer == 0 else 2 * P
                        act.wait_ge(hsT_in_psum[layer], b + 1)
                        if not (static(b) and b == 0):
                            act.wait_ge(ys_in_psum[layer], b)
                        A(hsT[:, 0:w], ps[2][:, 0:w], ACT.Copy).then_inc(hsT_ready[layer], 1)
                    if n is not None:
                        if static(n) and n == 0:
                            rowsT(0)
                        act.wait_ge(gu_in_psum[layer], n + 1)
                        if not (static(n) and n == 0):
                            act.wait_ge(hs_ready[layer], n)
                        if layer == 0:
                            A(sgs[:, 0:H0], ps[0][:, 0:H0], ACT.Silu).then_inc(silu_ready[layer], 1)
                        else:
                            A(sgs[:, 0:2 * H1].rearrange("p (j h) -> p j h", j=2),
                              ps[0][:, :].rearrange("p (j a h) -> p j a h", j=2, a=2)[:, :, 0, :], ACT.Silu)\
                                .then_inc(silu_ready[layer], 1)
                        if not (static(n) and n == NS - 1):
                            rowsT(n + 1)
                    if b is not None:
                        act.wait_ge(ys_in_psum[layer], b + 1)
                        if not (static(b) and b < 2):
                            act.wait_ge(ys_stored[layer][1 - p], (b // 2) * 16 * JT[layer])
                        w = D * JT[layer]
                        A(ys[:, 1 - p, 0:JT[layer], :].rearrange("p j d -> p (j d)"), ps[3][:, 0:w], ACT.Copy)\
                            .then_inc(ys_ready[layer], 1)

                body(0, None, 0)
                body(1, 0, 1)
                body(2, 1, 0)
                with act.Fori(1, (NS - 3) // 2) as i:
                    body(i * 2 + 1, i * 2, 1)
                    body(i * 2 + 2, i * 2 + 1, 0)
                body(NS - 2, NS - 3, 1)
                body(NS - 1, NS - 2, 0)
                body(None, NS - 1, 1)

            def tables(func):
                A(unread[:], mhalf[:], func)

            tables(ACT.Silu)
            act.wait_ge(xn1_kept, NB)
            shared(0, SHARED[0][0])
            sorted_tiles(0)
            shared(0, SHARED[0][1])
            tables(ACT.Exp)
            attention(1)
            act.wait_ge(centred, 1)
            A(rw[1], rw[0], ACT.Exp).then_inc(exp_ready, 1)
            tables(ACT.Silu)
            act.wait_ge(xn1_kept, 2 * NB)
            shared(1, SHARED[1][0])
            sorted_tiles(1)
            act.wait_ge(sh_used[1], NB // MG)
            results_in(act, 1, rows_b)

        @block.tensor
        def _(pe):
            mm, tr = nc.tensor.matmul, nc.tensor.transpose

            def attention(layer):
                wq, wk, wv, wo = (w_att[:, layer, i] for i in range(4))
                r0 = E0 if layer else 0
                ne = E1 if layer else E0

                def since(signal, count):
                    if not static(count) or count > 0:
                        pe.wait_ge(signal, count)

                def body(m, n, b, c):
                    def scores(half, k):
                        if n is None:
                            return
                        if half == 0 and k == 0:
                            pe.wait_ge(q_ready, at(layer, n) + 1)
                            pe.wait_ge(kz_ready, at(layer, n) + 1)
                        if k == 0:
                            since(shifted, at(layer, n) * 4 - 2 + 2 * half)
                        for j in (2 * half, 2 * half + 1):
                            r = slice(32 * j, 32 * j + 32)
                            last = mm(ps_s[j][:, k * 256:(k + 1) * 256], qT[r, k, :],
                                      kz[r, k].rearrange("p h s -> p (h s)"), start=True, stop=True)
                        if k == KC - 1:
                            last.then_inc(scores_in_psum, 1)

                    def weightsT(j):
                        if b is None:
                            return
                        pe.wait_ge(probs_ready, at(layer, b) * 4 + j + 1)
                        if j == 0:
                            since(pt_ready, at(layer, b) * 4 - 1)
                            since(xn1T_ready, at(layer, b) - 1)
                            since(xnT_kept, at(layer, b) - 1)
                        elif j == 1:
                            since(attnT_ready, at(layer, b))
                        else:
                            pe.wait_ge(pt_ready, at(layer, b) * 4 + j - 1)
                        bank = ps_pb if j % 2 == 0 else ps_pa
                        for i in range(4):
                            last = tr(bank[:, i * P:(i + 1) * P], pr[:, j, i, :], ident)
                        last.then_inc(pt_in_psum, 1)

                    def weighted_values(j):
                        if b is None:
                            return
                        pe.wait_ge(pt_ready, at(layer, b) * 4 + j + 1)
                        if j == 0:
                            pe.wait_ge(v_ready, at(layer, b) + 1)
                            since(x1_ready, at(layer, b))
                            since(lg_ready, at(layer, b) - 1)
                        for i in range(4):
                            h = head_of(j, i)
                            last = mm(ps_po[:, h * VW:(h + 1) * VW], pt[:, j, i, :], va[:, h, :], start=True, stop=True)
                        if j == 3:
                            last.then_inc(av_in_psum, 1)

                    def attended():
                        if c is None:
                            return
                        pe.wait_ge(attn_ready, at(layer, c) + 1)
                        since(pt_ready, at(layer, c) * 4 + 4)
                        for k in range(KC):
                            last = tr(ps_pa[:, k * P:(k + 1) * P], attn[:, k * P:(k + 1) * P], ident)
                        last.then_inc(attnT_in_psum, 1)

                    def keys():
                        if m is None:
                            return
                        pe.wait_ge(ctx_k_in, (at(layer, m) + 1) * 16)
                        since(v_ready, at(layer, m) - 1)
                        since(q_ready, at(layer, m))
                        for o in range(KC):
                            for k in range(KC):
                                last = mm(ps_pm[:, o * P:(o + 1) * P], wk[:, k, o * P:(o + 1) * P], ctx_k[:, k, :],
                                          start=(k == 0), stop=(k == KC - 1))
                        last.then_inc(k_in_psum, 1)

                    def output():
                        if c is None:
                            return
                        pe.wait_ge(attnT_ready, at(layer, c) + 1)
                        since(lg_ready, at(layer, c))
                        for k in range(KC):
                            last = mm(ps_po[:, 0:D], attnT[:, k, :], wo[:, k, :], start=(k == 0), stop=(k == KC - 1))
                        last.then_inc(wo_in_psum, 1)

                    def rows_in():
                        if m is None:
                            return
                        pe.wait_ge(xn_ready, at(layer, m) + 1)
                        pe.wait_ge(kz_ready, at(layer, m) + 1)
                        for k in range(KC):
                            last = tr(ps_pm[:, k * P:(k + 1) * P], xn[:, k * P:(k + 1) * P], ident)
                        last.then_inc(xnT_in_psum, 1)

                    def queries():
                        if m is None:
                            return
                        pe.wait_ge(xnT_ready, at(layer, m) + 1)
                        for o in range(KC):
                            for k in range(KC):
                                last = mm(ps_pm[:, o * P:(o + 1) * P], wq[:, k, o * P:(o + 1) * P], xnT[:, k, :],
                                          start=(k == 0), stop=(k == KC - 1))
                        last.then_inc(q_in_psum, 1)

                    def rows_out():
                        if c is None:
                            return
                        pe.wait_ge(xn1_ready, at(layer, c) + 1)
                        if b is None:
                            pe.wait_ge(xn1T_ready, at(layer, c))
                            pe.wait_ge(xnT_kept, at(layer, c))
                        for k in range(KC):
                            last = tr(ps_pb[:, k * P:(k + 1) * P], xn1[:, k * P:(k + 1) * P], ident)
                        last.then_inc(xn1T_in_psum, 1)

                    def values():
                        if n is None:
                            return
                        if layer == 0 and static(n) and n == 0:
                            pe.wait_ge(watt0b_in, 16)
                            pe.wait_ge(small_in, 64)
                        pe.wait_ge(ctx_v_in, (at(layer, n) + 1) * 16)
                        if m is not None:
                            pe.wait_ge(q_ready, at(layer, m) + 1)
                        else:
                            pe.wait_ge(v_ready, at(layer, n))
                        for k in range(KC):
                            last = mm(ps_pm[:, 0:D], ctx_v[:, k, :], wv[:, k, :], start=(k == 0), stop=(k == KC - 1))
                        last.then_inc(v_in_psum, 1)

                    def logits():
                        if c is None:
                            return
                        pe.wait_ge(xn1T_ready, at(layer, c) + 1)
                        if b is not None:
                            pe.wait_ge(attn_ready, at(layer, b) + 1)
                        for k in range(KC):
                            last = mm(ps_po[:, 0:ne], xn1T[:, k, :], rt[:, k, r0:r0 + ne], start=(k == 0), stop=(k == KC - 1))
                        last.then_inc(lg_in_psum, 1)

                    attended()
                    weightsT(0)
                    scores(0, 0)
                    scores(0, 1)
                    keys()
                    weightsT(1)
                    scores(1, 0)
                    output()
                    scores(1, 1)
                    weightsT(2)
                    weightsT(3)
                    weighted_values(0)
                    rows_in()
                    weighted_values(1)
                    queries()
                    weighted_values(2)
                    weighted_values(3)
                    rows_out()
                    values()
                    logits()
                pipeline(pe, body)

            pe.wait_ge(consts_in, 16)
            pe.wait_ge(watt0_in, 16)
            attention(0)

            def ranks(layer):
                w = NB * (E1 if layer else E0)
                pe.wait_ge(picks_ready[layer], 1)
                mm(ps_pm[:, 0:w], tri, picks[:, 0:w], start=True, stop=True)
                mm(ps_po[:, 0:w], ones, picks[:, 0:w], start=True, stop=True).then_inc(ranks_in_psum[layer], 1)

            def shared(layer, groups):
                wd = 2 * KC * H0 if layer == 0 else (CONV + 1) * KC * H1

                def down(g, c, q):
                    h = half(layer, g, c)
                    pe.wait_ge(sh_hidden[layer], q + 1)
                    if c == 0:
                        if g:
                            pe.wait_ge(sh_added[layer], g * MG)
                        else:
                            pe.wait_ge(slots_ready[layer], 1 + layer)
                    last_c = c == HC0 - 1 or layer == 1
                    for i in range(MG):
                        last = mm(ps[4 + i][:, 0:D], hT[:, h, i * P:(i + 1) * P], w_sh[:, wd + c * D:wd + (c + 1) * D],
                                  start=(c == 0), stop=last_c)
                    last.then_inc(sh_used[layer], 1)

                def gate_up(g, c, q):
                    h = half(layer, g, c)
                    if q >= 2:
                        pe.wait_ge(sh_hidden[layer], q - 1)
                    batches = bass.ds(g * MG, MG)
                    gate, up = ps[h][:, :].rearrange("p (b s) -> p b s", b=MG), \
                        ps[2 + h][:, :].rearrange("p (b s) -> p b s", b=MG)
                    if layer == 0:
                        for o, to in ((0, gate), (H0, up)):
                            for k in range(KC):
                                at_w = k * 2 * H0 + o + c * P
                                last = mm(to, w_sh[:, at_w:at_w + P], xnT_all[:, k, batches, 2:PADW],
                                          start=(k == 0), stop=(k == KC - 1))
                    else:
                        for k in range(KC):
                            for o in range(CONV):
                                at_w = (k * CONV + o) * H1
                                mm(gate, w_sh[:, at_w:at_w + H1], xnT_all[:, k, batches, o:o + P],
                                   start=(k == 0 and o == 0), stop=(k == KC - 1 and o == CONV - 1))
                        for k in range(KC):
                            at_w = (KC * CONV + k) * H1
                            last = mm(up, w_sh[:, at_w:at_w + H1], xnT_all[:, k, batches, 2:PADW],
                                      start=(k == 0), stop=(k == KC - 1))
                    last.then_inc(sh_gu_in_psum[layer], 1)

                steps = shared_steps(layer, groups)
                ahead = 4 if groups[0] == 0 else 1
                for i, step in enumerate(steps):
                    gate_up(*step)
                    if step[2] == EARLY[layer] - 1:
                        ranks(layer)
                    if i == ahead - 1:
                        for j in range(i):
                            down(*steps[j])
                    elif i >= ahead:
                        down(*steps[i - 1])
                down(*steps[-1])
                pe.wait_ge(sh_added[layer], (groups[-1] + 1) * MG)

            def sorted_tiles(layer):
                nj = JT[layer]

                def rowsT(n, p):
                    pe.wait_ge(xs_in[layer][p], (n // 2 + 1) * 16)
                    if not (static(n) and n == 0):
                        pe.wait_ge(xsT_ready[layer], n)
                    for j in range(nj):
                        for k in range(KC):
                            last = tr(ps[4][:, (j * KC + k) * P:(j * KC + k + 1) * P], xs[:, p, j, k * P:(k + 1) * P],
                                      ident)
                    last.then_inc(xsT_in_psum[layer], 1)

                base = R1 if layer else E0

                def experts_of(n):
                    code = pe.value_load(step_experts[0:1, bass.ds(n, 1)], min_val=0, max_val=base ** (2 * nj) - 1)
                    return [(code // base ** i) % base for i in range(nj)], [(code // base ** i) % base for i in range(nj, 2 * nj)]

                def body(n, b, p):
                    if n is not None:
                        experts_n, experts_b = experts_of(n)
                    else:
                        experts_b, _ = experts_of(b)
                    if b is not None:
                        pe.wait_ge(hs_ready[layer], b + 1)
                        if not (static(b) and b == 0):
                            pe.wait_ge(hsT_ready[layer], b)
                        for k in range(HC0 if layer == 0 else 2):
                            last = tr(ps[2][:, k * P:(k + 1) * P], hs[:, k * P:(k + 1) * P], ident)
                        last.then_inc(hsT_in_psum[layer], 1)
                    if n is not None:
                        if static(n) and n == 0:
                            rowsT(0, 0)
                        pe.wait_ge(xsT_ready[layer], n + 1)
                        for j in range(nj):
                            e = experts_n[j]
                            if layer == 0:
                                for o in range(2):
                                    for k in range(KC):
                                        at_w = k * 2 * H0 + o * H0
                                        last = mm(ps[o][:, :], xsT[:, k * P:(k + 1) * P], w_ffn[:, e, at_w:at_w + H0],
                                                  start=(k == 0), stop=(k == KC - 1))
                            else:
                                for k in range(KC):
                                    last = mm(ps[0][:, j * 256:(j + 1) * 256],
                                              xsT[:, (j * KC + k) * P:(j * KC + k + 1) * P],
                                              w1_ffn[:, e, k * 256:(k + 1) * 256], start=(k == 0), stop=(k == KC - 1))
                        last.then_inc(gu_in_psum[layer], 1)
                        if not (static(n) and n == NS - 1):
                            rowsT(n + 1, 1 - p)
                    if b is not None:
                        pe.wait_ge(hsT_ready[layer], b + 1)
                        if not (static(b) and b == 0):
                            pe.wait_ge(ys_ready[layer], b)
                        for j in range(nj):
                            e = experts_b[j]
                            if layer == 0:
                                for k in range(HC0):
                                    at_w = 2 * KC * H0 + k * D
                                    last = mm(ps[3][:, 0:D], hsT[:, k * P:(k + 1) * P], w_ffn[:, e, at_w:at_w + D],
                                              start=(k == 0), stop=(k == HC0 - 1))
                            else:
                                last = mm(ps[3][:, j * D:(j + 1) * D], hsT[:, j * P:(j + 1) * P],
                                          w1_ffn[:, e, 512:768], start=True, stop=True)
                        last.then_inc(ys_in_psum[layer], 1)

                body(0, None, 0)
                body(1, 0, 1)
                body(2, 1, 0)
                with pe.Fori(1, (NS - 3) // 2) as i:
                    body(i * 2 + 1, i * 2, 1)
                    body(i * 2 + 2, i * 2 + 1, 0)
                body(NS - 2, NS - 3, 1)
                body(NS - 1, NS - 2, 0)
                body(None, NS - 1, 1)

            def ffn(layer):
                pe.wait_ge(lg_ready, NB * (layer + 1))
                pe.wait_ge(x1_ready, NB * (layer + 1))
                pe.wait_ge(ffn_in[0] if layer == 0 else ffn_in[3], 16 if layer == 0 else 16 * (R1 + 1))
                shared(layer, SHARED[layer][0])
                pe.wait_ge(experts_ready[layer], 1)
                if layer == 0:
                    pe.wait_ge(ffn_in[1], 48)
                    pe.wait_ge(ffn_in[2], 80)
                sorted_tiles(layer)

            ffn(0)
            pe.wait_ge(ys_ready[0], NS)
            shared(0, SHARED[0][1])
            pe.wait_ge(watt1_in, 16)
            attention(1)
            ffn(1)

        @block.vector
        def _(dve):
            V = nc.vector

            def attention(layer):
                def stats(n):
                    if layer:
                        dve.wait_ge(x2_ready, n + 1)
                        apart(dve)
                    apart(dve)
                    V.bn_stats(ln_st[:, 0, :], x_res[:, n, :]).then_inc(stats_done, 1)
                    dve.wait_ge(stats_done, at(layer, n) + 1)
                    apart(dve)
                    V.bn_aggr(ln_mv[:, 0, :], ln_st[:, 0, :]).then_inc(aggr_done, 1)
                    dve.wait_ge(aggr_done, at(layer, n) + 1)
                    V.tensor_scalar(ln_ve[:, 0:1], ln_mv[:, 0, 1:2], EPS, None, ALU.add).then_inc(var_ready, 1)

                def normalise(n):
                    dve.wait_ge(rstd_ready, at(layer, n) + 1)
                    if not (layer == 0 and static(n) and n == 0):
                        dve.wait_ge(xnT_in_psum, at(layer, n))
                    V.tensor_scalar(xn[:], x_res[:, n, :], ln_mv[:, 0, 0:1], ln_rs[:, 0:1], ALU.subtract, ALU.mult)\
                        .then_inc(xn_ready, 1)

                def shift(n, half, between=None, before=None):
                    first = layer == 0 and static(n) and n == 0
                    banks = (2 * half, 2 * half + 1)
                    s4 = {j: ps_s[j][:, :].rearrange("p (i s) -> p i s", i=4) for j in banks}
                    dve.wait_ge(scores_in_psum, at(layer, n) * 2 + half + 1)
                    if layer == 0:
                        for j in banks:
                            if not first:
                                dve.wait_ge(probs_ready, at(layer, n) * 4 - 3 + j)
                            V.tensor_tensor(sc[:, j], s4[j], bias_all[:, n, :].unsqueeze(1).broadcast_to([P, 4, P]),
                                            ALU.add).then_inc(biased, 1)
                            s4[j] = sc[:, j]
                    if between and layer == 0:
                        between()
                    for j in banks:
                        if layer == 0:
                            dve.wait_ge(biased, at(layer, n) * 4 + j + 1)
                        V.tensor_reduce(mx[:, j, :], s4[j], AX.X, ALU.max).then_inc(max_ready, 1)
                    if between and layer:
                        between()
                    if before:
                        before()
                    for j in banks:
                        dve.wait_ge(max_ready, at(layer, n) * 4 + j + 1)
                        if layer and not first:
                            dve.wait_ge(probs_ready, at(layer, n) * 4 - 3 + j)
                        V.tensor_tensor(sc[:, j], s4[j], mx[:, j, :].unsqueeze(2).broadcast_to([P, 4, P]), ALU.subtract)\
                            .then_inc(shifted, 1)

                def body(m, n, b, c):
                    def residual():
                        dve.wait_ge(wo_in_psum, at(layer, c) + 1)
                        if layer:
                            dve.wait_ge(bo_added, c + 1)
                        V.tensor_tensor(x_res[:, c, :], ps_po[:, 0:D], x_res[:, c, :], ALU.add).then_inc(x1_ready, 1)

                    second_batch = static(m) and m == 1
                    if second_batch and layer:
                        normalise(1)
                    if m is not None and not second_batch:
                        stats(m)
                    if n is not None:
                        if layer == 0:
                            dve.wait_ge(bias_ready, n // MG + 1)
                        shift(n, 0, before=residual if c is not None and layer == 0 else None)
                    if m is not None and not second_batch:
                        normalise(m)
                    if static(m) and m == 0:
                        stats(1)
                    if c is not None and (layer or n is None):
                        residual()
                    if c is not None:
                        dve.wait_ge(x1_ready, at(layer, c) + 1)
                        apart(dve)
                        V.bn_stats(ln_st[:, 1, :], x_res[:, c, :]).then_inc(stats1_done, 1)
                        dve.wait_ge(stats1_done, at(layer, c) + 1)
                        apart(dve)
                        V.bn_aggr(ln_mv[:, 1, :], ln_st[:, 1, :]).then_inc(aggr1_done, 1)
                        dve.wait_ge(aggr1_done, at(layer, c) + 1)
                        V.tensor_scalar(ln_ve[:, 1:2], ln_mv[:, 1, 1:2], EPS, None, ALU.add).then_inc(var1_ready, 1)

                    def normalise1():
                        dve.wait_ge(rstd1_ready, at(layer, c) + 1)
                        if not (layer == 0 and static(c) and c == 0):
                            dve.wait_ge(xn1T_in_psum, at(layer, c))
                            dve.wait_ge(xn1_kept, at(layer, c))
                        V.tensor_scalar(xn1[:], x_res[:, c, :], ln_mv[:, 1, 0:1], ln_rs[:, 1:2],
                                        ALU.subtract, ALU.mult).then_inc(xn1_ready, 1)


                    def weighted_rows():
                        dve.wait_ge(av_in_psum, at(layer, b) + 1)
                        po = ps_po[:, 0:NH * VW].rearrange("p (h d) -> p h d", h=NH)
                        V.reciprocal(rsum[:].unsqueeze(2), po[:, :, HD:VW]).then_inc(rsum_ready, 1)
                        dve.wait_ge(rsum_ready, at(layer, b) + 1)
                        if not (layer == 0 and static(b) and b == 0):
                            dve.wait_ge(attnT_in_psum, at(layer, b))
                        V.tensor_tensor(attn[:].rearrange("p (h d) -> p h d", h=NH), po[:, :, 0:HD],
                                        rsum[:].unsqueeze(2).broadcast_to([P, NH, HD]), ALU.mult).then_inc(attn_ready, 1)

                    within = layer == 0 and n is not None
                    if n is not None:
                        shift(n, 1, normalise1 if c is not None else None, weighted_rows if b is not None and within else None)
                    elif c is not None:
                        normalise1()
                    if b is not None and not within:
                        weighted_rows()
                    if n is not None and layer:
                        dve.wait_ge(v_in_psum, at(layer, n) + 1)
                        V.tensor_tensor(va[:, :, 0:HD], ps_pm[:, 0:D].rearrange("p (h d) -> p h d", h=NH),
                                        bvo[:, 0, :].rearrange("p (h d) -> p h d", h=NH), ALU.add).then_inc(v_ready, 1)

                pipeline_start(layer, body, normalise)

            def pipeline_start(layer, body, normalise):
                if layer:
                    pipeline(dve, body)
                    return
                body(0, None, None, None)
                for k in range(KB):
                    if k == 12:
                        normalise(1)
                    dve.wait_ge(hid_ready, k + 1)
                    if k == 0:
                        V.tensor_scalar(acc0[:], hid[0], c_bc[:, 0:1], bb2, ALU.mult, ALU.add).then_inc(hid0_added, 1)
                    else:
                        dve.wait_ge(hid0_added, k)
                        V.scalar_tensor_tensor(acc0[:], hid[k % 4], c_bc[:, k:k + 1], acc0[:], ALU.mult, ALU.add)\
                            .then_inc(hid0_added, 1)
                dve.wait_ge(hid0_added, KB)
                dve.wait_ge(mask0_in, 16)
                four = bias_all[:, 0:MG, :].rearrange("p b s -> p (b s)")
                V.tensor_tensor(four, four, acc0[:], ALU.add).then_inc(bias_ready, 1)
                dve.wait_ge(x_in, 16)
                dve.wait_ge(small_in, 64)
                dve.wait_ge(consts_in, 16)
                V.tensor_scalar(qb4[:], qkb[:, 0, :], 0.25, None, ALU.mult).then_inc(setup_dve, 1)
                for k in range(KC):
                    V.tensor_scalar(kbm[:, k, :], par, qkb[:, 1, k:k + 1], None, ALU.mult).then_inc(setup_dve, 1)
                body(1, 0, None, None)
                body(2, 1, 0, None)
                body(3, 2, 1, 0)
                with dve.Fori(3, NB - 1) as n:
                    body(n + 1, n, n - 1, n - 2)
                body(None, NB - 1, NB - 2, NB - 3)
                body(None, None, NB - 1, NB - 2)
                body(None, None, None, NB - 1)

            dve.wait_ge(x0_in, 16)
            dve.wait_ge(mlp_in, 16)
            attention(0)

            chain = [0]

            def then(instruction):
                chain[0] += 1
                instruction.then_inc(route_step, 1)
                dve.wait_ge(route_step, chain[0])

            def hidden(layer, g, c, q):
                h = half(layer, g, c)
                dve.wait_ge(sh_silu[layer], q + 1)
                if q >= 2:
                    dve.wait_ge(sh_used[layer], q - 1)
                V.tensor_tensor(hT[:, h, :], ps[2 + h][:, :], sg[:, h, :], ALU.mult).then_inc(sh_hidden[layer], 1)

            def routing(layer):
                ne = E1 if layer else E0
                w = NB * ne
                be = lambda v: v[:, 0:w].rearrange("p (b e) -> p b e", b=NB)
                eb = lambda v: v[:, 0:w].rearrange("p (e b) -> p e b", e=ne)
                over_e = lambda v: v.unsqueeze(2).broadcast_to([P, NB, ne])
                over_b = lambda v: v.unsqueeze(1).broadcast_to([P, NB, ne])
                prio = cst[:, C_PRI:C_PRI + ne]
                dve.wait_ge(lg_ready, NB * (layer + 1))
                dve.wait_ge(xn1_kept, NB * (layer + 1))

                def pick(values, to, best):
                    then(V.tensor_reduce(best, values, AX.X, ALU.max))
                    then(V.tensor_tensor(be(rw[7]), values, over_e(best), ALU.is_equal))
                    then(V.tensor_tensor(be(rw[7]), be(rw[7]), over_b(prio), ALU.mult))
                    then(V.tensor_reduce(small[:, 7, :], be(rw[7]), AX.X, ALU.max))
                    then(V.tensor_tensor(to, be(rw[7]), over_e(small[:, 7, :]), ALU.is_equal))

                if layer == 0:
                    pick(lg[:, :, 0:ne], be(rw[3]), small[:, 0, :])
                    V.tensor_copy(picks[:, 0:w], rw[3][:, 0:w]).then_inc(picks_ready[layer], 1)
                    chosen = [rw[3]]
                else:
                    then(V.tensor_tensor(be(rw[0]), lg[:], over_b(rbias[:]), ALU.add))
                    then(V.tensor_reduce(small[:, 0, :], be(rw[0]), AX.X, ALU.max))
                    V.tensor_tensor(be(rw[0]), be(rw[0]), over_e(small[:, 0, :]), ALU.subtract).then_inc(centred, 1)
                    dve.wait_ge(exp_ready, 1)
                    then(V.tensor_reduce(small[:, 1, :], be(rw[1]), AX.X, ALU.add))
                    then(V.reciprocal(small[:, 2, :], small[:, 1, :]))
                    then(V.tensor_tensor(be(rw[2]), be(rw[1]), over_e(small[:, 2, :]), ALU.mult))
                    pick(be(rw[2]), be(rw[3]), small[:, 3, :])
                    then(V.scalar_tensor_tensor(rw[4], rw[3], -2.0, rw[2], ALU.mult, ALU.add))
                    pick(be(rw[4]), be(rw[5]), small[:, 4, :])
                    V.tensor_tensor(picks[:, 0:w], rw[3], rw[5], ALU.add).then_inc(picks_ready[layer], 1)
                    then(V.tensor_tensor(small[:, 5, :], small[:, 3, :], small[:, 4, :], ALU.add))
                    then(V.tensor_scalar(small[:, 5, :], small[:, 5, :], 1e-6, None, ALU.add))
                    then(V.reciprocal(small[:, 6, :], small[:, 5, :]))
                    then(V.tensor_tensor(wgt[:, 0, :], small[:, 3, :], small[:, 6, :], ALU.mult))
                    then(V.tensor_tensor(wgt[:, 1, :], small[:, 4, :], small[:, 6, :], ALU.mult))
                    chosen = [rw[3], rw[5]]
                dve.wait_ge(ranks_in_psum[layer], 1)
                then(V.tensor_copy(eb(rw[8]), be(ps_po).rearrange("p b e -> p e b")))
                then(V.tensor_tensor_scan(rw[9][:, 0:w], seg[:, 0:w], rw[8][:, 0:w], 0.0, ALU.mult, ALU.add))
                total = eb(rw[9])[:, :, NB - 1]
                need, upto = small[:, 1, 0:ne], small[:, 2, 0:ne]
                then(V.tensor_scalar(need_i[:, 0:ne], total, float(P - 1), None, ALU.add))
                then(V.tensor_scalar(need_i[:, 0:ne], need_i[:, 0:ne], P.bit_length() - 1, None, ALU.arith_shift_right))
                then(V.tensor_copy(need, need_i[:, 0:ne]))
                then(V.tensor_tensor_scan(upto, ones[:, 0:ne], need, 0.0, ALU.mult, ALU.add))
                then(V.tensor_tensor(small[:, 3, 0:ne], upto, need, ALU.subtract))
                then(V.tensor_scalar(small[:, 3, 0:ne], small[:, 3, 0:ne], float(P), None, ALU.mult))
                then(V.tensor_tensor(rw[9][:, 0:w], rw[9][:, 0:w], rw[8][:, 0:w], ALU.subtract))
                then(V.tensor_tensor(be(rw[10]), be(ps_pm), eb(rw[9]).rearrange("p e b -> p b e"), ALU.add))
                then(V.tensor_tensor(be(rw[10]), be(rw[10]), over_b(small[:, 3, 0:ne]), ALU.add))
                if layer:
                    then(V.tensor_copy(be(rw[10])[:, :, R1], result_rows))
                for a, one in enumerate(chosen):
                    if a:
                        then(V.tensor_scalar(be(rw[10])[:, :, R1], be(rw[10])[:, :, R1], float(SECOND), None, ALU.add))
                    then(V.tensor_tensor(be(rw[11]), be(rw[10]), be(one), ALU.mult))
                    then(V.tensor_reduce(small[:, 4 + a, :], be(rw[11]), AX.X, ALU.add))
                    V.tensor_copy(slot[:, a, :], small[:, 4 + a, :]).then_inc(slots_ready[layer], 1)
                    if a == 0:
                        for step in shared_steps(layer, (0, 1))[:EARLY[layer]]:
                            hidden(layer, *step)
                nt, nr = (T1, R1) if layer else (T0, E0)
                big = work[:, 0:nt * nr].rearrange("p (t e) -> p t e", t=nt)
                then(V.tensor_tensor(big, upto[:, 0:nr].unsqueeze(1).broadcast_to([P, nt, nr]),
                                     cst[:, C_TIL:C_TIL + nt].unsqueeze(2).broadcast_to([P, nt, nr]), ALU.is_le))
                then(V.tensor_reduce(te_f[:, 0:nt], big, AX.X, ALU.add))
                then(V.tensor_scalar(te_f[:, 0:nt], te_f[:, 0:nt], float(nr - 1), None, ALU.min))
                digits = te_f[:, 0:NS]
                if layer:
                    pairs = te_f[:].rearrange("p (n j) -> p n j", j=2)
                    digits = small[:].rearrange("p a b -> p (a b)")[:, 0:NS]
                    then(V.scalar_tensor_tensor(digits, pairs[:, :, 1], float(nr), pairs[:, :, 0], ALU.mult, ALU.add))
                then(V.scalar_tensor_tensor(rw[11][:, 1:NS], digits[:, 0:NS - 1], float(nr ** JT[layer]),
                                            digits[:, 1:NS], ALU.mult, ALU.add))
                then(V.tensor_copy(rw[11][:, 0:1], digits[:, 0:1]))
                V.tensor_copy(step_experts[:], rw[11][:, 0:NS]).then_inc(experts_ready[layer], 1)

            def shared(layer, groups):
                def add(g):
                    dve.wait_ge(sh_used[layer], g * HC0 + HC0 if layer == 0 else g + 1)
                    for i in range(MG):
                        V.tensor_tensor(x_res[:, g * MG + i, :], ps[4 + i][:, 0:D], x_res[:, g * MG + i, :], ALU.add)\
                            .then_inc(sh_added[layer], 1)

                for g, c, q in shared_steps(layer, groups):
                    if q >= EARLY[layer]:
                        hidden(layer, g, c, q)
                    if layer == 0 and c == 0 and g != groups[0]:
                        add(g - 1)
                    if layer and q >= 2:
                        add(q - 2)
                if layer:
                    add(groups[-2])
                add(groups[-1])

            def sorted_tiles(layer):
                def keep_ids(n, p):
                    dve.wait_ge(xs_in[1][p], (n // 2 + 1) * 16)
                    own = own_rows.rearrange("p (n j) -> p n j", j=JT[1])[:, bass.ds(n, 1), :]
                    V.tensor_tensor(row_ids[:, bass.ds(n, 1), :], xs[:, p:p + 1, :, D], own, ALU.max)\
                        .then_inc(ids_kept, 1)

                def body(n, p):
                    if layer:
                        keep_ids(n, p)
                    dve.wait_ge(silu_ready[layer], n + 1)
                    if not (static(n) and n == 0):
                        dve.wait_ge(hsT_in_psum[layer], n)
                    if layer == 0:
                        V.tensor_tensor(hs[:, 0:H0], ps[1][:, :], sgs[:, 0:H0], ALU.mult).then_inc(hs_ready[layer], 1)
                    else:
                        V.tensor_tensor(hs[:, 0:2 * H1].rearrange("p (j h) -> p j h", j=2),
                                        ps[0][:, :].rearrange("p (j a h) -> p j a h", j=2, a=2)[:, :, 1, :],
                                        sgs[:, 0:2 * H1].rearrange("p (j h) -> p j h", j=2), ALU.mult)\
                            .then_inc(hs_ready[layer], 1)
                body(0, 0)
                with dve.Fori(0, NS // 2) as i:
                    body(i * 2 + 1, 1)
                    body(i * 2 + 2, 0)

            routing(0)
            shared(0, SHARED[0][0])
            sorted_tiles(0)
            for p in range(2):
                dve.wait_ge(ys_stored[0][p], 16 * ((NS + 1 - p) // 2))
            shared(0, SHARED[0][1])
            attention(1)
            routing(1)
            shared(1, SHARED[1][0])
            sorted_tiles(1)
            for g in range(NB // MG):
                dve.wait_ge(results_loaded[g], 2 * 16)
                for b in range(g * MG, (g + 1) * MG):
                    V.scalar_tensor_tensor(x_res[:, b, :], xn_all[:, b, :], wgt[:, 0, b:b + 1], x_res[:, b, :],
                                           ALU.mult, ALU.add).then_inc(weighted, 1)
                for b in range(g * MG, (g + 1) * MG):
                    dve.wait_ge(weighted, b + 1)
                    last = V.scalar_tensor_tensor(x_res[:, b, :], rows_b[:, b, :], wgt[:, 1, b:b + 1], x_res[:, b, :],
                                                  ALU.mult, ALU.add)
                last.then_inc(out_ready, 1)


def static(i):
    return isinstance(i, int)


def kernel(**inputs):
    import numpy as _np
    import concourse.bacc as _bacc
    from concourse import mybir as _mybir
    from concourse.bass_utils import run_bass_kernel_spmd as _run

    a = {k: _np.asarray(v) for k, v in inputs.items()}

    def chunks(w):
        return w.reshape(w.shape[0] // P, P, -1).transpose(1, 0, 2)

    cst = _np.zeros((P, C_END), _np.float32)
    i = _np.arange(P)
    cst[:, C_ID:C_ID + P] = i[:, None] == i[None, :]
    cst[:, C_TRI:C_TRI + P] = i[:, None] < i[None, :]
    cst[:, C_ONE:C_ONE + P] = 1
    cst[:, C_PAR] = i % 32 < HD
    cst[:, C_PAR + 1] = i % 32 >= HD
    cst[:, C_PRI:C_PRI + E1] = E1 - _np.arange(E1)
    cst[:, C_TIL:C_SEG] = _np.arange(C_SEG - C_TIL)
    cst[:, C_SEG:C_OUT] = _np.arange(NB * E1) % NB > 0
    cst[:, C_OUT:C_OUT + NB] = RESULTS + P * _np.arange(NB) + i[:, None]
    cst[:, C_OWN:C_END] = P * _np.arange(T1) + i[:, None]
    bc = lambda v: _np.ascontiguousarray(_np.broadcast_to(v.reshape(1, -1), (P, v.size)))
    host = {
        "consts": cst,
        "x": a["x"].transpose(1, 0, 2),
        "ctxT": chunks(a["ctx_1024"].reshape(NB * P, D).T),
        "dist": a["fside_BxSxS2_0"].transpose(1, 0, 2),
        "mask": a["mask_Bx1xSxS2_ff0"][:, 0].transpose(1, 0, 2),
        "w_att0": _np.stack([chunks(a["L0_xattn_Wq"].reshape(D, D)), chunks(a["L0_xattn_Wk"].reshape(D, D)),
                             chunks(a["L0_xattn_Wv"].reshape(D, D)), chunks(a["L0_xattn_Wo"].reshape(D, D))], 1),
        "w_att1": _np.stack([chunks(a["L1_xattn_W" + x].T) for x in "qkvo"], 1),
        "rt": chunks(_np.concatenate([a["L0_ffn_router"].T, a["L1_ffn_router_w"]], 1)),
        "mlp": bc(_np.concatenate([a["L0_xattn_Wb1"][0], a["L0_xattn_bb1"], a["L0_xattn_Wb2"][:, 0],
                                   a["L0_xattn_bb2"]])),
        "qkb": _np.stack([a["L1_xattn_bq"].reshape(KC, P).T, a["L1_xattn_bk"].reshape(KC, P).T], 1),
        "bvo": bc(_np.concatenate([a["L1_xattn_bv"], a["L1_xattn_bo"]])).reshape(P, 2, D),
        "w_ffn0": _np.concatenate([
            _np.concatenate([a["L0_ffn_gate"], a["L0_ffn_up"]], 1).transpose(2, 0, 1)
            .reshape(KC, P, E0, 2 * H0).transpose(1, 2, 0, 3).reshape(P, E0, -1),
            a["L0_ffn_down"].transpose(2, 0, 1).reshape(HC0, P, E0, D).transpose(1, 2, 0, 3).reshape(P, E0, -1)], 2),
        "w_sh0": _np.concatenate([
            chunks(_np.concatenate([a["L0_ffn_w_gate_s"], a["L0_ffn_w_up_s"]], 0).T).reshape(P, -1),
            chunks(a["L0_ffn_w_down_s"].T).reshape(P, -1)], 1),
        "w_ffn1": _np.concatenate([
            _np.concatenate([a["L1_ffn_expert_gate_w"], a["L1_ffn_expert_up_w"]], 2).transpose(1, 0, 2)
            .reshape(KC, P, R1, 2 * H1).transpose(1, 2, 0, 3).reshape(P, R1, -1),
            a["L1_ffn_expert_down_w"].transpose(1, 0, 2)], 2),
        "w_sh1": _np.concatenate([
            a["L1_ffn_conv_w"].transpose(1, 2, 0).reshape(KC, P, CONV * H1).transpose(1, 0, 2).reshape(P, -1),
            chunks(a["L1_ffn_shared_up_w"]).reshape(P, -1), a["L1_ffn_shared_down_w"]], 1),
        "rbias": bc(a["L1_ffn_router_bias"]),
    }
    nc = _bacc.Bacc("TRN2", target_bir_lowering=False, num_devices=1)
    arrays, aps = {}, {}
    for name, v in host.items():
        v = _np.ascontiguousarray(v)
        arrays[f"in_{name}"] = v
        aps[name] = nc.dram_tensor(f"in_{name}", v.shape, _mybir.dt.from_np(v.dtype), kind="ExternalInput").ap()
    out = nc.dram_tensor("out_0", (NB, P, D), _mybir.dt.float32, kind="ExternalOutput").ap()
    rows = [nc.dram_tensor("rows0", (T0 * P, D), _mybir.dt.float32).ap(),
            nc.dram_tensor("rows1", (RESULTS + 2 * SECOND, D + 1), _mybir.dt.float32).ap()]
    build_program(nc, aps, out, rows)
    r = _run(nc, [arrays], core_ids=[0])
    return r.results[0]["out_0"]
```
